# Optimizing a Trainium2 kernel written in Bass

```python
import numpy as np
import jax
import jax.numpy as jnp

def _softmax(x, axis=-1):
    return jax.nn.softmax(x, axis=axis)

def _gelu(x):
    return jax.nn.gelu(x, approximate=True)

def _silu(x):
    return jax.nn.silu(x)

def _sigmoid(x):
    return jax.nn.sigmoid(x)

def _layernorm(x, axis=-1, eps=1e-05):
    m = jnp.mean(x, axis=axis, keepdims=True)
    v = jnp.var(x, axis=axis, keepdims=True)
    return (x - m) / jnp.sqrt(v + eps)

def _scatter_add(tgt, idx, src, axis=0):
    return tgt.at[idx].add(src)

def _segment_sum(src, seg, n):
    return jax.ops.segment_sum(src, seg, n)
kernel_name = 'mk_xattn_ffn_d2_seqx_r4_c72392'

def setup_inputs(seed: int=0):
    np.random.seed(seed)
    _w = jnp.asarray

    def _rec_inputs():
        import jax
        import jax.numpy as jnp
        _rk = jax.random.key(seed)
        x = -0.0002928 + 1 * jax.random.normal(jax.random.fold_in(_rk, 1), (8, 256, 256), jnp.float32)
        _lenS = 256 - jax.random.randint(jax.random.fold_in(_rk, 7), (8,), 0, max(1, 256 // 4) + 1, jnp.int32)
        _lenS2 = 120 - jax.random.randint(jax.random.fold_in(_rk, 8), (8,), 0, max(1, 120 // 4) + 1, jnp.int32)
        _ctx_1024P = jax.random.normal(jax.random.fold_in(_rk, 11), (8, 16, 256), jnp.float32)
        _ctx_1024c = jax.random.dirichlet(jax.random.fold_in(_rk, 511), 0.3 * jnp.ones((16,), jnp.float32), (8, 120))
        _ctx_1024t = jnp.einsum('bsk,bkd->bsd', _ctx_1024c, _ctx_1024P)
        _ctx_1024t = _ctx_1024t * jax.lax.rsqrt(jnp.mean(jnp.square(_ctx_1024t)) + 1e-12) * 0.953939
        ctx_1024 = -1.39393e-06 + 0.999914 * (_ctx_1024t + 0.3 * jax.random.normal(jax.random.fold_in(_rk, 611), (8, 120, 256), jnp.float32))
        _validS = jnp.arange(256)[None, :] < _lenS[:, None]
        _validS2 = jnp.arange(120)[None, :] < _lenS2[:, None]
        _causal = jnp.tril(jnp.ones((256, 256), dtype=bool))
        mask_1x1xSxS2_ik0 = jnp.where(jnp.broadcast_to(_validS2[0:1, None, None, :], (1, 1, 256, 120)), 0, 1).astype(jnp.int32)
        return (x, ctx_1024, mask_1x1xSxS2_ik0)
    x, ctx_1024, mask_1x1xSxS2_ik0 = _rec_inputs()

    def _L0_xattn_setup():
        import jax, jax.numpy as jnp
        import numpy as np
        D_MODEL = 256
        H = 16
        D_K = D_MODEL // H
        NEG_INF = -1000000000.0
        key = jax.random.key(seed)
        kq, kk, kv, kwq, kwk, kwv, kwo = jax.random.split(key, 7)
        B, S = (2, 512)
        query = jax.random.normal(kq, (B, S, D_MODEL), dtype=jnp.float32)
        key_t = jax.random.normal(kk, (B, S, D_MODEL), dtype=jnp.float32)
        value = jax.random.normal(kv, (B, S, D_MODEL), dtype=jnp.float32)
        masked_val = jnp.tril(jnp.ones((S, S), dtype=jnp.int32))[None, None, :, :]
        scale = 1.0 / np.sqrt(D_MODEL)
        w_q = jax.random.normal(kwq, (D_MODEL, D_MODEL), dtype=jnp.float32) * scale
        w_k = jax.random.normal(kwk, (D_MODEL, D_MODEL), dtype=jnp.float32) * scale
        w_v = jax.random.normal(kwv, (D_MODEL, D_MODEL), dtype=jnp.float32) * scale
        w_o = jax.random.normal(kwo, (D_MODEL, D_MODEL), dtype=jnp.float32) * scale
        return {'query': query, 'key': key_t, 'value': value, 'masked_val': masked_val, 'w_q': w_q, 'w_k': w_k, 'w_v': w_v, 'w_o': w_o}
    _L0_xattn_all = _L0_xattn_setup()
    _L0_xattn_in = {k: v for k, v in _L0_xattn_all.items() if k in ('w_q', 'w_k', 'w_v', 'w_o')}
    del _L0_xattn_all

    def _L0_ffn_setup():
        import jax, jax.numpy as jnp
        import numpy as np
        TOP_K = 8
        CAPACITY = 128

        def _silu(x):
            return x * jax.nn.sigmoid(x)
        key = jax.random.key(seed)
        ks = jax.random.split(key, 7)
        B, S, H, E, I, Is = (2, 256, 256, 64, 128, 512)
        s = 0.05
        return {'hidden_states': jax.random.normal(ks[0], (B, S, H), jnp.float32), 'gate_w': jax.random.normal(ks[1], (H, E), jnp.float32) * s, 'shared_gate_w': jax.random.normal(ks[2], (H, 1), jnp.float32) * s, 'shared_gate_up_w': jax.random.normal(ks[3], (H, 2 * Is), jnp.float32) * s, 'shared_down_w': jax.random.normal(ks[4], (Is, H), jnp.float32) * s, 'expert_gate_up_w': jax.random.normal(ks[5], (E, H, 2 * I), jnp.float32) * s, 'expert_down_w': jax.random.normal(ks[6], (E, I, H), jnp.float32) * s}
    _L0_ffn_all = _L0_ffn_setup()
    _L0_ffn_in = {k: v for k, v in _L0_ffn_all.items() if k in ('gate_w', 'shared_gate_w', 'shared_gate_up_w', 'shared_down_w', 'expert_gate_up_w', 'expert_down_w')}
    del _L0_ffn_all

    def _L1_xattn_setup():
        import jax, jax.numpy as jnp
        import numpy as np
        D_MODEL = 256
        H = 16
        D_H = D_MODEL // H
        key = jax.random.key(seed)
        ks = jax.random.split(key, 10)
        B, T_dec, T_enc = (2, 512, 512)
        s = 1.0 / np.sqrt(D_MODEL)
        return {'tgt': jax.random.normal(ks[0], (B, T_dec, D_MODEL), jnp.float32), 'memory': jax.random.normal(ks[1], (B, T_enc, D_MODEL), jnp.float32), 'W_q': jax.random.normal(ks[2], (D_MODEL, D_MODEL), jnp.float32) * s, 'b_q': jnp.zeros((D_MODEL,), jnp.float32), 'W_k': jax.random.normal(ks[3], (D_MODEL, D_MODEL), jnp.float32) * s, 'b_k': jnp.zeros((D_MODEL,), jnp.float32), 'W_v': jax.random.normal(ks[4], (D_MODEL, D_MODEL), jnp.float32) * s, 'b_v': jnp.zeros((D_MODEL,), jnp.float32), 'W_o': jax.random.normal(ks[5], (D_MODEL, D_MODEL), jnp.float32) * s, 'b_o': jnp.zeros((D_MODEL,), jnp.float32)}
    _L1_xattn_all = _L1_xattn_setup()
    _L1_xattn_in = {k: v for k, v in _L1_xattn_all.items() if k in ('W_q', 'b_q', 'W_k', 'b_k', 'W_v', 'b_v', 'W_o', 'b_o')}
    del _L1_xattn_all

    def _L1_ffn_setup():
        import jax, jax.numpy as jnp
        import numpy as np
        HIDDEN = 256
        N_EXPERTS = 32
        MOE_I = 128
        N_GROUP = 4
        TOPK_GROUP = 2
        TOP_K = 6
        N_LOCAL_GROUPS = 16
        ANCHOR_I = 64
        SHARED_I = 128
        ROUTED_SCALE = 0.2
        ANCHOR_ALPHA = 0.1
        BATCH, SEQ = (1, 256)

        def _moe_forward(hidden_states, gate_weight, gate_bias, w_gate, w_up, w_down, shared_w_gate, shared_w_up, shared_w_down, anchor_w_gate, anchor_w_up, anchor_w_down):
            B, S, H = hidden_states.shape
            x = hidden_states.reshape(-1, H)
            T = x.shape[0]
            E = gate_weight.shape[0]
            L = anchor_w_gate.shape[0]
            logits = x @ gate_weight.T
            scores = jax.nn.sigmoid(logits)
            sc = scores + gate_bias
            grp = sc.reshape(T, N_GROUP, E // N_GROUP)
            group_scores = jax.lax.top_k(grp, 2)[0].sum(-1)
            _, gidx = jax.lax.top_k(group_scores, TOPK_GROUP)
            gmask = jax.nn.one_hot(gidx, N_GROUP, dtype=sc.dtype).sum(1)
            emask = jnp.repeat(gmask, E // N_GROUP, axis=1)
            masked = jnp.where(emask > 0, sc, -jnp.inf)
            _, topidx = jax.lax.top_k(masked, TOP_K)
            tw = jnp.take_along_axis(scores, topidx, axis=-1)
            tw = tw / (tw.sum(-1, keepdims=True) + 1e-20) * ROUTED_SCALE
            g = jnp.einsum('th,ehi->tei', x, w_gate)
            u = jnp.einsum('th,ehi->tei', x, w_up)
            eo = jnp.einsum('tei,eih->teh', jax.nn.silu(g) * u, w_down)
            cw = (jax.nn.one_hot(topidx, E, dtype=x.dtype) * tw[..., None]).sum(1)
            routed = jnp.einsum('te,teh->th', cw, eo)
            shared = jax.nn.silu(x @ shared_w_gate) * (x @ shared_w_up) @ shared_w_down
            lg = topidx[:, 0] // (E // L)
            ag = jnp.einsum('th,lhi->tli', x, anchor_w_gate)
            au = jnp.einsum('th,lhi->tli', x, anchor_w_up)
            ao = jnp.einsum('tli,lih->tlh', jax.nn.silu(ag) * au, anchor_w_down)
            acw = jax.nn.one_hot(lg, L, dtype=x.dtype)
            anchor = jnp.einsum('tl,tlh->th', acw, ao)
            out = routed + shared + ANCHOR_ALPHA * anchor
            return out.reshape(B, S, H)
        key = jax.random.key(seed)
        ks = jax.random.split(key, 13)
        s = 0.02
        return {'hidden_states': jax.random.normal(ks[0], (BATCH, SEQ, HIDDEN), jnp.float32), 'gate_weight': s * jax.random.normal(ks[1], (N_EXPERTS, HIDDEN), jnp.float32), 'gate_bias': s * jax.random.normal(ks[2], (N_EXPERTS,), jnp.float32), 'w_gate': s * jax.random.normal(ks[3], (N_EXPERTS, HIDDEN, MOE_I), jnp.float32), 'w_up': s * jax.random.normal(ks[4], (N_EXPERTS, HIDDEN, MOE_I), jnp.float32), 'w_down': s * jax.random.normal(ks[5], (N_EXPERTS, MOE_I, HIDDEN), jnp.float32), 'shared_w_gate': s * jax.random.normal(ks[6], (HIDDEN, SHARED_I), jnp.float32), 'shared_w_up': s * jax.random.normal(ks[7], (HIDDEN, SHARED_I), jnp.float32), 'shared_w_down': s * jax.random.normal(ks[8], (SHARED_I, HIDDEN), jnp.float32), 'anchor_w_gate': s * jax.random.normal(ks[9], (N_LOCAL_GROUPS, HIDDEN, ANCHOR_I), jnp.float32), 'anchor_w_up': s * jax.random.normal(ks[10], (N_LOCAL_GROUPS, HIDDEN, ANCHOR_I), jnp.float32), 'anchor_w_down': s * jax.random.normal(ks[11], (N_LOCAL_GROUPS, ANCHOR_I, HIDDEN), jnp.float32)}
    _L1_ffn_all = _L1_ffn_setup()
    _L1_ffn_in = {k: v for k, v in _L1_ffn_all.items() if k in ('gate_weight', 'gate_bias', 'w_gate', 'w_up', 'w_down', 'shared_w_gate', 'shared_w_up', 'shared_w_down', 'anchor_w_gate', 'anchor_w_up', 'anchor_w_down')}
    del _L1_ffn_all
    return {'x': x, 'ctx_1024': ctx_1024, 'mask_1x1xSxS2_ik0': mask_1x1xSxS2_ik0, 'L0_xattn_w_q': _L0_xattn_in['w_q'], 'L0_xattn_w_k': _L0_xattn_in['w_k'], 'L0_xattn_w_v': _L0_xattn_in['w_v'], 'L0_xattn_w_o': _L0_xattn_in['w_o'], 'L0_ffn_gate_w': _L0_ffn_in['gate_w'], 'L0_ffn_shared_gate_w': _L0_ffn_in['shared_gate_w'], 'L0_ffn_shared_gate_up_w': _L0_ffn_in['shared_gate_up_w'], 'L0_ffn_shared_down_w': _L0_ffn_in['shared_down_w'], 'L0_ffn_expert_gate_up_w': _L0_ffn_in['expert_gate_up_w'], 'L0_ffn_expert_down_w': _L0_ffn_in['expert_down_w'], 'L1_xattn_W_q': _L1_xattn_in['W_q'], 'L1_xattn_b_q': _L1_xattn_in['b_q'], 'L1_xattn_W_k': _L1_xattn_in['W_k'], 'L1_xattn_b_k': _L1_xattn_in['b_k'], 'L1_xattn_W_v': _L1_xattn_in['W_v'], 'L1_xattn_b_v': _L1_xattn_in['b_v'], 'L1_xattn_W_o': _L1_xattn_in['W_o'], 'L1_xattn_b_o': _L1_xattn_in['b_o'], 'L1_ffn_gate_weight': _L1_ffn_in['gate_weight'], 'L1_ffn_gate_bias': _L1_ffn_in['gate_bias'], 'L1_ffn_w_gate': _L1_ffn_in['w_gate'], 'L1_ffn_w_up': _L1_ffn_in['w_up'], 'L1_ffn_w_down': _L1_ffn_in['w_down'], 'L1_ffn_shared_w_gate': _L1_ffn_in['shared_w_gate'], 'L1_ffn_shared_w_up': _L1_ffn_in['shared_w_up'], 'L1_ffn_shared_w_down': _L1_ffn_in['shared_w_down'], 'L1_ffn_anchor_w_gate': _L1_ffn_in['anchor_w_gate'], 'L1_ffn_anchor_w_up': _L1_ffn_in['anchor_w_up'], 'L1_ffn_anchor_w_down': _L1_ffn_in['anchor_w_down']}

def reference(x, ctx_1024, mask_1x1xSxS2_ik0, L0_xattn_w_q, L0_xattn_w_k, L0_xattn_w_v, L0_xattn_w_o, L0_ffn_gate_w, L0_ffn_shared_gate_w, L0_ffn_shared_gate_up_w, L0_ffn_shared_down_w, L0_ffn_expert_gate_up_w, L0_ffn_expert_down_w, L1_xattn_W_q, L1_xattn_b_q, L1_xattn_W_k, L1_xattn_b_k, L1_xattn_W_v, L1_xattn_b_v, L1_xattn_W_o, L1_xattn_b_o, L1_ffn_gate_weight, L1_ffn_gate_bias, L1_ffn_w_gate, L1_ffn_w_up, L1_ffn_w_down, L1_ffn_shared_w_gate, L1_ffn_shared_w_up, L1_ffn_shared_w_down, L1_ffn_anchor_w_gate, L1_ffn_anchor_w_up, L1_ffn_anchor_w_down):
    import jax
    import jax.numpy as jnp

    def _L0_xattn_ref(query, key, value, masked_val, w_q, w_k, w_v, w_o):
        import jax, jax.numpy as jnp
        import numpy as np
        D_MODEL = 256
        H = 16
        D_K = D_MODEL // H
        NEG_INF = -1000000000.0
        B, Sq, _ = query.shape
        Sk = key.shape[1]
        Q = (query @ w_q.T).reshape(B, Sq, H, D_K).transpose(0, 2, 1, 3)
        K = (key @ w_k.T).reshape(B, Sk, H, D_K).transpose(0, 2, 1, 3)
        V = (value @ w_v.T).reshape(B, Sk, H, D_K).transpose(0, 2, 1, 3)
        scores = jnp.einsum('bhqd,bhkd->bhqk', Q, K) / jnp.sqrt(jnp.float32(D_K))
        scores = jnp.where(masked_val == 0, NEG_INF, scores)
        probs = jax.nn.softmax(scores, axis=-1)
        ctx = jnp.einsum('bhqk,bhkd->bhqd', probs, V)
        ctx = ctx.transpose(0, 2, 1, 3).reshape(B, Sq, H * D_K)
        return ctx @ w_o.T

    def _L0_ffn_ref(hidden_states, gate_w, shared_gate_w, shared_gate_up_w, shared_down_w, expert_gate_up_w, expert_down_w):
        import jax, jax.numpy as jnp
        import numpy as np
        TOP_K = 8
        CAPACITY = 128

        def _silu(x):
            return x * jax.nn.sigmoid(x)
        B, S, H = hidden_states.shape
        x = hidden_states.reshape(-1, H)
        T = x.shape[0]
        E = gate_w.shape[1]
        Is = shared_gate_up_w.shape[1] // 2
        I = expert_gate_up_w.shape[2] // 2
        gu = x @ shared_gate_up_w
        shared = _silu(gu[:, :Is]) * gu[:, Is:] @ shared_down_w
        shared = shared * jax.nn.sigmoid(x @ shared_gate_w)
        logits = x @ gate_w
        probs = jax.nn.softmax(logits.astype(jnp.float32), axis=-1)
        w, idx = jax.lax.top_k(probs, TOP_K)
        w = (w / jnp.sum(w, axis=-1, keepdims=True)).astype(x.dtype)
        e_flat = idx.reshape(-1)
        w_flat = w.reshape(-1)
        A = e_flat.shape[0]
        tok = jnp.arange(A) // TOP_K
        onehot = jax.nn.one_hot(e_flat, E, dtype=jnp.int32)
        pos = jnp.take_along_axis(jnp.cumsum(onehot, axis=0) - 1, e_flat[:, None], axis=1)[:, 0]
        slot = jnp.minimum(pos, CAPACITY)
        buf = jnp.zeros((E, CAPACITY + 1, H), x.dtype).at[e_flat, slot].set(x[tok])
        gu_e = jnp.einsum('ech,ehf->ecf', buf, expert_gate_up_w)
        act = _silu(gu_e[..., :I]) * gu_e[..., I:]
        out_e = jnp.einsum('eci,eih->ech', act, expert_down_w)
        y = out_e[e_flat, slot] * w_flat[:, None]
        y = jnp.where((pos < CAPACITY)[:, None], y, jnp.zeros_like(y))
        y = y.reshape(T, TOP_K, H).sum(axis=1)
        return (y + shared).reshape(B, S, H)

    def _L1_xattn_ref(tgt, memory, W_q, b_q, W_k, b_k, W_v, b_v, W_o, b_o):
        import jax, jax.numpy as jnp
        import numpy as np
        D_MODEL = 256
        H = 16
        D_H = D_MODEL // H
        B, T_dec, _ = tgt.shape
        T_enc = memory.shape[1]
        Q = tgt @ W_q + b_q
        K = memory @ W_k + b_k
        V = memory @ W_v + b_v
        Q = Q.reshape(B, T_dec, H, D_H).transpose(0, 2, 1, 3)
        K = K.reshape(B, T_enc, H, D_H).transpose(0, 2, 1, 3)
        V = V.reshape(B, T_enc, H, D_H).transpose(0, 2, 1, 3)
        S = jnp.einsum('bhqd,bhkd->bhqk', Q, K) / jnp.sqrt(jnp.float32(D_H)).astype(Q.dtype)
        A = jax.nn.softmax(S, axis=-1)
        Y = jnp.einsum('bhqk,bhkd->bhqd', A, V)
        Y = Y.transpose(0, 2, 1, 3).reshape(B, T_dec, D_MODEL)
        return Y @ W_o + b_o

    def _L1_ffn_ref(hidden_states, gate_weight, gate_bias, w_gate, w_up, w_down, shared_w_gate, shared_w_up, shared_w_down, anchor_w_gate, anchor_w_up, anchor_w_down):
        import jax, jax.numpy as jnp
        import numpy as np
        HIDDEN = 256
        N_EXPERTS = 32
        MOE_I = 128
        N_GROUP = 4
        TOPK_GROUP = 2
        TOP_K = 6
        N_LOCAL_GROUPS = 16
        ANCHOR_I = 64
        SHARED_I = 128
        ROUTED_SCALE = 0.2
        ANCHOR_ALPHA = 0.1
        BATCH, SEQ = (1, 256)

        def _moe_forward(hidden_states, gate_weight, gate_bias, w_gate, w_up, w_down, shared_w_gate, shared_w_up, shared_w_down, anchor_w_gate, anchor_w_up, anchor_w_down):
            B, S, H = hidden_states.shape
            x = hidden_states.reshape(-1, H)
            T = x.shape[0]
            E = gate_weight.shape[0]
            L = anchor_w_gate.shape[0]
            logits = x @ gate_weight.T
            scores = jax.nn.sigmoid(logits)
            sc = scores + gate_bias
            grp = sc.reshape(T, N_GROUP, E // N_GROUP)
            group_scores = jax.lax.top_k(grp, 2)[0].sum(-1)
            _, gidx = jax.lax.top_k(group_scores, TOPK_GROUP)
            gmask = jax.nn.one_hot(gidx, N_GROUP, dtype=sc.dtype).sum(1)
            emask = jnp.repeat(gmask, E // N_GROUP, axis=1)
            masked = jnp.where(emask > 0, sc, -jnp.inf)
            _, topidx = jax.lax.top_k(masked, TOP_K)
            tw = jnp.take_along_axis(scores, topidx, axis=-1)
            tw = tw / (tw.sum(-1, keepdims=True) + 1e-20) * ROUTED_SCALE
            g = jnp.einsum('th,ehi->tei', x, w_gate)
            u = jnp.einsum('th,ehi->tei', x, w_up)
            eo = jnp.einsum('tei,eih->teh', jax.nn.silu(g) * u, w_down)
            cw = (jax.nn.one_hot(topidx, E, dtype=x.dtype) * tw[..., None]).sum(1)
            routed = jnp.einsum('te,teh->th', cw, eo)
            shared = jax.nn.silu(x @ shared_w_gate) * (x @ shared_w_up) @ shared_w_down
            lg = topidx[:, 0] // (E // L)
            ag = jnp.einsum('th,lhi->tli', x, anchor_w_gate)
            au = jnp.einsum('th,lhi->tli', x, anchor_w_up)
            ao = jnp.einsum('tli,lih->tlh', jax.nn.silu(ag) * au, anchor_w_down)
            acw = jax.nn.one_hot(lg, L, dtype=x.dtype)
            anchor = jnp.einsum('tl,tlh->th', acw, ao)
            out = routed + shared + ANCHOR_ALPHA * anchor
            return out.reshape(B, S, H)
        return _moe_forward(hidden_states, gate_weight, gate_bias, w_gate, w_up, w_down, shared_w_gate, shared_w_up, shared_w_down, anchor_w_gate, anchor_w_up, anchor_w_down)
    x = x + _L0_xattn_ref(_layernorm(x, axis=-1), ctx_1024, ctx_1024, mask_1x1xSxS2_ik0, L0_xattn_w_q, L0_xattn_w_k, L0_xattn_w_v, L0_xattn_w_o)
    x = x + _L0_ffn_ref(_layernorm(x, axis=-1), L0_ffn_gate_w, L0_ffn_shared_gate_w, L0_ffn_shared_gate_up_w, L0_ffn_shared_down_w, L0_ffn_expert_gate_up_w, L0_ffn_expert_down_w)
    x = x + _L1_xattn_ref(_layernorm(x, axis=-1), ctx_1024, L1_xattn_W_q, L1_xattn_b_q, L1_xattn_W_k, L1_xattn_b_k, L1_xattn_W_v, L1_xattn_b_v, L1_xattn_W_o, L1_xattn_b_o)
    x = x + _L1_ffn_ref(_layernorm(x, axis=-1), L1_ffn_gate_weight, L1_ffn_gate_bias, L1_ffn_w_gate, L1_ffn_w_up, L1_ffn_w_down, L1_ffn_shared_w_gate, L1_ffn_shared_w_up, L1_ffn_shared_w_down, L1_ffn_anchor_w_gate, L1_ffn_anchor_w_up, L1_ffn_anchor_w_down)
    return x

_drawn_inputs = setup_inputs


def setup_inputs(seed=0):
    import zlib

    import numpy as np

    out = dict(_drawn_inputs(seed))
    spreads = {'L1_xattn_b_q': (0.0, 0.526),
     'L1_xattn_b_k': (0.0, 0.8),
     'L1_xattn_b_v': (0.0, 0.1),
     'L1_xattn_b_o': (0.0, 0.1)}
    factors = {'L1_ffn_gate_weight': 8.0,
     'L1_ffn_gate_bias': 8.0,
     'L1_ffn_w_gate': 8.0,
     'L1_ffn_w_up': 8.0,
     'L1_ffn_w_down': 8.0,
     'L1_ffn_shared_w_gate': 7.193,
     'L1_ffn_shared_w_up': 6.779,
     'L1_ffn_shared_w_down': 6.872,
     'L1_ffn_anchor_w_gate': 8.0,
     'L1_ffn_anchor_w_up': 8.0,
     'L1_ffn_anchor_w_down': 8.0}
    for name, (base, spread) in spreads.items():
        noise = np.random.default_rng([zlib.crc32(name.encode()), seed]).standard_normal(out[name].shape)
        drawn = base * np.exp(spread * noise) if base else spread * noise
        out[name] = jnp.asarray(drawn.astype(out[name].dtype))
    for name, factor in factors.items():
        out[name] = (out[name] * factor).astype(out[name].dtype)
    return out
```

```python
import numpy as np
import concourse.bass as bass
from concourse import mybir
from contextlib import ExitStack

F32 = mybir.dt.float32
I32 = mybir.dt.int32
U32 = mybir.dt.uint32
ALU = mybir.AluOpType
ACT = mybir.ActivationFunctionType
AX = mybir.AxisListType

P = 128
D = 256
NT = 16
NB = 8
SK = 120
H = 16
ROW = 280
E0 = 64
CAP = 128
R1 = 32
NA = 16
E1 = R1 + NA
T1 = 128
TA = 32
K0 = 8
K1 = 7
BIG = 65536.0
OFF = 30000.0
NEG = -3.0e38
EPS = 1e-5
MAGIC = float(0x5F3759DF)


def constants():
    p = np.arange(P, dtype=np.float32)[:, None]
    j = np.arange(P, dtype=np.float32)[None, :]
    t = np.arange(NT, dtype=np.float32)[None, :, None] * P + p[:, :, None]
    k = np.arange(8, dtype=np.float32)[None, None, :]
    parts = [
        ("ident", (p == j)),
        ("upper", (p < j)),
        ("ones", np.ones((P, P))),
        ("d0", (t * K0 + k - OFF).reshape(P, -1)),
        ("d1", (t * K1 + k - OFF).reshape(P, -1)),
        ("nb0", np.broadcast_to(BIG - CAP * j[:, :E0], (P, E0))),
        ("iota", np.broadcast_to(j[:, :48], (P, 48))),
        ("step", np.broadcast_to(P * j[:, :16], (P, 16))),
        ("part", p),
        ("pad", np.full((P, 48), NEG)),
    ]
    at, place, cols = 0, {}, []
    for name, a in parts:
        place[name] = (at, a.shape[1])
        at += a.shape[1]
        cols.append(np.asarray(a, np.float32))
    return np.ascontiguousarray(np.concatenate(cols, 1)), place


class Queues:

    def __init__(self):
        self.lists = {e: [] for e in ("pe", "act", "dve", "pool", "sp")}
        self.count = {}

    def put(self, engine, sem, inc, fn, waits):
        q = self.lists[engine]
        for w in waits:
            for tok in (w if isinstance(w, list) else [w]):
                if tok is not None:
                    q.append(("wait", tok))
        self.count[sem] = self.count.get(sem, 0) + inc
        q.append(("do", fn, sem, inc))
        return (sem, self.count[sem])

    def pe(self, fn, *waits):
        return self.put("pe", "pe", 1, fn, waits)

    def act(self, fn, *waits):
        return self.put("act", "act", 1, fn, waits)

    def dve(self, fn, *waits):
        return self.put("dve", "dve", 1, fn, waits)

    def pool(self, fn, *waits):
        return self.put("pool", "pool", 1, fn, waits)

    def dma(self, sem, fn, *waits, engine="sp"):
        return self.put(engine, sem, 16, fn, waits)

    def wait(self, engine, *waits):
        for tok in waits:
            self.lists[engine].append(("wait", tok))

    def run(self, engine, eng, sems):
        seen = {}
        for item in self.lists[engine]:
            if item[0] == "wait":
                sem, n = item[1]
                if seen.get(sem, 0) < n:
                    eng.wait_ge(sems[sem], n)
                    seen[sem] = n
            else:
                _, fn, sem, inc = item
                fn(eng).then_inc(sems[sem], inc)


def build(nc, a, out):
    place = constants()[1]
    ncst = sum(n for _, n in place.values())
    buf0 = nc.dram_tensor("buf0", [E0 * P, ROW], F32)
    buf1 = nc.dram_tensor("buf1", [(T1 + TA) * P, ROW], F32)
    yb0 = nc.dram_tensor("yb0", [2048 * K0, D], F32)
    yb1 = nc.dram_tensor("yb1", [2048 * K1, D], F32)
    x_d = a["x"].rearrange("b s d -> (b s) d").rearrange("(n p) d -> p n d", p=P)
    out_d = out.rearrange("b s d -> (b s) d").rearrange("(n p) d -> p n d", p=P)
    q = Queues()

    with ExitStack() as ctx:
        def sb(name, shape, dt=F32):
            return ctx.enter_context(nc.sbuf_tensor(name, shape, dt))

        PS = ctx.enter_context(nc.psum_tensor("PS", [P, 8, 512], F32))
        C = sb("C", [P, ncst])

        def cst(name):
            o, n = place[name]
            return C[:, o:o + n]

        ident, upper, ones = cst("ident"), cst("upper"), cst("ones")
        X = sb("X", [P, NT, D])
        H2T = sb("H2T", [P, 2, NT * P])
        HR = sb("HR", [P, 4, ROW])
        WS1 = sb("WS1", [P, 768])
        BX = sb("BX", [P, 4, ROW])
        XT = sb("XT", [P, 3, 2, P])
        SL = sb("SL", [P, 2, P])
        AC = sb("AC", [P, 2, P])
        AT = sb("AT", [P, 2, P])
        YT = sb("YT", [P, 3, D])
        DF = sb("DF", [P, T1 + TA])
        WC = sb("WC", [P, T1 + TA])
        DI = sb("DI", [P, T1 + TA], I32)
        TE = sb("TE", [P, T1 + TA])
        TI = sb("TI", [P, T1 + TA], I32)
        JK = sb("JK", [P, 2, 2, 8])
        SS_ = sb("SS_", [P, 2, 512])
        AS_ = sb("AS_", [P, 4, 512])
        BO = sb("BO", [1, D])
        BQK = sb("BQK", [P, 4])
        GB = sb("GB", [P, R1])
        WR1 = sb("WR1", [P, 2, R1])
        SIG = sb("SIG", [P, NT])
        ST = sb("ST", [P, 2, 2, 6])
        MV = sb("MV", [P, 2, 2, 2])
        NW = sb("NW", [P, 2, 6, 2])
        NWI = sb("NWI", [P, 2, 2, 2], I32)
        MX = sb("MX", [P, 2, 8])
        RC = sb("RC", [P, 2, H])
        T1_ = sb("T1_", [P, 2, 64])
        T2_ = sb("T2_", [P, 2, 64])
        KEY = sb("KEY", [P, 2, 64])
        SUM = sb("SUM", [P, 2, 64])
        M8 = sb("M8", [P, 2, 8])
        G8 = sb("G8", [P, 2, 4, 8])
        GS = sb("GS", [P, 2, 16])
        R8 = sb("R8", [P, 2, 2, 8])
        IX = sb("IX", [P, 2, 8], U32)
        AX1 = sb("AX1", [P, 2, 1], U32)
        EW8 = sb("EW8", [P, 2, 8])
        SC1 = sb("SC1", [P, 2, 8])
        RI = sb("RI", [P, 4, 8], I32)
        K8 = sb("K8", [P, 2, 8])
        NBT = sb("NBT", [P, E1])
        TOT = sb("TOT", [P, E1])
        TIL = sb("TIL", [P, E1])
        CUM = sb("CUM", [P, E1])
        CNT = sb("CNT", [P, 2])
        CMP = sb("CMP", [P, E1])
        R = sb("R", [P, 32768])

        at = [0]

        def reg(n):
            at[0] += n
            return R[:, at[0] - n:at[0]]

        KBD = reg(4 * 960).rearrange("p (s c n) -> p s c n", s=2, c=2)
        AW = reg(8 * 512).rearrange("p (w c n) -> p w c n", w=8, c=2)
        KT = reg(1920).rearrange("p (c n) -> p c n", c=2)
        CT = reg(1920).rearrange("p (c n) -> p c n", c=2)
        VA = reg(NB * H * 17).rearrange("p (b h d) -> p b h d", b=NB, h=H)
        YL = reg(2 * 2048).rearrange("p (s n) -> p s n", s=2)
        SALL = reg(NT * E1).rearrange("p (n e) -> p n e", n=NT)
        PALL = reg(NT * E1).rearrange("p (n e) -> p n e", n=NT)
        lo = at[0]
        HH = reg(2 * 512).rearrange("p (s n d) -> p s n d", s=2, n=2)
        HT = reg(2 * 512).rearrange("p (s c t) -> p s c t", s=2, c=2)
        QT = reg(2 * 512).rearrange("p (s c t) -> p s c t", s=2, c=2)
        SM = reg(3 * 960).rearrange("p (s h k) -> p s h k", s=3, h=8)
        PT = reg(4 * 512).rearrange("p (s h t) -> p s h t", s=4, h=4)
        CX = reg(2 * 256).rearrange("p (s d) -> p s d", s=2)
        CXT = reg(2 * 256).rearrange("p (s c t) -> p s c t", s=2, c=2)
        CAPM = reg(2 * SK).rearrange("p (n k) -> p n k", n=2)
        MSK = reg(2 * SK).rearrange("p (n k) -> p n k", n=2).bitcast(I32)
        MF = reg(2 * SK).rearrange("p (n k) -> p n k", n=2)
        BV = reg(D)
        LG = reg(128).rearrange("p (s e) -> p s e", s=2)
        RP = reg(128).rearrange("p (s e) -> p s e", s=2)
        SEL = reg(128).rearrange("p (s e) -> p s e", s=2)
        EQ = reg(8 * R1)
        WR0 = reg(130).rearrange("p (c n) -> p c n", c=2)
        assert at[0] <= 32768
        Z = AS_[:, 0:2, :].rearrange("p a n -> p (a n)")[:, 0:560]
        EWR = R[:, lo:lo + 6 * 768].rearrange("p (s n) -> p s n", s=6)
        SG0 = R[:, lo + 4608:lo + 4608 + 2048].rearrange("p (c n) -> p c n", c=2)
        SD0 = R[:, lo + 6656:lo + 6656 + 1024].rearrange("p (c n) -> p c n", c=4)
        W1 = R[:, 0:24576].rearrange("p (e n) -> p e n", e=R1)
        WA = R[:, 24576:28672].rearrange("p (l n) -> p l n", l=NA)
        WD = R[0:64, 28672:32768].rearrange("p (l n) -> p l n", l=NA)
        YF = R[:, 0:4 * 2048].rearrange("p (s n) -> p s n", s=4)

        def ld(sem, dst, src, *waits, engine="sp"):
            return q.dma(sem, lambda e: e.dma_start(dst, src), *waits, engine=engine)

        def chunks(name):
            return a[name].rearrange("(c p) n -> p c n", p=P)

        t_c = ld("l_c", C[:, :], a["cst"])
        t_x = [ld(f"l_x{i}", X[:, 4 * i:4 * i + 4, :], x_d[:, 4 * i:4 * i + 4, :]) for i in range(4)]
        names = ["wq0", "wk0", "wv0", "wo0", "wq1", "wk1", "wv1", "wo1"]
        t_ct = ld("l_ct", CT, chunks("ctxT"))
        t_w = {}
        for i in (1, 0, 2, 3):
            t_w[names[i]] = ld("l_" + names[i], AW[:, i, :, :], chunks(names[i]))
        t_mask = ld("l_mask", MSK, a["mask"].rearrange("(n p) k -> p n k", p=P))
        t_wr0 = ld("l_wr0", WR0, chunks("gate0"))
        for i in range(4, 8):
            t_w[names[i]] = ld("l_" + names[i], AW[:, i, :, :], chunks(names[i]))
        t_small = [
            ld("l_s0", BV, a["bv"].partition_broadcast(P)),
            ld("l_s1", BO[:, :], a["bo"].unsqueeze(0)),
            ld("l_s2", BQK[:, :], a["bqk"]),
            ld("l_s4", GB[:, :], a["gbias"].partition_broadcast(P)),
            ld("l_s5", WR1[:, :, :], chunks("gate1")),
            ld("l_s6", WS1[:, 0:256].rearrange("p (c n) -> p c n", c=2), chunks("sg1")),
            ld("l_s7", WS1[:, 256:512].rearrange("p (c n) -> p c n", c=2), chunks("su1")),
            ld("l_s8", WS1[:, 512:768], a["sd1"]),
        ]

        t_z = q.pool(lambda e: e.memset(Z, 0.0))
        t_kz = q.pool(lambda e: e.memset(KBD, 0.0))
        t_va1 = q.pool(lambda e: e.memset(VA[:, :, :, 16:17], 1.0))
        t_sum0 = q.pool(lambda e: e.memset(SUM[:, :, :], 0.0))
        t_r8 = q.pool(lambda e: e.memset(R8[:, :, :, :], NEG))
        t_gs = q.pool(lambda e: e.memset(GS[:, :, :], NEG))

        def clear(sem, tensor, r0, n):
            flat = tensor.rearrange("a b -> (a b)").rearrange("(p r n) -> p r n", p=P, n=560)
            dst = flat[:, r0:r0 + n, :]
            src = Z.unsqueeze(1).broadcast_to([P, n, 560])
            return q.dma(sem, lambda e: e.dma_start(dst, src), t_z, engine="act")

        clr = {"b0": [], "y0": [], "b1": []}
        todo = [("b0", buf0, r, 4) for r in range(0, 32, 4)]
        y0f = yb0.rearrange("a b -> (a b)").rearrange("(p r n) -> p r n", p=P, n=512)

        def clear_y(r0, n):
            dst = y0f[:, r0:r0 + n, :]
            src = Z[:, 0:512].unsqueeze(1).broadcast_to([P, n, 512])
            return q.dma("z_y0", lambda e: e.dma_start(dst, src), t_z, engine="act")

        for r in range(0, 32, 4):
            clr["b0"].append(clear("z_b0", buf0, r, 4))
        later = [("y0", r, 4) for r in range(0, 64, 4)] + [("b1", r, 4) for r in range(0, 80, 4)]

        def clear_some(n):
            for _ in range(n):
                if later:
                    kind, r, m = later.pop(0)
                    clr[kind].append(clear_y(r, m) if kind == "y0" else clear("z_b1", buf1, r, m))

        t = q.dve(lambda e: e.tensor_scalar(MF, MSK, 0.0, None, ALU.is_equal), t_mask)
        t2 = q.dve(lambda e: e.tensor_scalar(CAPM, MF, NEG, -NEG, ALU.mult, ALU.add), t)
        t_cap = q.dve(lambda e: e.scalar_tensor_tensor(
            out=CAPM, in0=MF, scalar=-4.0e9, in1=CAPM, op0=ALU.mult, op1=ALU.add), t2)

        free = {}

        def got(key):
            return free.get(key)

        misc = [0]

        def misc_half():
            i = misc[0] % 2
            misc[0] += 1
            return ("M", i), PS[:, (5, 7)[i], 0:256]

        def layernorm(n0, s, dst, waits):
            out_t = []
            st = []
            for i in range(2):
                t = q.dve(lambda e, i=i: e.bn_stats(ST[:, s, i, :], X[:, n0 + i, :]), waits[i])
                st.append(t)
            mv = []
            for i in range(2):
                mv.append(q.dve(lambda e, i=i: e.bn_aggr(MV[:, s, i, :], ST[:, s, i, :]), st[i]))
            V, A_, B_, Rr = (NW[:, s, j, :] for j in range(4))
            t = q.dve(lambda e: e.tensor_scalar(V, MV[:, s, :, 1], EPS, None, ALU.add), mv[1])
            t = q.dve(lambda e: e.tensor_scalar(NWI[:, s, 0, :], V.bitcast(I32), 1, None,
                                                ALU.logical_shift_right), t)
            t = q.dve(lambda e: e.tensor_scalar(NWI[:, s, 1, :], NWI[:, s, 0, :], -1.0, MAGIC,
                                                ALU.mult, ALU.add), t)
            cur = NWI[:, s, 1, :].bitcast(F32)
            for it in range(3):
                t = q.dve(lambda e, cur=cur: e.tensor_tensor(A_, cur, cur, ALU.mult), t)
                t = q.dve(lambda e: e.tensor_tensor(A_, A_, V, ALU.mult), t)
                t = q.dve(lambda e: e.tensor_scalar(B_, A_, -0.5, 1.5, ALU.mult, ALU.add), t)
                t = q.dve(lambda e, cur=cur: e.tensor_tensor(Rr, cur, B_, ALU.mult), t)
                cur = Rr
            for i in range(2):
                out_t.append(q.dve(lambda e, i=i: e.tensor_scalar(
                    dst(i), X[:, n0 + i, :], MV[:, s, i, 0:1], Rr[:, i:i + 1], ALU.subtract, ALU.mult),
                    t, waits[2 + i]))
            return out_t

        def mm(e, out_, pairs):
            for i, (l, r) in enumerate(pairs):
                m = e.matmul(out_, l, r, start=(i == 0), stop=(i == len(pairs) - 1))
            return m

        def tr2(e, out_, src):
            e.transpose(out_[:, 0:128], src[:, 0:128], ident)
            return e.transpose(out_[:, 128:256], src[:, 128:256], ident)

        def attention(l, x_ready, before, behind):
            wq, wk, wv, wo = (AW[:, 4 * l + i, :, :] for i in range(4))
            tw = [t_w[names[4 * l + i]] for i in range(4)]
            kt_t = []
            for c in range(2):
                for half in range(2):
                    bank = 2 * c + half
                    t = q.pe(lambda e, c=c, half=half, bank=bank: mm(
                        e, PS[:, bank, 0:480],
                        [(wk[:, k, c * P:c * P + P], CT[:, k, half * 480:half * 480 + 480]) for k in range(2)]),
                        tw[1], t_ct, got(("S", bank // 2)), got(("KT", 0)), got(("KT", 1)), got("E"))
                    dst = KT[:, c, half * 480:half * 480 + 480]
                    if l == 0:
                        t = q.act(lambda e, bank=bank, dst=dst: e.copy(dst, PS[:, bank, 0:480]), t)
                    else:
                        t = q.act(lambda e, bank=bank, dst=dst, c=c: e.activation(
                            dst, PS[:, bank, 0:480], ACT.Identity, bias=BQK[:, 2 + c:3 + c]), t, t_small)
                    kt_t.append(t)
            free[("S", 0)], free[("S", 1)] = kt_t[1], kt_t[3]
            qt_t, v_t, kb_t, h_t, ht_t = {}, {}, {}, {}, {}
            sm_t, ex_t, pt_t, x_t, c_t, cxt_t = {}, {}, {}, {}, {}, {}

            def pre0(b):
                s = b % 2
                kt_done = kt_t
                for h in range(8):
                    kb_t[b] = q.dma(f"kb{s}", lambda e, h=h: e.dma_start(
                        KBD[16 * h:16 * h + 16, s, :, h * SK:h * SK + SK],
                        KT[16 * h:16 * h + 16, :, b * SK:b * SK + SK]), kt_done, t_kz, got(("KBD", s)))
                free[("KT", s)] = kb_t[b]
                h_t[b] = layernorm(2 * b, 0, lambda i: HH[:, s, i, :],
                                   [x_ready(2 * b), x_ready(2 * b + 1), got(("HH", s, 0)), got(("HH", s, 1))])

            def pre1(b):
                s = b % 2
                ht_t[b] = []
                for i in range(2):
                    key, m = misc_half()
                    t = q.pe(lambda e, i=i, m=m: tr2(e, m, HH[:, s, i, :]), h_t[b][i], t_c, got(key))
                    free[("HH", s, i)] = t
                    t = q.act(lambda e, i=i, m=m: e.copy(
                        HT[:, s, :, i * P:i * P + P], m.rearrange("p (c t) -> p c t", c=2)), t, got(("HT", s)))
                    free[key] = t
                    ht_t[b].append(t)

            def pre2(b):
                s = b % 2
                qt_t[b] = []
                for c in range(2):
                    key, m = misc_half()
                    t = q.pe(lambda e, c=c, m=m: mm(
                        e, m, [(wq[:, k, c * P:c * P + P], HT[:, s, k, :]) for k in range(2)]),
                        ht_t[b], tw[0], got(key))
                    free[("HT", s)] = t
                    if l == 0:
                        t = q.act(lambda e, c=c, m=m: e.copy(QT[:, s, c, :], m), t, got(("QT", s)))
                    else:
                        t = q.act(lambda e, c=c, m=m: e.activation(
                            QT[:, s, c, :], m, ACT.Identity, bias=BQK[:, c:c + 1]), t, got(("QT", s)), t_small)
                    free[key] = t
                    qt_t[b].append(t)

            def pre3(b):
                key, m = misc_half()
                t = q.pe(lambda e: mm(
                    e, m[0:SK, :], [(CT[:, k, b * SK:b * SK + SK], wv[:, k, :]) for k in range(2)]),
                    tw[2], t_ct, got(key))
                dst = VA[0:SK, b, :, 0:16]
                src = m[0:SK, :].rearrange("p (h d) -> p h d", h=H)
                if l == 0:
                    t = q.dve(lambda e: e.tensor_copy(dst, src), t, t_va1)
                else:
                    t = q.dve(lambda e: e.tensor_tensor(
                        dst, src, BV[0:SK, :].rearrange("p (h d) -> p h d", h=H), ALU.add), t, t_small, got("VA"))
                free[key] = t
                v_t[b] = t

            def scores(u):
                n, c = u // 2, u % 2
                b, s = n // 2, (n // 2) % 2
                w = u % 2

                def go(e):
                    for half in range(2):
                        m = e.matmul(PS[:, 2 * w + half, :].rearrange("p (h k) -> p h k", h=4)[:, :, 0:SK],
                                     QT[:, s, c, (n % 2) * P:(n % 2) * P + P],
                                     KBD[:, s, c, half * 480:half * 480 + 480].rearrange("p (h k) -> p h k", h=4),
                                     start=True, stop=True)
                    return m

                t = q.pe(go, qt_t[b], kb_t[b], got(("S", w)))
                free[("QT", s)] = free[("KBD", s)] = t
                S = PS[:, 2 * w:2 * w + 2, :].rearrange("p w (h k) -> p (w h) k", k=P)[:, :, 0:SK]
                z = u % 3
                sm = SM[:, z, :, :]
                if l == 0:
                    t = q.dve(lambda e: e.scalar_tensor_tensor(
                        out=sm, in0=S, scalar=-4.0e9,
                        in1=CAPM[:, n % 2, :].unsqueeze(1).broadcast_to([P, 8, SK]),
                        op0=ALU.max, op1=ALU.min), t, t_cap, got(("SM", z)))
                    free[("S", w)] = t
                    t = q.dve(lambda e: e.tensor_reduce(MX[:, w, :], sm, AX.X, ALU.max), t)
                    t = q.dve(lambda e: e.tensor_tensor(
                        sm, sm, MX[:, w, :].unsqueeze(2).broadcast_to([P, 8, SK]), ALU.subtract), t)
                else:
                    t = q.dve(lambda e: e.tensor_reduce(MX[:, w, :], S, AX.X, ALU.max), t)
                    t = q.dve(lambda e: e.tensor_tensor(
                        sm, S, MX[:, w, :].unsqueeze(2).broadcast_to([P, 8, SK]), ALU.subtract),
                        t, got(("SM", z)))
                    free[("S", w)] = t
                ex_t[u] = q.act(lambda e: e.activation(sm, sm, ACT.Exp, scale=0.25), t)

            def turn(u, half):
                z = u % 3
                pt_t.setdefault(u, [])
                for half in (half,):
                    def go(e, half=half):
                        for i in range(4):
                            m = e.transpose(PS[0:SK, 4, i * P:i * P + P], SM[:, z, 4 * half + i, :], ident)
                        return m
                    t = q.pe(go, ex_t[u], got("PT"))
                    free[("SM", z)] = t
                    r = 2 * (u % 2) + half
                    src = PS[0:SK, 4, :].rearrange("p (h t) -> p h t", h=4)
                    if l == 1 and half == 1:
                        t = q.dve(lambda e, r=r, src=src: e.tensor_copy(PT[0:SK, r, :, :], src), t, got(("PTS", r)))
                    else:
                        t = q.act(lambda e, r=r, src=src: e.copy(PT[0:SK, r, :, :], src), t, got(("PTS", r)))
                    free["PT"] = t
                    pt_t[u].append(t)

            def values(u):
                n, c = u // 2, u % 2
                b = n // 2

                def go(e):
                    for i in range(8):
                        h = 8 * c + i
                        m = e.matmul(PS[:, 6, h * 17:h * 17 + 17], PT[0:SK, 2 * (u % 2) + i // 4, i % 4, :],
                                     VA[0:SK, b, h, :], start=True, stop=True)
                    return m
                t = q.pe(go, pt_t[u], v_t[b], got("O"))
                free[("PTS", 2 * (u % 2))] = free[("PTS", 2 * (u % 2) + 1)] = t
                free["VA"] = t
                c_t[u] = t

            def fin1(n):
                s = n % 2
                O = PS[:, 6, 0:272].rearrange("p (h d) -> p h d", h=H)
                t = q.dve(lambda e: e.reciprocal(RC[:, s, :], O[:, :, 16]), c_t[2 * n + 1])
                t = q.dve(lambda e: e.tensor_tensor(
                    CX[:, s, :].rearrange("p (h d) -> p h d", h=H), O[:, :, 0:16],
                    RC[:, s, :].unsqueeze(2).broadcast_to([P, H, 16]), ALU.mult), t, got(("CX", s)))
                free["O"] = t
                c_t[("x", n)] = t

            def fin2(n):
                s = n % 2
                key, m = misc_half()
                t = q.pe(lambda e: tr2(e, m, CX[:, s, :]), c_t[("x", n)], got(key))
                free[("CX", s)] = t
                t = q.act(lambda e: e.copy(CXT[:, s, :, :], m.rearrange("p (c t) -> p c t", c=2)),
                          t, got(("CXT", s)))
                free[key] = t
                cxt_t[n] = t

            def fin3(n):
                s = n % 2
                key, m = misc_half()

                def go(e):
                    pairs = [(CXT[:, s, k, :], wo[:, k, :]) for k in range(2)]
                    if l == 1:
                        pairs.append((ones[0:1, :], BO[0:1, :]))
                    return mm(e, m, pairs)
                t = q.pe(go, cxt_t[n], tw[3], got(key), t_small if l else None)
                free[("CXT", s)] = t
                t = q.dve(lambda e: e.tensor_tensor(X[:, n, :], m, X[:, n, :], ALU.add), t)
                free[key] = t
                x_t[n] = t

            NU = 2 * NT
            plan = {}

            def at_step(s, fn, *args):
                plan.setdefault(s, []).append((fn, args))

            for b in range(NB):
                for n in (2 * b, 2 * b + 1):
                    for i, f in enumerate(before):
                        at_step(4 * b - 6 + i, f, n)
                at_step(4 * b - 4, pre0, b)
                at_step(4 * b - 3, pre1, b)
                at_step(4 * b - 2, pre2, b)
                at_step(4 * b - 1, pre3, b)
            for u in range(NU + 3):
                if 2 <= u < NU + 2:
                    at_step(u, turn, u - 2, 0)
                if u < NU:
                    at_step(u, scores, u)
                if 2 <= u < NU + 2:
                    at_step(u, turn, u - 2, 1)
                if u >= 3:
                    at_step(u, values, u - 3)
            for n in range(NT):
                at_step(2 * n + 4, fin1, n)
                at_step(2 * n + 5, fin2, n)
                at_step(2 * n + 6, fin3, n)
            for b in range(NB):
                for i, f in enumerate(behind):
                    at_step(4 * b + 8 + i, f, b, x_t)
            for s in sorted(plan):
                for fn, args in plan[s]:
                    fn(*args)
                clear_some(1)

        h2_t, h2T_t, sel_t, w_t, sc_t, rt_free = {}, {}, {}, {}, {}, {}

        def norm2(b, x_t):
            h2_t[b] = layernorm(2 * b, 1, lambda i: HR[:, (2 * b + i) % 4, 0:D],
                                [x_t[2 * b], x_t[2 * b + 1], got(("HR", 2 * b % 4)), got(("HR", (2 * b + 1) % 4))])

        def turn2(b, x_t):
            for i in range(2):
                n = 2 * b + i
                key, m = misc_half()
                t = q.pe(lambda e, n=n, m=m: tr2(e, m, HR[:, n % 4, 0:D]), h2_t[b][i], got(key))
                t2 = q.act(lambda e, n=n, m=m: e.copy(
                    H2T[:, :, n * P:n * P + P], m.rearrange("p (c t) -> p c t", c=2)), t, got("H2T"))
                free[key] = t2
                h2T_t[n] = t2

        def route0(b, x_t):
            for i in range(2):
                n = 2 * b + i
                s = n % 2
                hr = HR[:, n % 4, :]
                key, RT = misc_half()
                t = q.pe(lambda e, n=n, RT=RT: mm(
                    e, RT[:, 0:65], [(H2T[:, k, n * P:n * P + P], WR0[:, k, :]) for k in range(2)]),
                    h2T_t[n], t_wr0, got(key))
                tl = q.dve(lambda e, s=s, RT=RT: e.tensor_copy(LG[:, s, :], RT[:, 0:64]), t)
                t = q.dve(lambda e, n=n, RT=RT: e.tensor_copy(SIG[:, n:n + 1], RT[:, 64:65]), t)
                free[key] = t
                ta = q.act(lambda e, n=n: e.activation(SIG[:, n:n + 1], SIG[:, n:n + 1], ACT.Exp, scale=-1.0), t)
                tm = q.dve(lambda e, s=s: e.max(M8[:, s, :], LG[:, s, :]), tl, got(("M8", s)))
                ti = q.dve(lambda e, s=s: e.max_index(IX[:, s, :], M8[:, s, :], LG[:, s, :]), tm)
                tr = q.dve(lambda e, s=s: e.match_replace(RP[:, s, :], M8[:, s, :], LG[:, s, :], NEG), tm)
                sel_t[n] = q.dve(lambda e, s=s: e.tensor_tensor(
                    SEL[:, s, :], RP[:, s, :], LG[:, s, :], ALU.not_equal), tr, got(("SEL", s)))
                tn = q.dve(lambda e, s=s: e.tensor_scalar(SC1[:, s, 0:1], M8[:, s, 0:1], -1.0, None, ALU.mult),
                           tm, got(("M8", s)))
                te = q.act(lambda e, s=s: e.activation(
                    EW8[:, s, :], M8[:, s, :], ACT.Exp, bias=SC1[:, s, 0:1], accum_out=SC1[:, s, 1:2]), tn)
                free[("M8", s)] = te
                tc = q.dve(lambda e, hr=hr, s=s: e.tensor_copy(hr[:, 256:264], IX[:, s, :]), ti, got(("HR", n % 4)))
                td = q.act(lambda e, hr=hr, n=n: e.copy(hr[:, 264:272], cst("d0")[:, 8 * n:8 * n + 8]),
                           got(("HR", n % 4)))
                t = q.dve(lambda e, s=s: e.reciprocal(SC1[:, s, 2:3], SC1[:, s, 1:2]), te)
                t = q.dve(lambda e, hr=hr, s=s: e.tensor_scalar(
                    hr[:, 272:280], EW8[:, s, :], SC1[:, s, 2:3], None, ALU.mult), t)
                t1 = q.dve(lambda e, n=n: e.tensor_scalar(SIG[:, n:n + 1], SIG[:, n:n + 1], 1.0, None, ALU.add), ta)
                t1 = q.dve(lambda e, n=n: e.reciprocal(SIG[:, n:n + 1], SIG[:, n:n + 1]), t1)
                free[("SIG", n)] = t1
                w_t[n] = [tc, td, t, h2_t[b][i], h2T_t[n]]

        sum_t = {0: t_sum0}

        def position(n, width, sel):
            s = n % 2

            key, m = misc_half()
            PO = m[:, 0:width]

            def go(e):
                return mm(e, PO, [(upper, sel), (ones, SUM[:, s, 0:width])])
            return q.pe(go, sel_t[n], sum_t[n], got(key)), key, PO

        def rows0(b, x_t):
            for i in range(2):
                n = 2 * b + i
                s = n % 2
                t, key, PO = position(n, 64, SEL[:, s, :])
                sum_t[n + 1] = q.dve(lambda e, s=s: e.tensor_tensor(
                    SUM[:, 1 - s, :], SUM[:, s, :], SEL[:, s, :], ALU.add), sel_t[n], sum_t[n],
                    got(("SUM", 1 - s)))
                free[("SUM", s)] = t
                t1 = q.dve(lambda e, s=s, PO=PO: e.scalar_tensor_tensor(
                    out=T1_[:, s, :], in0=PO, scalar=float(CAP), in1=SEL[:, s, :], op0=ALU.is_lt, op1=ALU.mult), t)
                free[("SEL", s)] = [t, t1]
                t2 = q.dve(lambda e, s=s, PO=PO: e.tensor_tensor(T2_[:, s, :], cst("nb0"), PO, ALU.subtract), t)
                free[key] = t2
                t = q.dve(lambda e, s=s: e.tensor_tensor(KEY[:, s, :], T1_[:, s, :], T2_[:, s, :], ALU.mult), t2)
                t = q.dve(lambda e, s=s: e.max(K8[:, s, :], KEY[:, s, :]), t)
                t = q.dve(lambda e, s=s, n=n: e.tensor_scalar(
                    RI[:, n % 4, :], K8[:, s, :], -1.0, BIG, ALU.mult, ALU.add), t, got(("HR", n % 4)))
                for k in range(K0):
                    free[("HR", n % 4)] = q.dma(f"sc{n % 4}", lambda e, n=n, k=k: e.indirect_dma_start(
                        out=buf0[:, :], out_offset=bass.IndirectOffsetOnAxis(
                            ap=RI[:, n % 4, k:k + 1].bitcast(U32), axis=0),
                        in_=HR[:, n % 4, :], in_offset=None, bounds_check=E0 * P - 1, oob_is_err=False),
                        t, w_t[n], clr["b0"][-1], engine="pool")

        def matches(i, scalar, *waits):
            s = i % 2
            ids, dd, ww = (BX[:, i % 4, o:o + 8] for o in (256, 264, 272))
            t1 = q.dve(lambda e: e.scalar_tensor_tensor(
                out=JK[:, s, 0, :], in0=ids, scalar=scalar, in1=dd, op0=ALU.is_equal, op1=ALU.mult,
                accum_out=DF[:, i:i + 1]), *waits)
            t2 = q.dve(lambda e: e.scalar_tensor_tensor(
                out=JK[:, s, 1, :], in0=ids, scalar=scalar, in1=ww, op0=ALU.is_equal, op1=ALU.mult,
                accum_out=WC[:, i:i + 1]))
            t3 = q.dve(lambda e: e.tensor_scalar(DI[:, i:i + 1], DF[:, i:i + 1], OFF, None, ALU.add), t1)
            free[("BXd", i % 4)] = t2
            return t2, t3

        def put_back(i, t, idx_t, w_tok, yb, bound):
            s = i % 3
            t = q.act(lambda e: e.activation(YT[:, s, :], PS[:, 4 + i % 2, 0:256], ACT.Copy, scale=WC[:, i:i + 1]),
                      t, w_tok, got(("YT", s)))
            free[("Y", i % 2)] = t
            free[("YT", s)] = q.dma(f"yt{s}", lambda e: e.indirect_dma_start(
                out=yb[:, :], out_offset=bass.IndirectOffsetOnAxis(ap=DI[:, i:i + 1].bitcast(U32), axis=0),
                in_=YT[:, s, :], in_offset=None, bounds_check=bound, oob_is_err=False),
                t, idx_t, engine="pool")
            return free[("YT", s)]

        def shared(nchunk, gate, up, down, w_tok, add):
            last = None
            for g in range(4):
                act_t = []
                for i in range(nchunk):
                    w = i % 2
                    rhs = [H2T[:, k, g * 512:g * 512 + 512] for k in range(2)]
                    tg = q.pe(lambda e, i=i, w=w, rhs=rhs: mm(
                        e, PS[:, 2 * w, :], [(gate(k, i), rhs[k]) for k in range(2)]),
                        [h2T_t[4 * g + j] for j in range(4)], w_tok, got(("shg", w)))
                    tu = q.pe(lambda e, i=i, w=w, rhs=rhs: mm(
                        e, PS[:, 2 * w + 1, :], [(up(k, i), rhs[k]) for k in range(2)]))
                    t = q.act(lambda e, w=w: e.activation(SS_[:, w, :], PS[:, 2 * w, :], ACT.Silu), tg,
                              got(("shs", w)))
                    t = q.dve(lambda e, i=i, w=w: e.tensor_tensor(
                        AS_[:, i, :], SS_[:, w, :], PS[:, 2 * w + 1, :], ALU.mult), t, tu, got(("sha", i)))
                    free[("shg", w)] = free[("shs", w)] = t
                    act_t.append(t)
                last = tu
                for j in range(4):
                    n = 4 * g + j
                    bank = 4 + j % 2
                    t = q.pe(lambda e, j=j, bank=bank: mm(
                        e, PS[:, bank, 0:256],
                        [(AS_[:, i, j * P:j * P + P], down(i)) for i in range(nchunk)]), act_t, got(("shy", bank)))
                    for i in range(nchunk):
                        free[("sha", i)] = t
                    free[("shy", bank)] = add(n, bank, t)
            free["H2T"] = last
            return t

        def barrier_banks():
            return [v for k, v in free.items() if isinstance(k, tuple) and k[0] in (
                "S", "M", "shg", "shy", "T", "GU", "Y", "T2")] + [free.get("O"), free.get("PT")]

        attention(0, lambda n: t_x[n // 4], [], [norm2, turn2, route0, rows0])
        scat0 = [free[("HR", i)] for i in range(4)]
        clear_some(100)
        a_done = [free[("SM", i)] for i in range(3)] + [free[("PTS", i)] for i in range(4)] + \
            [free[("CXT", i)] for i in range(2)] + [free[("QT", i)] for i in range(2)] + \
            [free[("CX", i)] for i in range(2)]
        banks = barrier_banks()
        t_s0 = [ld("l_sg0", SG0, chunks("sgu0"), a_done), ld("l_sd0", SD0, chunks("sd0"))]

        def e0_load(i):
            s = i % 6
            t1 = ld(f"ew{s}", EWR[:, s, 0:512].rearrange("p (c n) -> p c n", c=2),
                    a["egu"][i].rearrange("(c p) n -> p c n", p=P), got(("EW", s)))
            return [t1, ld(f"ew{s}", EWR[:, s, 512:768], a["ed"][i])]

        ew_t = {i: e0_load(i) for i in range(6)}

        def add0(n, bank, t):
            return q.dve(lambda e: e.scalar_tensor_tensor(
                out=X[:, n, :], in0=PS[:, bank, 0:256], scalar=SIG[:, n:n + 1], in1=X[:, n, :],
                op0=ALU.mult, op1=ALU.add), t, got(("SIG", n)))

        q.wait("pe", *[b for b in banks if b])
        q.wait("dve", clr["b1"][-1], clr["y0"][-1], clr["b0"][-1])
        shared(4, lambda k, i: SG0[:, k, i * P:i * P + P], lambda k, i: SG0[:, k, 512 + i * P:512 + i * P + P],
               lambda i: SD0[:, i, :], t_s0, add0)
        banks = [b for b in barrier_banks() if b]
        q.wait("pe", *banks)

        def bx_load(i, buf, *waits):
            return ld(f"bx{i % 4}", BX[:, i % 4, :], buf[i * P:i * P + P, :], *waits,
                      got(("BXp", i % 4)), got(("BXd", i % 4)))

        def stage_a(i, bx_t, scalar, *waits):
            s = i % 2
            t = q.pe(lambda e: tr2(e, PS[:, s, 0:256], BX[:, i % 4, 0:D]), bx_t[i], got(("T", s)))
            free[("BXp", i % 4)] = t
            t = q.dve(lambda e: e.tensor_copy(XT[:, i % 3, :, :], PS[:, s, 0:256].rearrange("p (c t) -> p c t", c=2)),
                      t, got(("XT", i % 3)))
            free[("T", s)] = t
            return t, matches(i, scalar, bx_t[i], *waits)

        bx_t, xt_t, mt_t, ac_t, sp0 = {}, {}, {}, {}, []
        for i in range(4):
            bx_t[i] = bx_load(i, buf0, scat0)
        for i in range(E0 + 2):
            if i < E0:
                xt_t[i], mt_t[i] = stage_a(i, bx_t, float(i))
                if i + 4 < E0:
                    bx_t[i + 4] = bx_load(i + 4, buf0)
            if 0 <= i - 1 < E0:
                j = i - 1
                s = j % 2

                def go(e, j=j, s=s):
                    for o in range(2):
                        m = mm(e, PS[:, 2 + s, o * P:o * P + P],
                               [(EWR[:, j % 6, k * 256 + o * P:k * 256 + o * P + P], XT[:, j % 3, k, :])
                                for k in range(2)])
                    return m
                t = q.pe(go, xt_t[j], ew_t[j], got(("GU", s)))
                free[("XT", j % 3)] = t
                t1 = q.act(lambda e, s=s: e.activation(SL[:, s, :], PS[:, 2 + s, 0:P], ACT.Silu), t, got(("SL", s)))
                t = q.dve(lambda e, s=s: e.tensor_tensor(AC[:, s, :], SL[:, s, :], PS[:, 2 + s, P:2 * P], ALU.mult),
                          t1, got(("AC", s)))
                free[("GU", s)] = free[("SL", s)] = t
                ac_t[j] = t
            if 0 <= i - 2 < E0:
                j = i - 2
                s = j % 2
                t = q.pe(lambda e, j=j, s=s: mm(e, PS[:, 4 + s, 0:256], [(AC[:, s, :], EWR[:, j % 6, 512:768])]),
                         ac_t[j], got(("Y", s)))
                free[("AC", s)] = t
                free[("EW", j % 6)] = t
                sp0.append(put_back(j, t, mt_t[j][1], mt_t[j][0], yb0, 2048 * K0 - 1)
                           if j else put_back(j, t, [mt_t[j][1], clr["y0"][-1]], mt_t[j][0], yb0, 2048 * K0 - 1))
                if j + 6 < E0:
                    ew_t[j + 6] = e0_load(j + 6)
        scat_y0 = sp0[-3:]

        banks = [b for b in barrier_banks() if b]
        q.wait("pe", *banks)
        e0_done = [free[("EW", i)] for i in range(6)]
        for e_ in ("dve", "act"):
            q.wait(e_, *e0_done)
        yv = yb0.rearrange("(t k) d -> t (k d)", k=K0)
        y_t, xc_t = {}, {}

        def y_load(n):
            y_t[n] = ld(f"yl{n % 2}", YL[:, n % 2, :], yv[n * P:n * P + P, :], scat_y0, got(("YL", n % 2)))

        def y_add(n):
            yl = YL[:, n % 2, :]
            t = q.dve(lambda e: e.tensor_reduce(yl[:, 0:256], yl.rearrange("p (k d) -> p d k", k=K0), AX.X, ALU.add),
                      y_t[n]) if False else None
            t = q.dve(lambda e: e.tensor_tensor(yl[:, 0:1024], yl[:, 0:1024], yl[:, 1024:2048], ALU.add), y_t[n])
            t = q.dve(lambda e: e.tensor_tensor(yl[:, 0:512], yl[:, 0:512], yl[:, 512:1024], ALU.add), t)
            t = q.dve(lambda e: e.tensor_tensor(yl[:, 0:256], yl[:, 0:256], yl[:, 256:512], ALU.add), t)
            t = q.dve(lambda e: e.tensor_tensor(X[:, n, :], X[:, n, :], yl[:, 0:256], ALU.add), t)
            free[("YL", n % 2)] = t
            xc_t[n] = t

        t_sum1 = q.dve(lambda e: e.memset(SUM[:, :, :], 0.0))
        sum_t[0] = t_sum1
        free.pop(("SUM", 0), None)
        free.pop(("SUM", 1), None)

        pos_t = {}

        def route1(b, x_t):
            for i in range(2):
                n = 2 * b + i
                s = n % 2
                hr = HR[:, n % 4, :]
                key, RT = misc_half()
                t = q.pe(lambda e, n=n, RT=RT: mm(
                    e, RT[:, 0:R1], [(H2T[:, k, n * P:n * P + P], WR1[:, k, :]) for k in range(2)]),
                    h2T_t[n], t_small, got(key))
                sco = T1_[:, s, 0:R1]
                scb = T2_[:, s, 0:R1]
                mk = KEY[:, s, 0:40]
                t = q.act(lambda e, sco=sco, RT=RT: e.activation(sco, RT[:, 0:R1], ACT.Exp, scale=-1.0), t,
                          got(("r1", s)))
                free[key] = t
                t = q.dve(lambda e, sco=sco: e.tensor_scalar(sco, sco, 1.0, None, ALU.add), t)
                t_sco = q.dve(lambda e, sco=sco: e.reciprocal(sco, sco), t)
                t_scb = q.dve(lambda e, sco=sco, scb=scb: e.tensor_tensor(scb, sco, GB[:, :], ALU.add), t_sco)
                for g in range(4):
                    tg = q.dve(lambda e, g=g, s=s, scb=scb: e.max(G8[:, s, g, :], scb[:, 8 * g:8 * g + 8]), t_scb)
                gs = GS[:, s, 0:10]
                t = q.dve(lambda e, s=s: e.tensor_tensor(GS[:, s, 0:4], G8[:, s, :, 0], G8[:, s, :, 1], ALU.add), tg, t_gs)
                tm = q.dve(lambda e, s=s, gs=gs: e.max(M8[:, s, :], gs), t)
                t = q.dve(lambda e, s=s: e.tensor_copy(R8[:, s, 0, 0:2], M8[:, s, 0:2]), tm, t_r8)
                t = q.dve(lambda e, s=s, gs=gs: e.match_replace(RP[:, s, 0:10], R8[:, s, 0, :], gs, -1.0e38), t)
                t = q.dve(lambda e, s=s: e.tensor_tensor(
                    CNTG[:, s, :], RP[:, s, 0:4], GS[:, s, 0:4], ALU.is_equal), t)
                tk = q.dve(lambda e, mk=mk: e.tensor_copy(mk[:, R1:40], cst("pad")[:, 0:8]))
                t = q.dve(lambda e, s=s, mk=mk, scb=scb: e.scalar_tensor_tensor(
                    out=mk[:, 0:R1].rearrange("p (g k) -> p g k", g=4),
                    in0=CNTG[:, s, :].unsqueeze(2).broadcast_to([P, 4, 8]), scalar=-1.0e30,
                    in1=scb.rearrange("p (g k) -> p g k", g=4), op0=ALU.mult, op1=ALU.add), t)
                tm = q.dve(lambda e, s=s, mk=mk: e.max(M8[:, s, :], mk), t, tk)
                ti = q.dve(lambda e, s=s, mk=mk: e.max_index(IX[:, s, :], M8[:, s, :], mk), tm)
                t = q.dve(lambda e, s=s: e.tensor_copy(R8[:, s, 1, 0:6], M8[:, s, 0:6]), tm)
                t = q.dve(lambda e, s=s, mk=mk: e.match_replace(RP[:, s, 16:56], R8[:, s, 1, :], mk, -2.0e38), t)
                ts = q.dve(lambda e, s=s, mk=mk, n=n: e.tensor_tensor(
                    SALL[:, n, 0:R1], RP[:, s, 16:16 + R1], mk[:, 0:R1], ALU.not_equal), t)
                ta = q.dve(lambda e, s=s: e.tensor_scalar(AX1[:, s, :], IX[:, s, 0:1], 1, None,
                                                          ALU.logical_shift_right), ti)
                idf = hr[:, 256:264]
                tc = q.dve(lambda e, idf=idf, s=s: e.tensor_copy(idf[:, 0:6], IX[:, s, 0:6]), ti, got(("HR", n % 4)))
                tc2 = q.dve(lambda e, idf=idf, s=s: e.tensor_copy(SC1[:, s, 4:5], AX1[:, s, :]), ta)
                tc3 = q.dve(lambda e, idf=idf, s=s: e.tensor_scalar(idf[:, 6:7], SC1[:, s, 4:5], float(R1), None,
                                                                    ALU.add), tc2)
                tc4 = q.dve(lambda e, idf=idf: e.memset(idf[:, 7:8], -1.0))
                sel_t[n] = q.dve(lambda e, s=s, n=n: e.tensor_scalar(
                    SALL[:, n, R1:E1], cst("iota")[:, 0:NA], SC1[:, s, 4:5], None, ALU.is_equal), tc2)
                td = q.act(lambda e, hr=hr, n=n: e.copy(hr[:, 264:272], cst("d1")[:, 8 * n:8 * n + 8]),
                           got(("HR", n % 4)))
                eq = EQ[:, 0:6 * R1].rearrange("p (k e) -> p k e", k=6)
                t = q.dve(lambda e, eq=eq, idf=idf: e.tensor_tensor(
                    eq, idf[:, 0:6].unsqueeze(2).broadcast_to([P, 6, R1]),
                    cst("iota")[:, 0:R1].unsqueeze(1).broadcast_to([P, 6, R1]), ALU.is_equal), tc)
                t = q.dve(lambda e, eq=eq, sco=sco: e.tensor_tensor(
                    eq, eq, sco.unsqueeze(1).broadcast_to([P, 6, R1]), ALU.mult), t)
                t = q.dve(lambda e, eq=eq, s=s: e.tensor_reduce(EW8[:, s, 0:6], eq, AX.X, ALU.add), t)
                t2 = q.dve(lambda e, s=s: e.tensor_reduce(SC1[:, s, 1:2], EW8[:, s, 0:6], AX.X, ALU.add), t)
                t2 = q.dve(lambda e, s=s: e.tensor_scalar(SC1[:, s, 1:2], SC1[:, s, 1:2], 1e-20, None, ALU.add), t2)
                t2 = q.dve(lambda e, s=s: e.reciprocal(SC1[:, s, 2:3], SC1[:, s, 1:2]), t2)
                t2 = q.dve(lambda e, s=s, hr=hr: e.tensor_scalar(
                    hr[:, 272:278], EW8[:, s, 0:6], SC1[:, s, 2:3], 0.2, ALU.mult, ALU.mult), t2)
                tw_ = q.dve(lambda e, hr=hr: e.memset(hr[:, 278:280], 0.1))
                free[("r1", s)] = t2
                w_t[n] = [tc, tc3, tc4, t2, tw_, td, ts, h2T_t[n], h2_t[b][i]]
                sel_t[n] = [sel_t[n], ts]

        def stay1(b, x_t):
            for i in range(2):
                n = 2 * b + i
                s = n % 2
                t, key, PO = position(n, E1, SALL[:, n, :])
                sum_t[n + 1] = q.dve(lambda e, s=s, n=n: e.tensor_tensor(
                    SUM[:, 1 - s, 0:E1], SUM[:, s, 0:E1], SALL[:, n, :], ALU.add), sel_t[n], sum_t[n],
                    got(("SUM", 1 - s)))
                free[("SUM", s)] = t
                t = q.dve(lambda e, n=n, PO=PO: e.tensor_copy(PALL[:, n, :], PO), t)
                free[key] = t
                pos_t[n] = t
                free[("HR", n % 4)] = ld(f"hs{n % 4}", rows_d[n * P:n * P + P, :], HR[:, n % 4, :], w_t[n])
                stay_t[n] = free[("HR", n % 4)]

        CNTG = sb("CNTG", [P, 2, 4])
        rows_d = nc.dram_tensor("rows_d", [2048, ROW], F32)
        stay_t = {}
        attention(1, lambda n: xc_t[n], [y_load, y_add], [norm2, turn2, route1, stay1])
        clear_some(100)

        key, PO = misc_half()
        t = q.pe(lambda e: mm(e, PO[:, 0:E1], [(ones, SUM[:, 0, 0:E1])]), sum_t[NT], got(key))
        t = q.dve(lambda e: e.tensor_copy(TOT[:, :], PO[:, 0:E1]), t)
        free[key] = t
        CM3 = R[:, lo:lo + E1 * 16].rearrange("p (e j) -> p e j", j=16)
        t = q.dve(lambda e: e.tensor_tensor(
            CM3, TOT[:, :].unsqueeze(2).broadcast_to([P, E1, 16]),
            cst("step").unsqueeze(1).broadcast_to([P, E1, 16]), ALU.is_gt), t, free[("HH", 0, 0)], free[("HH", 0, 1)])
        t = q.dve(lambda e: e.tensor_reduce(TIL[:, :], CM3, AX.X, ALU.add), t)
        tc = []
        for lo_, hi_, ini in ((0, R1, 0.0), (R1, E1, float(T1))):
            tc.append(q.dve(lambda e, lo_=lo_, hi_=hi_, ini=ini: e.tensor_tensor_scan(
                CUM[:, lo_:hi_], ones[:, 0:hi_ - lo_], TIL[:, lo_:hi_], ini, ALU.mult, ALU.add), t))
        t = q.dve(lambda e: e.tensor_tensor(NBT[:, :], CUM[:, :], TIL[:, :], ALU.subtract), tc)
        t_nb = q.dve(lambda e: e.tensor_scalar(NBT[:, :], NBT[:, :], -float(P), BIG, ALU.mult, ALU.add), t)
        t1 = q.dve(lambda e: e.tensor_scalar(CMP[:, 0:R1], CUM[:, 0:R1], cst("part"), 0.0, ALU.is_le, ALU.add,
                                             accum_out=CNT[:, 0:1]), tc)
        t2 = q.dve(lambda e: e.tensor_scalar(CNT[:, 1:2], cst("part"), float(T1), None, ALU.add))
        t2 = q.dve(lambda e: e.tensor_scalar(CMP[:, R1:E1], CUM[:, R1:E1], CNT[:, 1:2], 0.0, ALU.is_le, ALU.add,
                                             accum_out=SC1[:, 0, 5:6]), t2)
        t1 = q.dve(lambda e: e.tensor_scalar(CNT[:, 0:1], CNT[:, 0:1], float(R1 - 1), None, ALU.min), t1)
        t2 = q.dve(lambda e: e.tensor_scalar(CNT[:, 1:2], SC1[:, 0, 5:6], float(NA - 1), None, ALU.min), t2)
        banks = [b for b in barrier_banks() if b]
        q.wait("pe", *banks)

        def tiles(e):
            e.matmul(PS[:, 0, 0:T1], CNT[:, 0:1].broadcast_to([P, P]), ident, start=True, stop=True)
            return e.matmul(PS[:, 0, T1:T1 + TA], CNT[:, 1:2].broadcast_to([P, P]), ident[:, 0:TA],
                            start=True, stop=True)
        t = q.pe(tiles, t1, t2)
        t_ti = q.dve(lambda e: e.tensor_copy(TI[:, :], PS[:, 0, 0:T1 + TA]), t)
        t_te = q.dve(lambda e: e.tensor_copy(TE[:, 0:T1], PS[:, 0, 0:T1]), t)
        t_te = q.dve(lambda e: e.tensor_scalar(TE[:, T1:T1 + TA], PS[:, 0, T1:T1 + TA], float(R1), None, ALU.add), t)

        for n in range(4):
            pass
        hr_t = {}
        scat1 = []

        def row_load(n):
            hr_t[n] = ld(f"hl{n % 4}", HR[:, n % 4, :], rows_d[n * P:n * P + P, :], stay_t[n],
                         free[("HR", n % 4)], stay_t[NT - 4 + n] if n < 4 else None)

        for n in range(4):
            row_load(n)
        t_done = None
        for n in range(NT):
            s = n % 2
            t = q.dve(lambda e, s=s, n=n: e.tensor_tensor(T2_[:, s, 0:E1], NBT[:, :], PALL[:, n, :], ALU.subtract),
                      t_nb, pos_t[n])
            t = q.dve(lambda e, s=s, n=n: e.tensor_tensor(
                KEY[:, s, 0:E1], T2_[:, s, 0:E1], SALL[:, n, :], ALU.mult), t, sel_t[n])
            t_done = t
            t = q.dve(lambda e, s=s: e.max(K8[:, s, :], KEY[:, s, 0:E1]), t)
            t = q.dve(lambda e, s=s, n=n: e.tensor_scalar(
                RI[:, n % 4, :], K8[:, s, :], -1.0, BIG, ALU.mult, ALU.add), t,
                scat1[n - 4] if n >= 4 else None, scat0)
            for k in range(K1):
                tok = q.dma(f"sd{n % 4}", lambda e, n=n, k=k: e.indirect_dma_start(
                    out=buf1[:, :], out_offset=bass.IndirectOffsetOnAxis(
                        ap=RI[:, n % 4, k:k + 1].bitcast(U32), axis=0),
                    in_=HR[:, n % 4, :], in_offset=None, bounds_check=(T1 + TA) * P - 1, oob_is_err=False),
                    t, hr_t[n], clr["b1"][-1], engine="pool")
            scat1.append(tok)
            free[("HR", n % 4)] = tok
            if n + 4 < NT:
                row_load(n + 4)

        a1_done = [v for k, v in free.items() if isinstance(k, tuple) and k[0] in (
            "SM", "PTS", "CXT", "CX", "QT", "KBD", "HH", "HT", "YL", "KT")] + [free["VA"], t_done]
        w1_t = []
        for g in range(8):
            es = slice(4 * g, 4 * g + 4)
            for k in range(2):
                for o, nm in enumerate(("w1g", "w1u")):
                    w1_t.append(ld(f"w1_{g}", W1[:, es, k * 256 + o * P:k * 256 + o * P + P],
                                   a[nm][es, k * P:k * P + P, :].rearrange("e p n -> p e n"), a1_done))
            w1_t.append(ld(f"w1_{g}", W1[:, es, 512:768], a["w1d"][es].rearrange("e p n -> p e n")))
        for k in range(2):
            for o, nm in enumerate(("wag", "wau")):
                w1_t.append(ld("w1_a", WA[:, :, k * P + o * 64:k * P + o * 64 + 64],
                               a[nm][:, k * P:k * P + P, :].rearrange("l p n -> p l n")))
        w1_t.append(ld("w1_a", WD, a["wad"].rearrange("l p n -> p l n")))

        def add1(n, bank, t):
            return q.dve(lambda e: e.tensor_tensor(X[:, n, :], PS[:, bank, 0:256], X[:, n, :], ALU.add), t)

        q.wait("pe", t_ti, t_te)
        sg1 = WS1[:, 0:256].rearrange("p (c n) -> p c n", c=2)
        su1 = WS1[:, 256:512].rearrange("p (c n) -> p c n", c=2)
        shared(1, lambda k, i: sg1[:, k, :], lambda k, i: su1[:, k, :], lambda i: WS1[:, 512:768], t_small, add1)
        banks = [b for b in barrier_banks() if b]
        q.wait("pe", *banks)

        bx_t, xt_t, mt_t, ac_t, at_t, sp1 = {}, {}, {}, {}, {}, []
        NTL = T1 + TA
        reg_v = {}

        def width(i):
            return P if i < T1 else 64

        for i in range(4):
            bx_t[i] = bx_load(i, buf1, scat1[-4:])
        for i in range(NTL + 3):
            if i < NTL:
                xt_t[i], mt_t[i] = stage_a(i, bx_t, TE[:, i:i + 1], t_te)
                if i + 4 < NTL:
                    bx_t[i + 4] = bx_load(i + 4, buf1)
            if 0 <= i - 1 < NTL:
                j = i - 1
                s = j % 2
                w = width(j)

                def go(e, j=j, s=s, w=w):
                    r = e.value_load(TI[0:1, j:j + 1], min_val=0, max_val=(R1 if j < T1 else NA) - 1)
                    reg_v[j] = r
                    src = W1 if j < T1 else WA
                    for k in range(2):
                        m = e.matmul(PS[:, 2 + s, 0:2 * w], XT[:, j % 3, k, :],
                                     src[:, bass.ds(r, 1), k * 2 * w:(k + 1) * 2 * w].rearrange("p a n -> p (a n)"),
                                     start=(k == 0), stop=(k == 1))
                    return m
                t = q.pe(go, xt_t[j], w1_t if j == 0 else None, got(("GU", s)))
                free[("XT", j % 3)] = t
                t1 = q.act(lambda e, s=s, w=w: e.activation(SL[:, s, 0:w], PS[:, 2 + s, 0:w], ACT.Silu), t,
                           got(("SL", s)))
                t = q.dve(lambda e, s=s, w=w: e.tensor_tensor(
                    AC[:, s, 0:w], SL[:, s, 0:w], PS[:, 2 + s, w:2 * w], ALU.mult), t1, got(("AC", s)))
                free[("GU", s)] = free[("SL", s)] = t
                ac_t[j] = t
            if 0 <= i - 2 < NTL:
                j = i - 2
                s = j % 2
                w = width(j)
                t = q.pe(lambda e, s=s, w=w: e.transpose(PS[0:w, 6 + s, 0:P], AC[:, s, 0:w], ident), ac_t[j],
                         got(("T2", s)))
                free[("AC", s)] = t
                t = q.act(lambda e, s=s, w=w: e.copy(AT[0:w, s, :], PS[0:w, 6 + s, 0:P]), t, got(("AT", s)))
                free[("T2", s)] = t
                at_t[j] = t
            if 0 <= i - 3 < NTL:
                j = i - 3
                s = j % 2
                w = width(j)

                def go(e, j=j, s=s, w=w):
                    src = W1[:, bass.ds(reg_v[j], 1), 512:768] if j < T1 else WD[:, bass.ds(reg_v[j], 1), :]
                    return e.matmul(PS[:, 4 + s, 0:256], AT[0:w, s, :], src.rearrange("p a n -> p (a n)"),
                                    start=True, stop=True)
                t = q.pe(go, at_t[j], got(("Y", s)))
                free[("AT", s)] = t
                sp1.append(put_back(j, t, mt_t[j][1], mt_t[j][0], yb1, 2048 * K1 - 1))

        yv1 = yb1.rearrange("(t k) d -> t (k d)", k=K1)
        y1_t = {}
        last = [free[("AT", 0)], free[("AT", 1)]] + sp1[-3:]

        def y1_load(n):
            y1_t[n] = ld(f"yf{n % 4}", YF[:, n % 4, 0:K1 * D], yv1[n * P:n * P + P, :], last, got(("YF", n % 4)))

        for n in range(4):
            y1_load(n)
        for n in range(NT):
            yl = YF[:, n % 4, :]
            t = q.dve(lambda e, yl=yl: e.tensor_tensor(yl[:, 0:768], yl[:, 0:768], yl[:, 768:1536], ALU.add), y1_t[n])
            t = q.dve(lambda e, yl=yl: e.tensor_tensor(yl[:, 0:256], yl[:, 0:256], yl[:, 256:512], ALU.add), t)
            t = q.dve(lambda e, yl=yl: e.tensor_tensor(yl[:, 512:768], yl[:, 512:768], yl[:, 1536:1792], ALU.add))
            t = q.dve(lambda e, yl=yl: e.tensor_tensor(yl[:, 0:256], yl[:, 0:256], yl[:, 512:768], ALU.add), t)
            t = q.dve(lambda e, yl=yl, n=n: e.tensor_tensor(X[:, n, :], X[:, n, :], yl[:, 0:256], ALU.add), t)
            free[("YF", n % 4)] = t
            if n + 4 < NT:
                y1_load(n + 4)
            t_out = ld("out", out_d[:, n, :], X[:, n, :], t, engine="act")
        q.wait("act", t_out)

        sems = {name: ctx.enter_context(nc.semaphore("s_" + name)) for name in q.count}
        block = ctx.enter_context(nc.Block())

        @block.sync
        def _(e):
            q.run("sp", e, sems)

        @block.gpsimd
        def _(e):
            q.run("pool", e, sems)

        @block.scalar
        def _(e):
            q.run("act", e, sems)

        @block.vector
        def _(e):
            q.run("dve", e, sems)

        @block.tensor
        def _(e):
            q.run("pe", e, sems)


def kernel(**inputs):
    import concourse.bacc as _bacc
    from concourse.bass_utils import run_bass_kernel_spmd as _run

    g = {k: np.asarray(v) for k, v in inputs.items()}
    c = np.ascontiguousarray
    arrays = {
        "x": g["x"],
        "cst": constants()[0],
        "ctxT": c(g["ctx_1024"].reshape(NB * SK, D).T),
        "mask": c(g["mask_1x1xSxS2_ik0"].reshape(256, SK)),
        "wq0": c(g["L0_xattn_w_q"].T), "wk0": c(g["L0_xattn_w_k"].T),
        "wv0": c(g["L0_xattn_w_v"].T), "wo0": c(g["L0_xattn_w_o"].T),
        "wq1": g["L1_xattn_W_q"], "wk1": g["L1_xattn_W_k"],
        "wv1": g["L1_xattn_W_v"], "wo1": g["L1_xattn_W_o"],
        "bqk": np.concatenate([g["L1_xattn_b_q"].reshape(2, P).T, g["L1_xattn_b_k"].reshape(2, P).T], 1),
        "bv": g["L1_xattn_b_v"], "bo": g["L1_xattn_b_o"],
        "gate0": np.concatenate([g["L0_ffn_gate_w"], g["L0_ffn_shared_gate_w"]], 1),
        "sgu0": g["L0_ffn_shared_gate_up_w"], "sd0": g["L0_ffn_shared_down_w"],
        "egu": g["L0_ffn_expert_gate_up_w"], "ed": g["L0_ffn_expert_down_w"],
        "gate1": c(g["L1_ffn_gate_weight"].T), "gbias": g["L1_ffn_gate_bias"],
        "w1g": g["L1_ffn_w_gate"], "w1u": g["L1_ffn_w_up"], "w1d": g["L1_ffn_w_down"],
        "sg1": g["L1_ffn_shared_w_gate"], "su1": g["L1_ffn_shared_w_up"], "sd1": g["L1_ffn_shared_w_down"],
        "wag": g["L1_ffn_anchor_w_gate"], "wau": g["L1_ffn_anchor_w_up"], "wad": g["L1_ffn_anchor_w_down"],
    }
    nc = _bacc.Bacc("TRN2", target_bir_lowering=False, num_devices=1)
    feed, args = {}, {}
    for name, v in arrays.items():
        v = np.ascontiguousarray(v)
        feed["in_" + name] = v
        args[name] = nc.dram_tensor("in_" + name, v.shape, mybir.dt.from_np(v.dtype), kind="ExternalInput").ap()
    out = nc.dram_tensor("out_0", (NB, 256, D), F32, kind="ExternalOutput").ap()
    build(nc, args, out)
    r = _run(nc, [feed], core_ids=[0])
    return r.results[0]["out_0"]
```

```python
import numpy as np
import concourse.bass as bass
from concourse import mybir
from contextlib import ExitStack

F32 = mybir.dt.float32
I32 = mybir.dt.int32
U32 = mybir.dt.uint32
ALU = mybir.AluOpType
ACT = mybir.ActivationFunctionType
AX = mybir.AxisListType

P = 128
D = 256
NT = 16
NB = 8
SK = 120
H = 16
ROW = 280
E0 = 64
CAP = 128
R1 = 32
NA = 16
E1 = R1 + NA
T1 = 128
TA = 32
K0 = 8
K1 = 7
BIG = 65536.0
OFF = 30000.0
NEG = -3.0e38
EPS = 1e-5
MAGIC = float(0x5F3759DF)


def constants():
    p = np.arange(P, dtype=np.float32)[:, None]
    j = np.arange(P, dtype=np.float32)[None, :]
    t = np.arange(NT, dtype=np.float32)[None, :, None] * P + p[:, :, None]
    k = np.arange(8, dtype=np.float32)[None, None, :]
    parts = [
        ("ident", (p == j)),
        ("upper", (p < j)),
        ("ones", np.ones((P, P))),
        ("d0", (t * K0 + k - OFF).reshape(P, -1)),
        ("d1", (t * K1 + k - OFF).reshape(P, -1)),
        ("nb0", np.broadcast_to(BIG - CAP * j[:, :E0], (P, E0))),
        ("iota", np.broadcast_to(j[:, :48], (P, 48))),
        ("step", np.broadcast_to(P * j[:, :16], (P, 16))),
        ("part", p),
        ("pad", np.full((P, 48), NEG)),
    ]
    at, place, cols = 0, {}, []
    for name, a in parts:
        place[name] = (at, a.shape[1])
        at += a.shape[1]
        cols.append(np.asarray(a, np.float32))
    return np.ascontiguousarray(np.concatenate(cols, 1)), place


class Queues:

    def __init__(self):
        self.lists = {e: [] for e in ("pe", "act", "dve", "pool", "sp")}
        self.count = {}

    def put(self, engine, sem, inc, fn, waits):
        q = self.lists[engine]
        for w in waits:
            for tok in (w if isinstance(w, list) else [w]):
                if tok is not None:
                    q.append(("wait", tok))
        self.count[sem] = self.count.get(sem, 0) + inc
        q.append(("do", fn, sem, inc))
        return (sem, self.count[sem])

    def pe(self, fn, *waits):
        return self.put("pe", "pe", 1, fn, waits)

    def act(self, fn, *waits):
        return self.put("act", "act", 1, fn, waits)

    def dve(self, fn, *waits):
        return self.put("dve", "dve", 1, fn, waits)

    def pool(self, fn, *waits):
        return self.put("pool", "pool", 1, fn, waits)

    def dma(self, sem, fn, *waits, engine="sp"):
        return self.put(engine, sem, 16, fn, waits)

    def wait(self, engine, *waits):
        for tok in waits:
            self.lists[engine].append(("wait", tok))

    def run(self, engine, eng, sems):
        seen = {}
        for item in self.lists[engine]:
            if item[0] == "wait":
                sem, n = item[1]
                if seen.get(sem, 0) < n:
                    eng.wait_ge(sems[sem], n)
                    seen[sem] = n
            elif item[0] == "set":
                eng.preload_act_table_set(item[1])
            else:
                _, fn, sem, inc = item
                fn(eng).then_inc(sems[sem], inc)


def build(nc, a, out):
    place = constants()[1]
    ncst = sum(n for _, n in place.values())
    buf0 = nc.dram_tensor("buf0", [E0 * P, ROW], F32)
    buf1 = nc.dram_tensor("buf1", [(T1 + TA) * P, ROW], F32)
    yb0 = nc.dram_tensor("yb0", [2048 * K0, D], F32)
    yb1 = nc.dram_tensor("yb1", [2048 * K1, D], F32)
    x_d = a["x"].rearrange("b s d -> (b s) d").rearrange("(n p) d -> p n d", p=P)
    out_d = out.rearrange("b s d -> (b s) d").rearrange("(n p) d -> p n d", p=P)
    q = Queues()

    with ExitStack() as ctx:
        def sb(name, shape, dt=F32):
            return ctx.enter_context(nc.sbuf_tensor(name, shape, dt))

        PS = ctx.enter_context(nc.psum_tensor("PS", [P, 8, 512], F32))
        C = sb("C", [P, ncst])

        def cst(name):
            o, n = place[name]
            return C[:, o:o + n]

        ident, upper, ones = cst("ident"), cst("upper"), cst("ones")
        X = sb("X", [P, NT, D])
        H2T = sb("H2T", [P, 2, NT * P])
        HR = sb("HR", [P, 4, ROW])
        WS1 = sb("WS1", [P, 768])
        BX = sb("BX", [P, 4, ROW])
        XT = sb("XT", [P, 3, 2, P])
        SL = sb("SL", [P, 2, P])
        AC = sb("AC", [P, 2, P])
        AT = sb("AT", [P, 2, P])
        YT = sb("YT", [P, 3, D])
        DF = sb("DF", [P, T1 + TA])
        WC = sb("WC", [P, T1 + TA])
        DI = sb("DI", [P, T1 + TA], I32)
        TE = sb("TE", [P, T1 + TA])
        TI = sb("TI", [P, T1 + TA], I32)
        JK = sb("JK", [P, 2, 2, 8])
        SS_ = sb("SS_", [P, 2, 512])
        AS_ = sb("AS_", [P, 4, 512])
        BO = sb("BO", [1, D])
        BQK = sb("BQK", [P, 4])
        GB = sb("GB", [P, R1])
        WR1 = sb("WR1", [P, 2, R1])
        SIG = sb("SIG", [P, NT])
        ST = sb("ST", [P, 4, 2, 6])
        MV = sb("MV", [P, 4, 2, 2])
        NW = sb("NW", [P, 4, 2, 2])
        MX = sb("MX", [P, 3, 8])
        RC = sb("RC", [P, 2, H])
        T2_ = sb("T2_", [P, 4, 64])
        KEY = sb("KEY", [P, 4, 64])
        SUM = sb("SUM", [P, 2, 64])
        M8 = sb("M8", [P, 4, 8])
        G8 = sb("G8", [P, 4, 4, 8])
        GS = sb("GS", [P, 4, 16])
        R8 = sb("R8", [P, 4, 2, 8])
        IX = sb("IX", [P, 4, 8], U32)
        AX1 = sb("AX1", [P, 4, 1], U32)
        EW8 = sb("EW8", [P, 4, 8])
        SC1 = sb("SC1", [P, 4, 8])
        RI = sb("RI", [P, 4, 8], I32)
        K8 = sb("K8", [P, 4, 8])
        NBT = sb("NBT", [P, E1])
        TOT = sb("TOT", [P, E1])
        TIL = sb("TIL", [P, E1])
        CUM = sb("CUM", [P, E1])
        CNT = sb("CNT", [P, 2])
        CMP = sb("CMP", [P, E1])
        R = sb("R", [P, 32768])

        at = [0]

        def reg(n):
            at[0] += n
            return R[:, at[0] - n:at[0]]

        KBD = reg(4 * 960).rearrange("p (s c n) -> p s c n", s=2, c=2)
        AW = reg(8 * 512).rearrange("p (w c n) -> p w c n", w=8, c=2)
        KT = reg(1920).rearrange("p (c n) -> p c n", c=2)
        CT = reg(1920).rearrange("p (c n) -> p c n", c=2)
        VA = reg(NB * H * 17).rearrange("p (b h d) -> p b h d", b=NB, h=H)
        YL = reg(2 * 2048).rearrange("p (s n) -> p s n", s=2)
        SALL = reg(NT * E1).rearrange("p (n e) -> p n e", n=NT)
        PALL = reg(NT * E1).rearrange("p (n e) -> p n e", n=NT)
        lo = at[0]
        HH = reg(2 * 512).rearrange("p (s n d) -> p s n d", s=2, n=2)
        HT = reg(2 * 512).rearrange("p (s c t) -> p s c t", s=2, c=2)
        QT = reg(2 * 512).rearrange("p (s c t) -> p s c t", s=2, c=2)
        SM = reg(3 * 960).rearrange("p (s h k) -> p s h k", s=3, h=8)
        PT = reg(4 * 512).rearrange("p (s h t) -> p s h t", s=4, h=4)
        CX = reg(2 * 256).rearrange("p (s d) -> p s d", s=2)
        CXT = reg(2 * 256).rearrange("p (s c t) -> p s c t", s=2, c=2)
        CAPM = reg(2 * SK).rearrange("p (n k) -> p n k", n=2)
        MSK = reg(2 * SK).rearrange("p (n k) -> p n k", n=2).bitcast(I32)
        MF = reg(2 * SK).rearrange("p (n k) -> p n k", n=2)
        BV = reg(D)
        LG = reg(256).rearrange("p (s e) -> p s e", s=4)
        RP = reg(256).rearrange("p (s e) -> p s e", s=4)
        SEL = reg(256).rearrange("p (s e) -> p s e", s=4)
        EQ = reg(12 * R1).rearrange("p (s n) -> p s n", s=2)
        T1_ = reg(256).rearrange("p (s e) -> p s e", s=4)
        WR0 = reg(130).rearrange("p (c n) -> p c n", c=2)
        assert at[0] <= 32768
        Z = AS_[:, 0:2, :].rearrange("p a n -> p (a n)")[:, 0:560]
        EWR = R[:, lo:lo + 6 * 768].rearrange("p (s n) -> p s n", s=6)
        SG0 = R[:, lo + 4608:lo + 4608 + 2048].rearrange("p (c n) -> p c n", c=2)
        SD0 = R[:, lo + 6656:lo + 6656 + 1024].rearrange("p (c n) -> p c n", c=4)
        W1 = R[:, 0:24576].rearrange("p (e n) -> p e n", e=R1)
        WA = R[:, 24576:28672].rearrange("p (l n) -> p l n", l=NA)
        WD = R[0:64, 28672:32768].rearrange("p (l n) -> p l n", l=NA)
        YF = R[:, 0:4 * 2048].rearrange("p (s n) -> p s n", s=4)

        def ld(sem, dst, src, *waits, engine="sp"):
            return q.dma(sem, lambda e: e.dma_start(dst, src), *waits, engine=engine)

        def chunks(name):
            return a[name].rearrange("(c p) n -> p c n", p=P)

        q.lists["act"].append(("set", "natural_log_exp_and_others"))
        t_c = ld("l_c", C[:, :], a["cst"])
        t_x = [ld(f"l_x{i}", X[:, 4 * i:4 * i + 4, :], x_d[:, 4 * i:4 * i + 4, :]) for i in range(4)]
        names = ["wq0", "wk0", "wv0", "wo0", "wq1", "wk1", "wv1", "wo1"]
        t_ct = ld("l_ct", CT, chunks("ctxT"))
        t_w = {}
        for i in (1, 0, 2, 3):
            t_w[names[i]] = ld("l_" + names[i], AW[:, i, :, :], chunks(names[i]))
        t_mask = ld("l_mask", MSK, a["mask"].rearrange("(n p) k -> p n k", p=P))
        t_wr0 = ld("l_wr0", WR0, chunks("gate0"))
        for i in range(4, 8):
            t_w[names[i]] = ld("l_" + names[i], AW[:, i, :, :], chunks(names[i]))
        t_small = [
            ld("l_s0", BV, a["bv"].partition_broadcast(P)),
            ld("l_s1", BO[:, :], a["bo"].unsqueeze(0)),
            ld("l_s2", BQK[:, :], a["bqk"]),
            ld("l_s4", GB[:, :], a["gbias"].partition_broadcast(P)),
            ld("l_s5", WR1[:, :, :], chunks("gate1")),
            ld("l_s6", WS1[:, 0:256].rearrange("p (c n) -> p c n", c=2), chunks("sg1")),
            ld("l_s7", WS1[:, 256:512].rearrange("p (c n) -> p c n", c=2), chunks("su1")),
            ld("l_s8", WS1[:, 512:768], a["sd1"]),
        ]

        t_z = q.pool(lambda e: e.memset(Z, 0.0))
        t_kz = q.pool(lambda e: e.memset(KBD, 0.0))
        t_va1 = q.pool(lambda e: e.memset(VA[:, :, :, 16:17], 1.0))
        t_sum0 = q.pool(lambda e: e.memset(SUM[:, :, :], 0.0))
        t_r8 = q.pool(lambda e: e.memset(R8[:, :, :, :], NEG))
        t_gs = q.pool(lambda e: e.memset(GS[:, :, :], NEG))

        def clear(sem, tensor, r0, n):
            flat = tensor.rearrange("a b -> (a b)").rearrange("(p r n) -> p r n", p=P, n=560)
            dst = flat[:, r0:r0 + n, :]
            src = Z.unsqueeze(1).broadcast_to([P, n, 560])
            return q.dma(sem, lambda e: e.dma_start(dst, src), t_z, engine="act")

        clr = {"b0": [], "y0": [], "b1": []}
        y0f = yb0.rearrange("a b -> (a b)").rearrange("(p r n) -> p r n", p=P, n=512)

        def clear_y(r0, n):
            dst = y0f[:, r0:r0 + n, :]
            src = Z[:, 0:512].unsqueeze(1).broadcast_to([P, n, 512])
            return q.dma("z_y0", lambda e: e.dma_start(dst, src), t_z, engine="act")

        later = [("b0", r, 4) for r in range(0, 32, 4)] + [("y0", r, 4) for r in range(0, 64, 4)] + [("b1", r, 4) for r in range(0, 80, 4)]

        def clear_some(n):
            for _ in range(n):
                if later:
                    kind, r, m = later.pop(0)
                    clr[kind].append(clear_y(r, m) if kind == "y0" else
                                     clear("z_" + kind, buf0 if kind == "b0" else buf1, r, m))

        t = q.dve(lambda e: e.tensor_scalar(MF, MSK, 0.0, None, ALU.is_equal), t_mask)
        t2 = q.dve(lambda e: e.tensor_scalar(CAPM, MF, NEG, -NEG, ALU.mult, ALU.add), t)
        t_cap = q.dve(lambda e: e.scalar_tensor_tensor(
            out=CAPM, in0=MF, scalar=-4.0e9, in1=CAPM, op0=ALU.mult, op1=ALU.add), t2)

        free = {}

        def got(key):
            return free.get(key)

        held = {5: False, 7: False}

        def misc():
            while True:
                for bank in (5, 7):
                    if not held[bank]:
                        held[bank] = True
                        return bank, PS[:, bank, 0:256]
                yield

        def give(bank, t):
            free[("M", bank)] = t
            held[bank] = False

        def got_bank(bank):
            return free.get(("M", bank))

        def layernorm(n0, s, dst, waits, out_t):
            st = []
            for i in range(2):
                st.append(q.dve(lambda e, i=i: e.bn_stats(ST[:, s, i, :], X[:, n0 + i, :]), waits[i]))
                yield
            for i in range(2):
                t = q.dve(lambda e, i=i: e.bn_aggr(MV[:, s, i, :], ST[:, s, i, :]), st[i])
            yield
            ve, rs = NW[:, s, 0, :], NW[:, s, 1, :]
            t = q.dve(lambda e: e.tensor_scalar(ve, MV[:, s, :, 1], EPS, None, ALU.add), t)
            yield
            t = q.act(lambda e: e.activation(ve, ve, ACT.Ln), t)
            t = q.act(lambda e: e.activation(rs, ve, ACT.Exp, scale=-0.5), t)
            yield
            yield
            for i in range(2):
                out_t.append(q.dve(lambda e, i=i: e.tensor_scalar(
                    dst(i), X[:, n0 + i, :], MV[:, s, i, 0:1], rs[:, i:i + 1], ALU.subtract, ALU.mult),
                    t, waits[2 + i]))
                yield

        def mm(e, out_, pairs):
            for i, (l, r) in enumerate(pairs):
                m = e.matmul(out_, l, r, start=(i == 0), stop=(i == len(pairs) - 1))
            return m

        def tr2(e, out_, src):
            e.transpose(out_[:, 0:128], src[:, 0:128], ident)
            return e.transpose(out_[:, 128:256], src[:, 128:256], ident)

        def attention(l, x_ready, before, route, rows):
            wq, wk, wv, wo = (AW[:, 4 * l + i, :, :] for i in range(4))
            tw = [t_w[names[4 * l + i]] for i in range(4)]
            kt_t = []
            for c in range(2):
                for half in range(2):
                    bank = 2 * c + half
                    t = q.pe(lambda e, c=c, half=half, bank=bank: mm(
                        e, PS[:, bank, 0:480],
                        [(wk[:, k, c * P:c * P + P], CT[:, k, half * 480:half * 480 + 480]) for k in range(2)]),
                        tw[1], t_ct, got(("KT", 0)), got(("KT", 1)))
                    dst = KT[:, c, half * 480:half * 480 + 480]
                    if l == 0:
                        t = q.act(lambda e, bank=bank, dst=dst: e.copy(dst, PS[:, bank, 0:480]), t)
                    else:
                        t = q.act(lambda e, bank=bank, dst=dst, c=c: e.activation(
                            dst, PS[:, bank, 0:480], ACT.Identity, bias=BQK[:, 2 + c:3 + c]), t, t_small)
                    kt_t.append(t)
            free[("S", 0)], free[("S", 1)], free[("S", 2)], free[("PT", 0)] = kt_t
            qt_t, v_t, kb_t, h_t, ht_t = {}, {}, {}, {}, {}
            ex_t, pt_t, x_t, c_t, s_t, mx_t = {}, {}, {}, {}, {}, {}

            def prepare(b):
                s = b % 2
                for n in (2 * b, 2 * b + 1):
                    yield from before(n)
                h_t[b] = []
                yield from layernorm(2 * b, s, lambda i: HH[:, s, i, :],
                                     [x_ready(2 * b), x_ready(2 * b + 1), got(("HH", s, 0)), got(("HH", s, 1))],
                                     h_t[b])
                while b > 1 and (4 * b - 5, 1) not in s_t:
                    yield
                for h in range(8):
                    kb_t[b] = q.dma(f"kb{s}", lambda e, h=h: e.dma_start(
                        KBD[16 * h:16 * h + 16, s, :, h * SK:h * SK + SK],
                        KT[16 * h:16 * h + 16, :, b * SK:b * SK + SK]), kt_t, t_kz, got(("KBD", s)))
                free[("KT", s)] = kb_t[b]
                hts = []
                for i in range(2):
                    bank, m = yield from misc()
                    t = q.pe(lambda e, i=i, m=m: tr2(e, m, HH[:, s, i, :]), h_t[b][i], t_c, got_bank(bank))
                    free[("HH", s, i)] = t
                    yield
                    t = q.act(lambda e, i=i, m=m: e.copy(
                        HT[:, s, :, i * P:i * P + P], m.rearrange("p (c t) -> p c t", c=2)), t, got(("HT", s)))
                    give(bank, t)
                    hts.append(t)
                ht_t[b] = hts
                yield
                yield
                qts = []
                for c in range(2):
                    bank, m = yield from misc()
                    t = q.pe(lambda e, c=c, m=m: mm(
                        e, m, [(wq[:, k, c * P:c * P + P], HT[:, s, k, :]) for k in range(2)]),
                        ht_t[b], tw[0], got_bank(bank))
                    free[("HT", s)] = t
                    yield
                    if l == 0:
                        t = q.act(lambda e, c=c, m=m: e.copy(QT[:, s, c, :], m), t, got(("QT", s)))
                    else:
                        t = q.act(lambda e, c=c, m=m: e.activation(
                            QT[:, s, c, :], m, ACT.Identity, bias=BQK[:, c:c + 1]), t, got(("QT", s)), t_small)
                    give(bank, t)
                    qts.append(t)
                bank, m = yield from misc()
                t = q.pe(lambda e: mm(
                    e, m[0:SK, :], [(CT[:, k, b * SK:b * SK + SK], wv[:, k, :]) for k in range(2)]),
                    tw[2], t_ct, got_bank(bank))
                yield
                dst = VA[0:SK, b, :, 0:16]
                src = m[0:SK, :].rearrange("p (h d) -> p h d", h=H)
                if l == 0:
                    t = q.dve(lambda e: e.tensor_copy(dst, src), t, t_va1)
                else:
                    t = q.dve(lambda e: e.tensor_tensor(
                        dst, src, BV[0:SK, :].rearrange("p (h d) -> p h d", h=H), ALU.add), t, t_small, got("VA"))
                give(bank, t)
                v_t[b] = t
                qt_t[b] = qts

            def scores(u, half):
                n, c = u // 2, u % 2
                b, s = n // 2, (n // 2) % 2
                while b not in qt_t:
                    step()
                w = (2 * u + half) % 3
                s_t[u, half] = q.pe(lambda e: e.matmul(
                    psum_scores(u, half),
                    QT[:, s, c, (n % 2) * P:(n % 2) * P + P],
                    KBD[:, s, c, half * 480:half * 480 + 480].rearrange("p (h k) -> p h k", h=4),
                    start=True, stop=True), qt_t[b], kb_t[b], got(("S", w)))
                free[("QT", s)] = free[("KBD", s)] = s_t[u, half]

            def psum_scores(u, half):
                return PS[:, (2 * u + half) % 3, :].rearrange("p (h k) -> p h k", k=P)[:, :, 0:SK]

            def cap(u, half):
                n, z = u // 2, u % 3
                s_t[u, half] = q.dve(lambda e: e.scalar_tensor_tensor(
                    out=SM[:, z, 4 * half:4 * half + 4, :], in0=psum_scores(u, half), scalar=-4.0e9,
                    in1=CAPM[:, n % 2, :].unsqueeze(1).broadcast_to([P, 4, SK]),
                    op0=ALU.max, op1=ALU.min), s_t[u, half], t_cap, got(("SM", z)))
                free[("S", (2 * u + half) % 3)] = s_t[u, half]

            def highest(u, half=None):
                z = u % 3
                if half is None:
                    src, dst, t = SM[:, z, :, :], MX[:, z, :], [s_t[u, 0], s_t[u, 1]]
                else:
                    src, dst, t = psum_scores(u, half), MX[:, z, 4 * half:4 * half + 4], s_t[u, half]
                mx_t[u] = q.dve(lambda e: e.tensor_reduce(dst, src, AX.X, ALU.max), t, got(("MX", z)))

            def scale_max(u):
                z = u % 3
                mx_t[u] = q.dve(lambda e: e.tensor_scalar(MX[:, z, :], MX[:, z, :], -0.25, None, ALU.mult), mx_t[u])

            def lower(u, half):
                z = u % 3
                hs = slice(4 * half, 4 * half + 4)
                mx_t[u] = q.dve(lambda e: e.tensor_tensor(
                    SM[:, z, hs, :], psum_scores(u, half),
                    MX[:, z, hs].unsqueeze(2).broadcast_to([P, 4, SK]), ALU.subtract), mx_t[u], got(("SM", z)))
                free[("S", (2 * u + half) % 3)] = mx_t[u]

            def exps(u, half):
                z = u % 3
                if l == 0:
                    for h in range(4 * half, 4 * half + 4):
                        t = q.act(lambda e, h=h: e.activation(SM[:, z, h, :], SM[:, z, h, :], ACT.Exp, scale=0.25,
                                                              bias=MX[:, z, h:h + 1]), mx_t[u])
                else:
                    hs = slice(4 * half, 4 * half + 4)
                    t = q.act(lambda e: e.activation(SM[:, z, hs, :], SM[:, z, hs, :], ACT.Exp, scale=0.25), mx_t[u])
                ex_t[u, half] = t
                free[("MX", z)] = t

            def turn(u, half):
                z = u % 3

                def go(e):
                    for i in range(4):
                        m = e.transpose(PS[0:SK, 3 + half, i * P:i * P + P], SM[:, z, 4 * half + i, :], ident)
                    return m
                pt_t[u, half] = q.pe(go, ex_t[u, half], got(("PT", half)))
                free[("SM", z)] = pt_t[u, half]

            def turned(u, half):
                r = 2 * (u % 2) + half
                src = PS[0:SK, 3 + half, :].rearrange("p (h t) -> p h t", h=4)
                if l == 1 and half == 1:
                    t = q.dve(lambda e: e.tensor_copy(PT[0:SK, r, :, :], src), pt_t[u, half], got(("PTS", r)))
                else:
                    t = q.act(lambda e: e.copy(PT[0:SK, r, :, :], src), pt_t[u, half], got(("PTS", r)))
                free[("PT", half)] = pt_t[u, half] = t

            def values(u):
                n, c = u // 2, u % 2
                b = n // 2

                def go(e):
                    for i in range(8):
                        h = 8 * c + i
                        m = e.matmul(PS[:, 6, h * 17:h * 17 + 17], PT[0:SK, 2 * (u % 2) + i // 4, i % 4, :],
                                     VA[0:SK, b, h, :], start=True, stop=True)
                    return m
                t = q.pe(go, pt_t[u, 0], pt_t[u, 1], v_t[b], got("O"))
                free[("PTS", 2 * (u % 2))] = free[("PTS", 2 * (u % 2) + 1)] = t
                free["VA"] = c_t[n] = t

            def divide(n):
                s = n % 2
                O = PS[:, 6, 0:272].rearrange("p (h d) -> p h d", h=H)
                t = q.dve(lambda e: e.reciprocal(RC[:, s, :], O[:, :, 16]), c_t[n])
                t = q.dve(lambda e: e.tensor_tensor(
                    CX[:, s, :].rearrange("p (h d) -> p h d", h=H), O[:, :, 0:16],
                    RC[:, s, :].unsqueeze(2).broadcast_to([P, H, 16]), ALU.mult), t, got(("CX", s)))
                free["O"] = c_t[n] = t
                active.append(finish(n))

            def finish(n):
                s = n % 2
                yield
                yield
                bank, m = yield from misc()
                t = q.pe(lambda e, m=m: tr2(e, m, CX[:, s, :]), c_t[n], got_bank(bank))
                free[("CX", s)] = t
                yield
                t = q.act(lambda e, m=m: e.copy(CXT[:, s, :, :], m.rearrange("p (c t) -> p c t", c=2)),
                          t, got(("CXT", s)))
                give(bank, t)
                yield
                yield
                bank, m = yield from misc()

                def go(e):
                    pairs = [(CXT[:, s, k, :], wo[:, k, :]) for k in range(2)]
                    if l == 1:
                        pairs.append((ones[0:1, :], BO[0:1, :]))
                    return mm(e, m, pairs)
                t = q.pe(go, t, tw[3], got_bank(bank), t_small if l else None)
                free[("CXT", s)] = t
                yield
                t = q.dve(lambda e: e.tensor_tensor(X[:, n, :], m, X[:, n, :], ALU.add), t)
                give(bank, t)
                x_t[n] = t
                if n % 2:
                    active.append(behind(n // 2))

            def behind(b):
                s = 2 + b % 2
                for i in range(2):
                    while b > 1 and (2 * b + i - 4) not in hr_left:
                        yield
                h2_t[b] = []
                yield from layernorm(2 * b, s, lambda i: HR[:, (2 * b + i) % 4, 0:D],
                                     [x_t[2 * b], x_t[2 * b + 1],
                                      got(("HR", 2 * b % 4)), got(("HR", (2 * b + 1) % 4))], h2_t[b])
                active.extend([per_tile(2 * b), per_tile(2 * b + 1)])

            def per_tile(n):
                bank, m = yield from misc()
                t = q.pe(lambda e: tr2(e, m, HR[:, n % 4, 0:D]), h2_t[n // 2][n % 2], got_bank(bank))
                yield
                t = q.act(lambda e: e.copy(
                    H2T[:, :, n * P:n * P + P], m.rearrange("p (c t) -> p c t", c=2)), t, got("H2T"))
                give(bank, t)
                h2T_t[n] = t
                yield
                yield
                yield from route(n)
                while n not in sum_t:
                    yield
                yield from rows(n)
                hr_left.add(n)

            active, hr_left = [], set()

            def step():
                for g in list(active):
                    try:
                        next(g)
                    except StopIteration:
                        active.remove(g)

            NU = 2 * NT
            LEAD = 9
            def main(u, slot):
                here, v, ahead = 0 <= u < NU, u - 1, 0 <= u + 1 < NU
                if slot == 0:
                    if ahead:
                        scores(u + 1, 0)
                    if here:
                        cap(u, 0) if l == 0 else highest(u, 0)
                elif slot == 1:
                    if 0 <= u - 2 < NU:
                        values(u - 2)
                    if here:
                        cap(u, 1) if l == 0 else lower(u, 0)
                elif slot == 2:
                    if 0 <= v < NU:
                        turn(v, 0)
                    if here:
                        highest(u) if l == 0 else highest(u, 1)
                elif slot == 3:
                    if 0 <= v < NU:
                        turn(v, 1)
                        turned(v, 0)
                    if ahead:
                        scores(u + 1, 1)
                    if here:
                        scale_max(u) if l == 0 else lower(u, 1)
                elif slot == 4:
                    if 0 <= v < NU:
                        turned(v, 1)
                    if here:
                        exps(u, 0)
                    if 0 <= u - 2 < NU and u % 2:
                        divide((u - 2) // 2)
                elif here:
                    exps(u, 1)

            for u in range(-LEAD, NU + 2):
                if u % 4 == (-LEAD) % 4 and (u + LEAD) // 4 < NB:
                    active.append(prepare((u + LEAD) // 4))
                for slot in range(6):
                    main(u, slot)
                    step()
                clear_some(1)
            while active:
                step()

        h2_t, h2T_t, sel_t, w_t = {}, {}, {}, {}

        def route0(n):
            s = n % 4
            hr = HR[:, n % 4, :]
            bank, m = yield from misc()
            t = q.pe(lambda e: mm(
                e, m[:, 0:65], [(H2T[:, k, n * P:n * P + P], WR0[:, k, :]) for k in range(2)]),
                h2T_t[n], t_wr0, got_bank(bank))
            td = q.act(lambda e: e.copy(hr[:, 264:272], cst("d0")[:, 8 * n:8 * n + 8]), got(("HR", n % 4)))
            yield
            tl = q.dve(lambda e: e.tensor_copy(LG[:, s, :], m[:, 0:64]), t)
            ta = q.dve(lambda e: e.tensor_copy(SIG[:, n:n + 1], m[:, 64:65]), t)
            give(bank, ta)
            yield
            tm = q.dve(lambda e: e.max(M8[:, s, :], LG[:, s, :]), tl)
            ta = q.act(lambda e: e.activation(SIG[:, n:n + 1], SIG[:, n:n + 1], ACT.Exp, scale=-1.0), ta)
            yield
            tr = q.dve(lambda e: e.match_replace(RP[:, s, :], M8[:, s, :], LG[:, s, :], NEG), tm)
            tn = q.dve(lambda e: e.tensor_scalar(SC1[:, s, 0:1], M8[:, s, 0:1], -1.0, None, ALU.mult), tm)
            ti = q.dve(lambda e: e.max_index(IX[:, s, :], M8[:, s, :], LG[:, s, :]), tm)
            te = q.act(lambda e: e.activation(
                EW8[:, s, :], M8[:, s, :], ACT.Exp, bias=SC1[:, s, 0:1], accum_out=SC1[:, s, 1:2]), tn)
            yield
            sel_t[n] = q.dve(lambda e: e.tensor_tensor(SEL[:, s, :], RP[:, s, :], LG[:, s, :], ALU.not_equal), tr)
            tc = q.dve(lambda e: e.tensor_copy(hr[:, 256:264], IX[:, s, :]), ti, got(("HR", n % 4)))
            t1 = q.dve(lambda e: e.tensor_scalar(SIG[:, n:n + 1], SIG[:, n:n + 1], 1.0, None, ALU.add), ta)
            yield
            t = q.dve(lambda e: e.reciprocal(SC1[:, s, 2:3], SC1[:, s, 1:2]), te)
            free[("SIG", n)] = q.dve(lambda e: e.reciprocal(SIG[:, n:n + 1], SIG[:, n:n + 1]), t1)
            yield
            t = q.dve(lambda e: e.tensor_scalar(hr[:, 272:280], EW8[:, s, :], SC1[:, s, 2:3], None, ALU.mult), t)
            w_t[n] = [tc, td, t, h2_t[n // 2][n % 2], h2T_t[n]]

        sum_t = {0: t_sum0}

        def position(n, width, sel):
            bank, m = yield from misc()
            PO = m[:, 0:width]
            t = q.pe(lambda e: mm(e, PO, [(upper, sel), (ones, SUM[:, n % 2, 0:width])]),
                     sel_t[n], sum_t[n], got_bank(bank))
            yield
            return t, bank, PO

        def rows0(n):
            s, w = n % 4, n % 2
            t, bank, PO = yield from position(n, 64, SEL[:, s, :])
            t1 = q.dve(lambda e: e.scalar_tensor_tensor(
                out=T1_[:, s, :], in0=PO, scalar=float(CAP), in1=SEL[:, s, :], op0=ALU.is_lt, op1=ALU.mult), t)
            t2 = q.dve(lambda e: e.tensor_tensor(T2_[:, s, :], cst("nb0"), PO, ALU.subtract), t)
            give(bank, t2)
            sum_t[n + 1] = q.dve(lambda e: e.tensor_tensor(
                SUM[:, 1 - w, :], SUM[:, w, :], SEL[:, s, :], ALU.add), sel_t[n], sum_t[n], t)
            yield
            t = q.dve(lambda e: e.tensor_tensor(KEY[:, s, :], T1_[:, s, :], T2_[:, s, :], ALU.mult), t1, t2)
            yield
            t = q.dve(lambda e: e.max(K8[:, s, :], KEY[:, s, :]), t)
            yield
            t = q.dve(lambda e: e.tensor_scalar(
                RI[:, n % 4, :], K8[:, s, :], -1.0, BIG, ALU.mult, ALU.add), t, got(("HR", n % 4)))
            for k in range(K0):
                free[("HR", n % 4)] = q.dma(f"sc{n % 4}", lambda e, k=k: e.indirect_dma_start(
                    out=buf0[:, :], out_offset=bass.IndirectOffsetOnAxis(
                        ap=RI[:, n % 4, k:k + 1].bitcast(U32), axis=0),
                    in_=HR[:, n % 4, :], in_offset=None, bounds_check=E0 * P - 1, oob_is_err=False),
                    t, w_t[n], clr["b0"][-1], engine="pool")

        def matches(i, scalar, *waits):
            s = i % 2
            ids, dd, ww = (BX[:, i % 4, o:o + 8] for o in (256, 264, 272))
            t1 = q.dve(lambda e: e.scalar_tensor_tensor(
                out=JK[:, s, 0, :], in0=ids, scalar=scalar, in1=dd, op0=ALU.is_equal, op1=ALU.mult,
                accum_out=DF[:, i:i + 1]), *waits)
            t2 = q.dve(lambda e: e.scalar_tensor_tensor(
                out=JK[:, s, 1, :], in0=ids, scalar=scalar, in1=ww, op0=ALU.is_equal, op1=ALU.mult,
                accum_out=WC[:, i:i + 1]))
            t3 = q.dve(lambda e: e.tensor_scalar(DI[:, i:i + 1], DF[:, i:i + 1], OFF, None, ALU.add), t1)
            free[("BXd", i % 4)] = t2
            return t2, t3

        def put_back(i, t, idx_t, w_tok, yb, bound):
            s = i % 3
            t = q.act(lambda e: e.activation(YT[:, s, :], PS[:, 4 + i % 2, 0:256], ACT.Copy, scale=WC[:, i:i + 1]),
                      t, w_tok, got(("YT", s)))
            free[("Y", i % 2)] = t
            free[("YT", s)] = q.dma(f"yt{s}", lambda e: e.indirect_dma_start(
                out=yb[:, :], out_offset=bass.IndirectOffsetOnAxis(ap=DI[:, i:i + 1].bitcast(U32), axis=0),
                in_=YT[:, s, :], in_offset=None, bounds_check=bound, oob_is_err=False),
                t, idx_t, engine="pool")
            return free[("YT", s)]

        def shared(nchunk, gate, up, down, w_tok, add):
            last = None
            for g in range(4):
                act_t = []
                for i in range(nchunk):
                    w = i % 2
                    rhs = [H2T[:, k, g * 512:g * 512 + 512] for k in range(2)]
                    tg = q.pe(lambda e, i=i, w=w, rhs=rhs: mm(
                        e, PS[:, 2 * w, :], [(gate(k, i), rhs[k]) for k in range(2)]),
                        [h2T_t[4 * g + j] for j in range(4)], w_tok, got(("shg", w)))
                    tu = q.pe(lambda e, i=i, w=w, rhs=rhs: mm(
                        e, PS[:, 2 * w + 1, :], [(up(k, i), rhs[k]) for k in range(2)]))
                    t = q.act(lambda e, w=w: e.activation(SS_[:, w, :], PS[:, 2 * w, :], ACT.Silu), tg,
                              got(("shs", w)))
                    t = q.dve(lambda e, i=i, w=w: e.tensor_tensor(
                        AS_[:, i, :], SS_[:, w, :], PS[:, 2 * w + 1, :], ALU.mult), t, tu, got(("sha", i)))
                    free[("shg", w)] = free[("shs", w)] = t
                    act_t.append(t)
                last = tu
                for j in range(4):
                    n = 4 * g + j
                    bank = 4 + j % 2
                    t = q.pe(lambda e, j=j, bank=bank: mm(
                        e, PS[:, bank, 0:256],
                        [(AS_[:, i, j * P:j * P + P], down(i)) for i in range(nchunk)]), act_t, got(("shy", bank)))
                    for i in range(nchunk):
                        free[("sha", i)] = t
                    free[("shy", bank)] = add(n, bank, t)
            free["H2T"] = last
            return free[("shy", bank)]

        def barrier_banks():
            return [v for k, v in free.items() if isinstance(k, tuple) and k[0] in (
                "S", "PT", "M", "shg", "shy", "T", "GU", "Y", "T2")] + [free.get("O")]

        def nothing(n):
            return iter(())

        attention(0, lambda n: t_x[n // 4], nothing, route0, rows0)
        scat0 = [free[("HR", i)] for i in range(4)]
        clear_some(100)
        a_done = [free[("SM", i)] for i in range(3)] + [free[("PTS", i)] for i in range(4)] + \
            [free[("CXT", i)] for i in range(2)] + [free[("QT", i)] for i in range(2)] + \
            [free[("CX", i)] for i in range(2)]
        banks = barrier_banks()
        t_s0 = [ld("l_sg0", SG0, chunks("sgu0"), a_done), ld("l_sd0", SD0, chunks("sd0"))]

        def e0_load(i):
            s = i % 6
            t1 = ld(f"ew{s}", EWR[:, s, 0:512].rearrange("p (c n) -> p c n", c=2),
                    a["egu"][i].rearrange("(c p) n -> p c n", p=P), got(("EW", s)))
            return [t1, ld(f"ew{s}", EWR[:, s, 512:768], a["ed"][i])]

        ew_t = {i: e0_load(i) for i in range(6)}

        def add0(n, bank, t):
            return q.dve(lambda e: e.scalar_tensor_tensor(
                out=X[:, n, :], in0=PS[:, bank, 0:256], scalar=SIG[:, n:n + 1], in1=X[:, n, :],
                op0=ALU.mult, op1=ALU.add), t, got(("SIG", n)))

        q.wait("pe", *[b for b in banks if b])
        q.wait("dve", clr["b1"][-1], clr["y0"][-1], clr["b0"][-1])
        sh_t = shared(4, lambda k, i: SG0[:, k, i * P:i * P + P], lambda k, i: SG0[:, k, 512 + i * P:512 + i * P + P],
               lambda i: SD0[:, i, :], t_s0, add0)
        banks = [b for b in barrier_banks() if b]
        q.wait("pe", *banks)

        def bx_load(i, buf, *waits):
            return ld(f"bx{i % 4}", BX[:, i % 4, :], buf[i * P:i * P + P, :], *waits,
                      got(("BXp", i % 4)), got(("BXd", i % 4)))

        def stage_a(i, bx_t, scalar, *waits):
            s = i % 2
            t = q.pe(lambda e: tr2(e, PS[:, s, 0:256], BX[:, i % 4, 0:D]), bx_t[i], got(("T", s)))
            free[("BXp", i % 4)] = t
            t = q.dve(lambda e: e.tensor_copy(XT[:, i % 3, :, :], PS[:, s, 0:256].rearrange("p (c t) -> p c t", c=2)),
                      t, got(("XT", i % 3)))
            free[("T", s)] = t
            return t, matches(i, scalar, bx_t[i], *waits)

        bx_t, xt_t, mt_t, ac_t, sp0 = {}, {}, {}, {}, []
        for i in range(4):
            bx_t[i] = bx_load(i, buf0, scat0)
        for i in range(E0 + 2):
            if i < E0:
                xt_t[i], mt_t[i] = stage_a(i, bx_t, float(i))
                if i + 4 < E0:
                    bx_t[i + 4] = bx_load(i + 4, buf0)
            if 0 <= i - 1 < E0:
                j = i - 1
                s = j % 2

                def go(e, j=j, s=s):
                    for o in range(2):
                        m = mm(e, PS[:, 2 + s, o * P:o * P + P],
                               [(EWR[:, j % 6, k * 256 + o * P:k * 256 + o * P + P], XT[:, j % 3, k, :])
                                for k in range(2)])
                    return m
                t = q.pe(go, xt_t[j], ew_t[j], got(("GU", s)))
                free[("XT", j % 3)] = t
                t1 = q.act(lambda e, s=s: e.activation(SL[:, s, :], PS[:, 2 + s, 0:P], ACT.Silu), t, got(("SL", s)))
                t = q.dve(lambda e, s=s: e.tensor_tensor(AC[:, s, :], SL[:, s, :], PS[:, 2 + s, P:2 * P], ALU.mult),
                          t1, got(("AC", s)))
                free[("GU", s)] = free[("SL", s)] = t
                ac_t[j] = t
            if 0 <= i - 2 < E0:
                j = i - 2
                s = j % 2
                t = q.pe(lambda e, j=j, s=s: mm(e, PS[:, 4 + s, 0:256], [(AC[:, s, :], EWR[:, j % 6, 512:768])]),
                         ac_t[j], got(("Y", s)))
                free[("AC", s)] = t
                free[("EW", j % 6)] = t
                sp0.append(put_back(j, t, mt_t[j][1], mt_t[j][0], yb0, 2048 * K0 - 1)
                           if j else put_back(j, t, [mt_t[j][1], clr["y0"][-1]], mt_t[j][0], yb0, 2048 * K0 - 1))
                if j + 6 < E0:
                    ew_t[j + 6] = e0_load(j + 6)
        scat_y0 = sp0[-3:]

        banks = [b for b in barrier_banks() if b]
        q.wait("pe", *banks)
        e0_done = [free[("EW", i)] for i in range(6)]
        for e_ in ("dve", "act"):
            q.wait(e_, *e0_done)
        yv = yb0.rearrange("(t k) d -> t (k d)", k=K0)
        y_t, xc_t = {}, {}

        def y_add(n):
            yl = YL[:, n % 2, :]
            t = ld(f"yl{n % 2}", yl, yv[n * P:n * P + P, :], scat_y0, got(("YL", n % 2)))
            yield
            yield
            yield
            t = q.pool(lambda e: e.tensor_tensor(yl[:, 0:1024], yl[:, 0:1024], yl[:, 1024:2048], ALU.add), t)
            t = q.pool(lambda e: e.tensor_tensor(yl[:, 0:512], yl[:, 0:512], yl[:, 512:1024], ALU.add), t)
            t = q.pool(lambda e: e.tensor_tensor(yl[:, 0:256], yl[:, 0:256], yl[:, 256:512], ALU.add), t)
            t = q.pool(lambda e: e.tensor_tensor(X[:, n, :], X[:, n, :], yl[:, 0:256], ALU.add), t, x0_done)
            free[("YL", n % 2)] = t
            xc_t[n] = t

        x0_done = sh_t
        t_sum1 = q.dve(lambda e: e.memset(SUM[:, :, :], 0.0))
        sum_t.clear()
        sum_t[0] = t_sum1
        free.pop(("SUM", 0), None)
        free.pop(("SUM", 1), None)

        pos_t = {}

        def route1(n):
            s, z = n % 4, n % 2
            hr = HR[:, n % 4, :]
            bank, m = yield from misc()
            t = q.pe(lambda e: mm(
                e, m[:, 0:R1], [(H2T[:, k, n * P:n * P + P], WR1[:, k, :]) for k in range(2)]),
                h2T_t[n], t_small, got_bank(bank))
            td = q.act(lambda e: e.copy(hr[:, 264:272], cst("d1")[:, 8 * n:8 * n + 8]), got(("HR", n % 4)))
            sco, scb, mk = T1_[:, s, 0:R1], T2_[:, s, 0:R1], KEY[:, s, 0:40]
            idf, gs = hr[:, 256:264], GS[:, s, 0:10]
            yield
            t = q.act(lambda e: e.activation(sco, m[:, 0:R1], ACT.Exp, scale=-1.0), t)
            give(bank, t)
            tk = q.dve(lambda e: e.tensor_copy(mk[:, R1:40], cst("pad")[:, 0:8]))
            yield
            t = q.dve(lambda e: e.tensor_scalar(sco, sco, 1.0, None, ALU.add), t)
            yield
            t_sco = q.dve(lambda e: e.reciprocal(sco, sco), t)
            yield
            t_scb = q.dve(lambda e: e.tensor_tensor(scb, sco, GB[:, :], ALU.add), t_sco)
            yield
            for g in range(4):
                tg = q.dve(lambda e, g=g: e.max(G8[:, s, g, :], scb[:, 8 * g:8 * g + 8]), t_scb)
            yield
            t = q.dve(lambda e: e.tensor_tensor(GS[:, s, 0:4], G8[:, s, :, 0], G8[:, s, :, 1], ALU.add), tg, t_gs)
            yield
            tm = q.dve(lambda e: e.max(M8[:, s, :], gs), t)
            yield
            t = q.dve(lambda e: e.tensor_copy(R8[:, s, 0, 0:2], M8[:, s, 0:2]), tm, t_r8)
            yield
            t = q.dve(lambda e: e.match_replace(RP[:, s, 0:10], R8[:, s, 0, :], gs, -1.0e38), t)
            yield
            t = q.dve(lambda e: e.tensor_tensor(CNTG[:, s, :], RP[:, s, 0:4], GS[:, s, 0:4], ALU.is_equal), t)
            yield
            t = q.dve(lambda e: e.scalar_tensor_tensor(
                out=mk[:, 0:R1].rearrange("p (g k) -> p g k", g=4),
                in0=CNTG[:, s, :].unsqueeze(2).broadcast_to([P, 4, 8]), scalar=-1.0e30,
                in1=scb.rearrange("p (g k) -> p g k", g=4), op0=ALU.mult, op1=ALU.add), t)
            yield
            tm = q.dve(lambda e: e.max(M8[:, s, :], mk), t, tk)
            yield
            t = q.dve(lambda e: e.tensor_copy(R8[:, s, 1, 0:6], M8[:, s, 0:6]), tm)
            ti = q.dve(lambda e: e.max_index(IX[:, s, :], M8[:, s, :], mk), tm)
            yield
            t = q.dve(lambda e: e.match_replace(RP[:, s, 16:56], R8[:, s, 1, :], mk, -2.0e38), t)
            tc = q.dve(lambda e: e.tensor_copy(idf[:, 0:6], IX[:, s, 0:6]), ti, got(("HR", n % 4)))
            ta = q.dve(lambda e: e.tensor_scalar(AX1[:, s, :], IX[:, s, 0:1], 1, None,
                                                 ALU.logical_shift_right), ti)
            yield
            ts = q.dve(lambda e: e.tensor_tensor(
                SALL[:, n, 0:R1], RP[:, s, 16:16 + R1], mk[:, 0:R1], ALU.not_equal), t)
            tc2 = q.dve(lambda e: e.tensor_copy(SC1[:, s, 4:5], AX1[:, s, :]), ta)
            eq = EQ[:, z, :].rearrange("p (k e) -> p k e", k=6)
            t = q.dve(lambda e: e.tensor_tensor(
                eq, idf[:, 0:6].unsqueeze(2).broadcast_to([P, 6, R1]),
                cst("iota")[:, 0:R1].unsqueeze(1).broadcast_to([P, 6, R1]), ALU.is_equal), tc)
            yield
            sel_t[n] = [ts, q.dve(lambda e: e.tensor_scalar(
                SALL[:, n, R1:E1], cst("iota")[:, 0:NA], SC1[:, s, 4:5], None, ALU.is_equal), tc2)]
            t = q.dve(lambda e: e.tensor_tensor(
                eq, eq, sco.unsqueeze(1).broadcast_to([P, 6, R1]), ALU.mult), t)
            tc3 = q.dve(lambda e: e.tensor_scalar(idf[:, 6:7], SC1[:, s, 4:5], float(R1), None, ALU.add), tc2)
            yield
            t = q.dve(lambda e: e.tensor_reduce(EW8[:, s, 0:6], eq, AX.X, ALU.add), t)
            tc4 = q.dve(lambda e: e.memset(idf[:, 7:8], -1.0))
            tw_ = q.dve(lambda e: e.memset(hr[:, 278:280], 0.1))
            yield
            t2 = q.dve(lambda e: e.tensor_reduce(SC1[:, s, 1:2], EW8[:, s, 0:6], AX.X, ALU.add), t)
            yield
            t2 = q.dve(lambda e: e.tensor_scalar(SC1[:, s, 1:2], SC1[:, s, 1:2], 1e-20, None, ALU.add), t2)
            yield
            t2 = q.dve(lambda e: e.reciprocal(SC1[:, s, 2:3], SC1[:, s, 1:2]), t2)
            yield
            t2 = q.dve(lambda e: e.tensor_scalar(
                hr[:, 272:278], EW8[:, s, 0:6], SC1[:, s, 2:3], 0.2, ALU.mult, ALU.mult), t2)
            w_t[n] = [tc, tc3, tc4, t2, tw_, td, ts, h2T_t[n], h2_t[n // 2][n % 2]]

        def stay1(n):
            w = n % 2
            t, bank, PO = yield from position(n, E1, SALL[:, n, :])
            sum_t[n + 1] = q.dve(lambda e: e.tensor_tensor(
                SUM[:, 1 - w, 0:E1], SUM[:, w, 0:E1], SALL[:, n, :], ALU.add), sel_t[n], sum_t[n], t)
            t = q.dve(lambda e: e.tensor_copy(PALL[:, n, :], PO), t)
            give(bank, t)
            pos_t[n] = t
            free[("HR", n % 4)] = ld(f"hs{n % 4}", rows_d[n * P:n * P + P, :], HR[:, n % 4, :], w_t[n])
            stay_t[n] = free[("HR", n % 4)]

        CNTG = sb("CNTG", [P, 4, 4])
        rows_d = nc.dram_tensor("rows_d", [2048, ROW], F32)
        stay_t = {}
        q.lists["act"].append(("set", "natural_log_exp_and_others"))
        attention(1, lambda n: xc_t[n], y_add, route1, stay1)
        clear_some(100)

        PO = PS[:, 7, 0:E1]
        t = q.pe(lambda e: mm(e, PO, [(ones, SUM[:, 0, 0:E1])]), sum_t[NT], got_bank(7))
        t = q.dve(lambda e: e.tensor_copy(TOT[:, :], PO), t)
        free[("M", 7)] = t
        CM3 = R[:, lo:lo + E1 * 16].rearrange("p (e j) -> p e j", j=16)
        t = q.dve(lambda e: e.tensor_tensor(
            CM3, TOT[:, :].unsqueeze(2).broadcast_to([P, E1, 16]),
            cst("step").unsqueeze(1).broadcast_to([P, E1, 16]), ALU.is_gt), t, free[("HH", 0, 0)], free[("HH", 0, 1)])
        t = q.dve(lambda e: e.tensor_reduce(TIL[:, :], CM3, AX.X, ALU.add), t)
        tc = []
        for lo_, hi_, ini in ((0, R1, 0.0), (R1, E1, float(T1))):
            tc.append(q.dve(lambda e, lo_=lo_, hi_=hi_, ini=ini: e.tensor_tensor_scan(
                CUM[:, lo_:hi_], ones[:, 0:hi_ - lo_], TIL[:, lo_:hi_], ini, ALU.mult, ALU.add), t))
        t = q.dve(lambda e: e.tensor_tensor(NBT[:, :], CUM[:, :], TIL[:, :], ALU.subtract), tc)
        t_nb = q.dve(lambda e: e.tensor_scalar(NBT[:, :], NBT[:, :], -float(P), BIG, ALU.mult, ALU.add), t)
        t1 = q.dve(lambda e: e.tensor_scalar(CMP[:, 0:R1], CUM[:, 0:R1], cst("part"), 0.0, ALU.is_le, ALU.add,
                                             accum_out=CNT[:, 0:1]), tc)
        t2 = q.dve(lambda e: e.tensor_scalar(CNT[:, 1:2], cst("part"), float(T1), None, ALU.add))
        t2 = q.dve(lambda e: e.tensor_scalar(CMP[:, R1:E1], CUM[:, R1:E1], CNT[:, 1:2], 0.0, ALU.is_le, ALU.add,
                                             accum_out=SC1[:, 0, 5:6]), t2)
        t1 = q.dve(lambda e: e.tensor_scalar(CNT[:, 0:1], CNT[:, 0:1], float(R1 - 1), None, ALU.min), t1)
        t2 = q.dve(lambda e: e.tensor_scalar(CNT[:, 1:2], SC1[:, 0, 5:6], float(NA - 1), None, ALU.min), t2)
        banks = [b for b in barrier_banks() if b]
        q.wait("pe", *banks)

        def tiles(e):
            e.matmul(PS[:, 0, 0:T1], CNT[:, 0:1].broadcast_to([P, P]), ident, start=True, stop=True)
            return e.matmul(PS[:, 0, T1:T1 + TA], CNT[:, 1:2].broadcast_to([P, P]), ident[:, 0:TA],
                            start=True, stop=True)
        t = q.pe(tiles, t1, t2)
        t_ti = q.dve(lambda e: e.tensor_copy(TI[:, :], PS[:, 0, 0:T1 + TA]), t)
        t_te = q.dve(lambda e: e.tensor_copy(TE[:, 0:T1], PS[:, 0, 0:T1]), t)
        t_te = q.dve(lambda e: e.tensor_scalar(TE[:, T1:T1 + TA], PS[:, 0, T1:T1 + TA], float(R1), None, ALU.add), t)

        for n in range(4):
            pass
        hr_t = {}
        scat1 = []

        def row_load(n):
            hr_t[n] = ld(f"hl{n % 4}", HR[:, n % 4, :], rows_d[n * P:n * P + P, :], stay_t[n],
                         free[("HR", n % 4)], stay_t[NT - 4 + n] if n < 4 else None)

        for n in range(4):
            row_load(n)
        t_done = None
        for n in range(NT):
            s = n % 2
            t = q.dve(lambda e, s=s, n=n: e.tensor_tensor(T2_[:, s, 0:E1], NBT[:, :], PALL[:, n, :], ALU.subtract),
                      t_nb, pos_t[n])
            t = q.dve(lambda e, s=s, n=n: e.tensor_tensor(
                KEY[:, s, 0:E1], T2_[:, s, 0:E1], SALL[:, n, :], ALU.mult), t, sel_t[n])
            t_done = t
            t = q.dve(lambda e, s=s: e.max(K8[:, s, :], KEY[:, s, 0:E1]), t)
            t = q.dve(lambda e, s=s, n=n: e.tensor_scalar(
                RI[:, n % 4, :], K8[:, s, :], -1.0, BIG, ALU.mult, ALU.add), t,
                scat1[n - 4] if n >= 4 else None, scat0)
            for k in range(K1):
                tok = q.dma(f"sd{n % 4}", lambda e, n=n, k=k: e.indirect_dma_start(
                    out=buf1[:, :], out_offset=bass.IndirectOffsetOnAxis(
                        ap=RI[:, n % 4, k:k + 1].bitcast(U32), axis=0),
                    in_=HR[:, n % 4, :], in_offset=None, bounds_check=(T1 + TA) * P - 1, oob_is_err=False),
                    t, hr_t[n], clr["b1"][-1], engine="pool")
            scat1.append(tok)
            free[("HR", n % 4)] = tok
            if n + 4 < NT:
                row_load(n + 4)

        a1_done = [v for k, v in free.items() if isinstance(k, tuple) and k[0] in (
            "SM", "PTS", "CXT", "CX", "QT", "KBD", "HH", "HT", "YL", "KT")] + [free["VA"], t_done]
        w1_t = []
        for g in range(8):
            es = slice(4 * g, 4 * g + 4)
            for k in range(2):
                for o, nm in enumerate(("w1g", "w1u")):
                    w1_t.append(ld(f"w1_{g}", W1[:, es, k * 256 + o * P:k * 256 + o * P + P],
                                   a[nm][es, k * P:k * P + P, :].rearrange("e p n -> p e n"), a1_done))
            w1_t.append(ld(f"w1_{g}", W1[:, es, 512:768], a["w1d"][es].rearrange("e p n -> p e n")))
        for k in range(2):
            for o, nm in enumerate(("wag", "wau")):
                w1_t.append(ld("w1_a", WA[:, :, k * P + o * 64:k * P + o * 64 + 64],
                               a[nm][:, k * P:k * P + P, :].rearrange("l p n -> p l n")))
        w1_t.append(ld("w1_a", WD, a["wad"].rearrange("l p n -> p l n")))

        def add1(n, bank, t):
            return q.dve(lambda e: e.tensor_tensor(X[:, n, :], PS[:, bank, 0:256], X[:, n, :], ALU.add), t)

        q.wait("pe", t_ti, t_te)
        sg1 = WS1[:, 0:256].rearrange("p (c n) -> p c n", c=2)
        su1 = WS1[:, 256:512].rearrange("p (c n) -> p c n", c=2)
        shared(1, lambda k, i: sg1[:, k, :], lambda k, i: su1[:, k, :], lambda i: WS1[:, 512:768], t_small, add1)
        banks = [b for b in barrier_banks() if b]
        q.wait("pe", *banks)

        bx_t, xt_t, mt_t, ac_t, at_t, sp1 = {}, {}, {}, {}, {}, []
        NTL = T1 + TA
        reg_v = {}

        def width(i):
            return P if i < T1 else 64

        for i in range(4):
            bx_t[i] = bx_load(i, buf1, scat1[-4:])
        for i in range(NTL + 3):
            if i < NTL:
                xt_t[i], mt_t[i] = stage_a(i, bx_t, TE[:, i:i + 1], t_te)
                if i + 4 < NTL:
                    bx_t[i + 4] = bx_load(i + 4, buf1)
            if 0 <= i - 1 < NTL:
                j = i - 1
                s = j % 2
                w = width(j)

                def go(e, j=j, s=s, w=w):
                    r = e.value_load(TI[0:1, j:j + 1], min_val=0, max_val=(R1 if j < T1 else NA) - 1)
                    reg_v[j] = r
                    src = W1 if j < T1 else WA
                    for k in range(2):
                        m = e.matmul(PS[:, 2 + s, 0:2 * w], XT[:, j % 3, k, :],
                                     src[:, bass.ds(r, 1), k * 2 * w:(k + 1) * 2 * w].rearrange("p a n -> p (a n)"),
                                     start=(k == 0), stop=(k == 1))
                    return m
                t = q.pe(go, xt_t[j], w1_t if j == 0 else None, got(("GU", s)))
                free[("XT", j % 3)] = t
                t1 = q.act(lambda e, s=s, w=w: e.activation(SL[:, s, 0:w], PS[:, 2 + s, 0:w], ACT.Silu), t,
                           got(("SL", s)))
                t = q.dve(lambda e, s=s, w=w: e.tensor_tensor(
                    AC[:, s, 0:w], SL[:, s, 0:w], PS[:, 2 + s, w:2 * w], ALU.mult), t1, got(("AC", s)))
                free[("GU", s)] = free[("SL", s)] = t
                ac_t[j] = t
            if 0 <= i - 2 < NTL:
                j = i - 2
                s = j % 2
                w = width(j)
                t = q.pe(lambda e, s=s, w=w: e.transpose(PS[0:w, 6 + s, 0:P], AC[:, s, 0:w], ident), ac_t[j],
                         got(("T2", s)))
                free[("AC", s)] = t
                t = q.act(lambda e, s=s, w=w: e.copy(AT[0:w, s, :], PS[0:w, 6 + s, 0:P]), t, got(("AT", s)))
                free[("T2", s)] = t
                at_t[j] = t
            if 0 <= i - 3 < NTL:
                j = i - 3
                s = j % 2
                w = width(j)

                def go(e, j=j, s=s, w=w):
                    src = W1[:, bass.ds(reg_v[j], 1), 512:768] if j < T1 else WD[:, bass.ds(reg_v[j], 1), :]
                    return e.matmul(PS[:, 4 + s, 0:256], AT[0:w, s, :], src.rearrange("p a n -> p (a n)"),
                                    start=True, stop=True)
                t = q.pe(go, at_t[j], got(("Y", s)))
                free[("AT", s)] = t
                sp1.append(put_back(j, t, mt_t[j][1], mt_t[j][0], yb1, 2048 * K1 - 1))

        yv1 = yb1.rearrange("(t k) d -> t (k d)", k=K1)
        y1_t = {}
        last = [free[("AT", 0)], free[("AT", 1)]] + sp1[-3:]

        def y1_load(n):
            y1_t[n] = ld(f"yf{n % 4}", YF[:, n % 4, 0:K1 * D], yv1[n * P:n * P + P, :], last, got(("YF", n % 4)))

        for n in range(4):
            y1_load(n)
        for n in range(NT):
            yl = YF[:, n % 4, :]
            t = q.dve(lambda e, yl=yl: e.tensor_tensor(yl[:, 0:768], yl[:, 0:768], yl[:, 768:1536], ALU.add), y1_t[n])
            t = q.dve(lambda e, yl=yl: e.tensor_tensor(yl[:, 0:256], yl[:, 0:256], yl[:, 256:512], ALU.add), t)
            t = q.dve(lambda e, yl=yl: e.tensor_tensor(yl[:, 512:768], yl[:, 512:768], yl[:, 1536:1792], ALU.add))
            t = q.dve(lambda e, yl=yl: e.tensor_tensor(yl[:, 0:256], yl[:, 0:256], yl[:, 512:768], ALU.add), t)
            t = q.dve(lambda e, yl=yl, n=n: e.tensor_tensor(X[:, n, :], X[:, n, :], yl[:, 0:256], ALU.add), t)
            free[("YF", n % 4)] = t
            if n + 4 < NT:
                y1_load(n + 4)
            t_out = ld("out", out_d[:, n, :], X[:, n, :], t, engine="act")
        q.wait("act", t_out)

        sems = {name: ctx.enter_context(nc.semaphore("s_" + name)) for name in q.count}
        block = ctx.enter_context(nc.Block())

        @block.sync
        def _(e):
            q.run("sp", e, sems)

        @block.gpsimd
        def _(e):
            q.run("pool", e, sems)

        @block.scalar
        def _(e):
            q.run("act", e, sems)

        @block.vector
        def _(e):
            q.run("dve", e, sems)

        @block.tensor
        def _(e):
            q.run("pe", e, sems)


def kernel(**inputs):
    import concourse.bacc as _bacc
    from concourse.bass_utils import run_bass_kernel_spmd as _run

    g = {k: np.asarray(v) for k, v in inputs.items()}
    c = np.ascontiguousarray
    arrays = {
        "x": g["x"],
        "cst": constants()[0],
        "ctxT": c(g["ctx_1024"].reshape(NB * SK, D).T),
        "mask": c(g["mask_1x1xSxS2_ik0"].reshape(256, SK)),
        "wq0": c(g["L0_xattn_w_q"].T), "wk0": c(g["L0_xattn_w_k"].T),
        "wv0": c(g["L0_xattn_w_v"].T), "wo0": c(g["L0_xattn_w_o"].T),
        "wq1": g["L1_xattn_W_q"], "wk1": g["L1_xattn_W_k"],
        "wv1": g["L1_xattn_W_v"], "wo1": g["L1_xattn_W_o"],
        "bqk": np.concatenate([g["L1_xattn_b_q"].reshape(2, P).T, g["L1_xattn_b_k"].reshape(2, P).T], 1),
        "bv": g["L1_xattn_b_v"], "bo": g["L1_xattn_b_o"],
        "gate0": np.concatenate([g["L0_ffn_gate_w"], g["L0_ffn_shared_gate_w"]], 1),
        "sgu0": g["L0_ffn_shared_gate_up_w"], "sd0": g["L0_ffn_shared_down_w"],
        "egu": g["L0_ffn_expert_gate_up_w"], "ed": g["L0_ffn_expert_down_w"],
        "gate1": c(g["L1_ffn_gate_weight"].T), "gbias": g["L1_ffn_gate_bias"],
        "w1g": g["L1_ffn_w_gate"], "w1u": g["L1_ffn_w_up"], "w1d": g["L1_ffn_w_down"],
        "sg1": g["L1_ffn_shared_w_gate"], "su1": g["L1_ffn_shared_w_up"], "sd1": g["L1_ffn_shared_w_down"],
        "wag": g["L1_ffn_anchor_w_gate"], "wau": g["L1_ffn_anchor_w_up"], "wad": g["L1_ffn_anchor_w_down"],
    }
    nc = _bacc.Bacc("TRN2", target_bir_lowering=False, num_devices=1)
    feed, args = {}, {}
    for name, v in arrays.items():
        v = np.ascontiguousarray(v)
        feed["in_" + name] = v
        args[name] = nc.dram_tensor("in_" + name, v.shape, mybir.dt.from_np(v.dtype), kind="ExternalInput").ap()
    out = nc.dram_tensor("out_0", (NB, 256, D), F32, kind="ExternalOutput").ap()
    build(nc, args, out)
    r = _run(nc, [feed], core_ids=[0])
    return r.results[0]["out_0"]
```

```python
import numpy as np
import concourse.bass as bass
from concourse import mybir
from contextlib import ExitStack

F32 = mybir.dt.float32
I32 = mybir.dt.int32
U32 = mybir.dt.uint32
ALU = mybir.AluOpType
ACT = mybir.ActivationFunctionType
AX = mybir.AxisListType

P = 128
D = 256
NT = 16
NB = 8
SK = 120
H = 16
ROW = 280
E0 = 64
CAP = 128
R1 = 32
NA = 16
E1 = R1 + NA
T1 = 128
TA = 32
K0 = 8
K1 = 7
NEW = 24
BIG = 65536.0
SEG = 17
DUM = R1 * SEG
SEG_A = DUM + 1
DUM_A = SEG_A + NA * SEG
BIG1 = 131072.0
OFF = 30000.0
NEG = -3.0e38
EPS = 1e-5
MAGIC = float(0x5F3759DF)


def constants():
    p = np.arange(P, dtype=np.float32)[:, None]
    j = np.arange(P, dtype=np.float32)[None, :]
    t = np.arange(NT, dtype=np.float32)[None, :, None] * P + p[:, :, None]
    k = np.arange(8, dtype=np.float32)[None, None, :]
    parts = [
        ("ident", (p == j)),
        ("upper", (p < j)),
        ("ones", np.ones((P, P))),
        ("d0", (t * K0 + k - OFF).reshape(P, -1)),
        ("d1", (np.where(k < 6, t * 6 + k, t) - OFF).reshape(P, -1)),
        ("nb0", np.broadcast_to(BIG - CAP * j[:, :E0], (P, E0))),
        ("iota", np.broadcast_to(j[:, :48], (P, 48))),
        ("step", np.broadcast_to(np.where(j == 0, -1, P * j)[:, :16], (P, 16))),
        ("nb1", np.broadcast_to(BIG1 - P * (SEG * j + (j >= R1))[:, :E1], (P, E1))),
        ("part", p),
        ("pad", np.full((P, 48), NEG)),
    ]
    at, place, cols = 0, {}, []
    for name, a in parts:
        place[name] = (at, a.shape[1])
        at += a.shape[1]
        cols.append(np.asarray(a, np.float32))
    return np.ascontiguousarray(np.concatenate(cols, 1)), place


class Queues:

    def __init__(self):
        self.lists = {e: [] for e in ("pe", "act", "dve", "pool", "sp")}
        self.count = {}

    def put(self, engine, sem, inc, fn, waits):
        q = self.lists[engine]
        for w in waits:
            for tok in (w if isinstance(w, list) else [w]):
                if tok is not None:
                    q.append(("wait", tok))
        self.count[sem] = self.count.get(sem, 0) + inc
        q.append(("do", fn, sem, inc))
        return (sem, self.count[sem])

    def pe(self, fn, *waits):
        return self.put("pe", "pe", 1, fn, waits)

    def act(self, fn, *waits):
        return self.put("act", "act", 1, fn, waits)

    def dve(self, fn, *waits):
        return self.put("dve", "dve", 1, fn, waits)

    def pool(self, fn, *waits):
        return self.put("pool", "pool", 1, fn, waits)

    def dma(self, sem, fn, *waits, engine="sp"):
        return self.put(engine, sem, 16, fn, waits)

    def wait(self, engine, *waits):
        for tok in waits:
            self.lists[engine].append(("wait", tok))

    def register(self, engine, fn, *waits):
        self.wait(engine, *waits)
        self.lists[engine].append(("register", fn))

    def run(self, engine, eng, sems):
        seen = {}
        for item in self.lists[engine]:
            if item[0] == "wait":
                sem, n = item[1]
                if seen.get(sem, 0) < n:
                    eng.wait_ge(sems[sem], n)
                    seen[sem] = n
            elif item[0] == "register":
                item[1](eng)
            elif item[0] == "set":
                eng.preload_act_table_set(item[1])
            else:
                _, fn, sem, inc = item
                fn(eng).then_inc(sems[sem], inc)


def build(nc, a, out):
    place = constants()[1]
    ncst = sum(n for _, n in place.values())
    buf0 = nc.dram_tensor("buf0", [E0 * P, ROW], F32)
    buf1 = nc.dram_tensor("buf1", [(DUM_A + 1) * P, ROW], F32)
    yb0 = nc.dram_tensor("yb0", [2048 * K0, D], F32)
    yb1 = nc.dram_tensor("yb1", [2048 * 6, D], F32)
    yba = nc.dram_tensor("yba", [2048, D], F32)
    x_d = a["x"].rearrange("b s d -> (b s) d").rearrange("(n p) d -> p n d", p=P)
    out_d = out.rearrange("b s d -> (b s) d").rearrange("(n p) d -> p n d", p=P)
    q = Queues()

    with ExitStack() as ctx:
        def sb(name, shape, dt=F32):
            return ctx.enter_context(nc.sbuf_tensor(name, shape, dt))

        PS = ctx.enter_context(nc.psum_tensor("PS", [P, 8, 512], F32))
        C = sb("C", [P, ncst])

        def cst(name):
            o, n = place[name]
            return C[:, o:o + n]

        ident, upper, ones = cst("ident"), cst("upper"), cst("ones")
        X = sb("X", [P, NT, D])
        H2T = sb("H2T", [P, 2, NT * P])
        HR = sb("HR", [P, 4, ROW])
        WS1 = sb("WS1", [P, 768])
        BX = sb("BX", [P, 4, ROW])
        XT = sb("XT", [P, 3, 2, P])
        SL = sb("SL", [P, 2, P])
        AC = sb("AC", [P, 3, P])
        AT = sb("AT", [P, 2, P])
        YT = sb("YT", [P, 3, D])
        DF = sb("DF", [P, 4])
        WC = sb("WC", [P, 8])
        DI = sb("DI", [P, T1 + TA], I32)
        TE = sb("TE", [P, T1 + TA])
        TI = sb("TI", [P, T1 + TA], I32)
        JK = sb("JK", [P, 2, 2, 8])
        SS_ = sb("SS_", [P, 2, 512])
        AS_ = sb("AS_", [P, 4, 512])
        BO = sb("BO", [1, D])
        BQK = sb("BQK", [P, 4])
        GB = sb("GB", [P, R1])
        WR1 = sb("WR1", [P, 2, R1])
        SIG = sb("SIG", [P, NT])
        ST = sb("ST", [P, 4, 2, 6])
        MV = sb("MV", [P, 4, 2, 2])
        NW = sb("NW", [P, 4, 2, 2])
        MX = sb("MX", [P, 3, 8])
        RC = sb("RC", [P, 2, H])
        T2_ = sb("T2_", [P, 4, 64])
        KEY = sb("KEY", [P, 4, 64])
        SUM = sb("SUM", [P, 2, 64])
        M8 = sb("M8", [P, 4, 8])
        G8 = sb("G8", [P, 4, 4, 8])
        GS = sb("GS", [P, 4, 16])
        R8 = sb("R8", [P, 4, 2, 8])
        IX = sb("IX", [P, 4, 8], U32)
        AX1 = sb("AX1", [P, 4, 1], U32)
        EW8 = sb("EW8", [P, 4, 8])
        SC1 = sb("SC1", [P, 4, 8])
        RI = sb("RI", [P, 4, 8], I32)
        K8 = sb("K8", [P, 4, 8])
        Z = sb("Z", [P, ROW])
        TU = sb("TU", [P, T1 + TA], I32)
        PAD = sb("PAD", [P, E1], I32)
        TOT = sb("TOT", [P, E1])
        TIL = sb("TIL", [P, E1])
        CUM = sb("CUM", [P, E1])
        CNT = sb("CNT", [P, 8])
        CMP = sb("CMP", [P, E1])
        R = sb("R", [P, 32768])

        at = [0]

        def reg(n):
            at[0] += n
            return R[:, at[0] - n:at[0]]

        CT = reg(1920).rearrange("p (c n) -> p c n", c=2)
        VA = reg(NB * H * 17).rearrange("p (b h d) -> p b h d", b=NB, h=H)
        AW1 = reg(4 * 512).rearrange("p (w c n) -> p w c n", w=4, c=2)
        KT = reg(1920).rearrange("p (c n) -> p c n", c=2)
        KBD = reg(4 * 960).rearrange("p (s c n) -> p s c n", s=2, c=2)
        AW0 = reg(4 * 512).rearrange("p (w c n) -> p w c n", w=4, c=2)
        YL = reg(3 * 2048).rearrange("p (s n) -> p s n", s=3)
        lo = at[0]
        HH = reg(2 * 512).rearrange("p (s n d) -> p s n d", s=2, n=2)
        HT = reg(2 * 512).rearrange("p (s c t) -> p s c t", s=2, c=2)
        QT = reg(2 * 512).rearrange("p (s c t) -> p s c t", s=2, c=2)
        SM = reg(3 * 960).rearrange("p (s h k) -> p s h k", s=3, h=8)
        PT = reg(4 * 512).rearrange("p (s h t) -> p s h t", s=4, h=4)
        CX = reg(2 * 256).rearrange("p (s d) -> p s d", s=2)
        CXT = reg(2 * 256).rearrange("p (s c t) -> p s c t", s=2, c=2)
        CAPM = reg(2 * SK).rearrange("p (n k) -> p n k", n=2)
        MSK = reg(2 * SK).rearrange("p (n k) -> p n k", n=2).bitcast(I32)
        MF = reg(2 * SK).rearrange("p (n k) -> p n k", n=2)
        BV = reg(D)
        LG = reg(256).rearrange("p (s e) -> p s e", s=4)
        RP = reg(256).rearrange("p (s e) -> p s e", s=4)
        SEL = reg(256).rearrange("p (s e) -> p s e", s=4)
        EQ = reg(12 * R1).rearrange("p (s n) -> p s n", s=2)
        T1_ = reg(256).rearrange("p (s e) -> p s e", s=4)
        WR0 = reg(130).rearrange("p (c n) -> p c n", c=2)
        assert at[0] <= 32768
        EWR = [R[:, lo - 3072 + 768 * i:lo - 2304 + 768 * i] for i in range(14)] + \
            [R[:, lo - 13824 + 768 * i:lo - 13056 + 768 * i] for i in range(10)]
        SG0 = R[:, lo - 6144:lo - 4096].rearrange("p (c n) -> p c n", c=2)
        SD0 = R[:, lo - 4096:lo - 3072].rearrange("p (c n) -> p c n", c=4)
        W1 = R[:, 0:24576].rearrange("p (e n) -> p e n", e=R1)
        WA = R[:, 24576:28672].rearrange("p (l n) -> p l n", l=NA)
        WD = R[0:64, 28672:32768].rearrange("p (l n) -> p l n", l=NA)
        YF = R[:, 0:NT * 1536].rearrange("p (s n) -> p s n", s=NT)
        YA = R[:, 24576:24576 + NT * D].rearrange("p (s n) -> p s n", s=NT)

        def ld(sem, dst, src, *waits, engine="sp"):
            return q.dma(sem, lambda e: e.dma_start(dst, src), *waits, engine=engine)

        def chunks(name):
            return a[name].rearrange("(c p) n -> p c n", p=P)

        q.lists["act"].append(("set", "natural_log_exp_and_others"))
        t_c = ld("l_c", C[:, :], a["cst"])
        t_x, t_w = {}, {}

        def x_load(i):
            t_x[i] = ld(f"l_x{i}", X[:, 4 * i:4 * i + 4, :], x_d[:, 4 * i:4 * i + 4, :])

        names = ["wq0", "wk0", "wv0", "wo0", "wq1", "wk1", "wv1", "wo1"]

        def w_load(i):
            t_w[names[i]] = ld("l_" + names[i], (AW1 if i > 3 else AW0)[:, i % 4, :, :], chunks(names[i]))

        w_load(1)
        t_ct = ld("l_ct", CT, chunks("ctxT"))
        x_load(0)
        w_load(0)
        w_load(2)
        t_mask = ld("l_mask", MSK, a["mask"].rearrange("(n p) k -> p n k", p=P))
        x_load(1)
        w_load(3)
        t_wr0 = ld("l_wr0", WR0, chunks("gate0"))
        x_load(2)
        x_load(3)
        t_z = q.pool(lambda e: e.memset(Z[:, :], 0.0))
        t_kz = q.pool(lambda e: e.memset(KBD, 0.0))
        t_va1 = q.pool(lambda e: e.memset(VA[:, :, :, 16:17], 1.0))
        t_sum0 = q.pool(lambda e: e.memset(SUM[:, :, :], 0.0))
        t_r8 = q.pool(lambda e: e.memset(R8[:, :, :, :], NEG))
        t_gs = q.pool(lambda e: e.memset(GS[:, :, :], NEG))

        clr = {"b0": [], "y0": []}
        b0f = buf0.rearrange("a b -> (a b)").rearrange("(p r n) -> p r n", p=P, n=ROW)
        y0f = yb0.rearrange("a b -> (a b)").rearrange("(p r n) -> p r n", p=P, n=D)

        def clear(kind, flat, r0, n):
            width = flat.shape[2]
            src = Z[:, 0:width].unsqueeze(1).broadcast_to([P, n, width])
            clr[kind].append(q.dma("z_" + kind, lambda e: e.dma_start(flat[:, r0:r0 + n, :], src), t_z, engine="act"))

        later = [("b0", b0f, r, 8) for r in range(0, 64, 8)] + [("y0", y0f, r, 8) for r in range(0, 128, 8)]

        def clear_some(n):
            for _ in range(n):
                if later:
                    clear(*later.pop(0))

        t_dum = [q.dma("z_dum", lambda e, u=u: e.dma_start(buf1[u * P:u * P + P, :], Z[:, :]), t_z, engine="act")
                 for u in (DUM, DUM_A)]

        t = q.dve(lambda e: e.tensor_scalar(MF, MSK, 0.0, None, ALU.is_equal), t_mask)
        t2 = q.dve(lambda e: e.tensor_scalar(CAPM, MF, NEG, -NEG, ALU.mult, ALU.add), t)
        t_cap = q.dve(lambda e: e.scalar_tensor_tensor(
            out=CAPM, in0=MF, scalar=-1.0e9, in1=CAPM, op0=ALU.mult, op1=ALU.add), t2)

        free = {}

        def got(key):
            return free.get(key)

        held = {5: False, 7: False}

        def misc():
            while True:
                for bank in (5, 7):
                    if not held[bank]:
                        held[bank] = True
                        return bank, PS[:, bank, 0:256]
                yield

        def give(bank, t):
            free[("M", bank)] = t
            held[bank] = False

        def got_bank(bank):
            return free.get(("M", bank))

        def layernorm(ns, s, dst, waits, out_t):
            m, t = len(ns), []
            for i, n in enumerate(ns):
                t.append(q.dve(lambda e, i=i, n=n: e.bn_stats(ST[:, s, i, :], X[:, n, :]), waits[i]))
                yield
            for i in range(m):
                tb = q.dve(lambda e, i=i: e.bn_aggr(MV[:, s, i, :], ST[:, s, i, :]), t[i])
            yield
            ve, rs = NW[:, s, 0, 0:m], NW[:, s, 1, 0:m]
            t = q.dve(lambda e: e.tensor_scalar(ve, MV[:, s, 0:m, 1], EPS, None, ALU.add), tb)
            yield
            t = q.act(lambda e: e.activation(ve, ve, ACT.Ln), t)
            t = q.act(lambda e: e.activation(rs, ve, ACT.Exp, scale=-0.5), t)
            yield
            yield
            for i, n in enumerate(ns):
                out_t.append(q.dve(lambda e, i=i, n=n: e.tensor_scalar(
                    dst(i), X[:, n, :], MV[:, s, i, 0:1], rs[:, i:i + 1], ALU.subtract, ALU.mult),
                    t, waits[m + i]))
                yield

        def mm(e, out_, pairs):
            for i, (l, r) in enumerate(pairs):
                m = e.matmul(out_, l, r, start=(i == 0), stop=(i == len(pairs) - 1))
            return m

        def tr2(e, out_, src):
            e.transpose(out_[:, 0:128], src[:, 0:128], ident)
            return e.transpose(out_[:, 128:256], src[:, 128:256], ident)

        def attention(l, t_kz, x_ready, before, route, rows, behind_it):
            wq, wk, wv, wo = ((AW1 if l else AW0)[:, i, :, :] for i in range(4))
            tw = [t_w[names[4 * l + i]] for i in range(4)]
            kt_t = []
            for c in range(2):
                for half in range(2):
                    bank = 2 * c + half
                    t = q.pe(lambda e, c=c, half=half, bank=bank: mm(
                        e, PS[:, bank, 0:480],
                        [(wk[:, k, c * P:c * P + P], CT[:, k, half * 480:half * 480 + 480]) for k in range(2)]),
                        tw[1], t_ct, got(("KT", 0)), got(("KT", 1)))
                    dst = KT[:, c, half * 480:half * 480 + 480]
                    if l == 0:
                        t = q.act(lambda e, bank=bank, dst=dst: e.copy(dst, PS[:, bank, 0:480]), t)
                    else:
                        t = q.act(lambda e, bank=bank, dst=dst, c=c: e.activation(
                            dst, PS[:, bank, 0:480], ACT.Identity, bias=BQK[:, 2 + c:3 + c]), t, t_small)
                    kt_t.append(t)
            free[("S", 0)], free[("S", 1)], free[("S", 2)], free[("PT", 0)] = kt_t
            qt_t, v_t, kb_t, h_t, ht_t = {}, {}, {}, {}, {}
            ex_t, pt_t, x_t, c_t, s_t, mx_t = {}, {}, {}, {}, {}, {}

            def prepare(b):
                s = b % 2
                while l and 2 * b + 1 not in xc_t:
                    yield
                h_t[b] = []
                yield from layernorm([2 * b, 2 * b + 1], s, lambda i: HH[:, s, i, :],
                                     [x_ready(2 * b), x_ready(2 * b + 1), got(("HH", s, 0)), got(("HH", s, 1))],
                                     h_t[b])
                while b > 1 and (4 * b - 5, 1) not in s_t:
                    yield
                for h in range(8):
                    kb_t[b] = q.dma(f"kb{s}", lambda e, h=h: e.dma_start(
                        KBD[16 * h:16 * h + 16, s, :, h * SK:h * SK + SK],
                        KT[16 * h:16 * h + 16, :, b * SK:b * SK + SK]), kt_t, t_kz, got(("KBD", s)))
                free[("KT", s)] = kb_t[b]
                hts = []
                for i in range(2):
                    bank, m = yield from misc()
                    t = q.pe(lambda e, i=i, m=m: tr2(e, m, HH[:, s, i, :]), h_t[b][i], t_c, got_bank(bank))
                    free[("HH", s, i)] = t
                    yield
                    t = q.act(lambda e, i=i, m=m: e.copy(
                        HT[:, s, :, i * P:i * P + P], m.rearrange("p (c t) -> p c t", c=2)), t, got(("HT", s)))
                    give(bank, t)
                    hts.append(t)
                ht_t[b] = hts
                yield
                yield
                qts = []
                for c in range(2):
                    bank, m = yield from misc()
                    t = q.pe(lambda e, c=c, m=m: mm(
                        e, m, [(wq[:, k, c * P:c * P + P], HT[:, s, k, :]) for k in range(2)]),
                        ht_t[b], tw[0], got_bank(bank))
                    free[("HT", s)] = t
                    yield
                    if l == 0:
                        t = q.act(lambda e, c=c, m=m: e.activation(
                            QT[:, s, c, :], m, ACT.Copy, scale=0.25), t, got(("QT", s)))
                    else:
                        t = q.act(lambda e, c=c, m=m: e.activation(
                            QT[:, s, c, :], m, ACT.Identity, bias=BQK[:, c:c + 1], scale=0.25),
                            t, got(("QT", s)), t_bq)
                    give(bank, t)
                    qts.append(t)
                bank, m = yield from misc()
                t = q.pe(lambda e: mm(
                    e, m[0:SK, :], [(CT[:, k, b * SK:b * SK + SK], wv[:, k, :]) for k in range(2)]),
                    tw[2], t_ct, got_bank(bank))
                yield
                dst = VA[0:SK, b, :, 0:16]
                src = m[0:SK, :].rearrange("p (h d) -> p h d", h=H)
                if l == 0:
                    t = q.dve(lambda e: e.tensor_copy(dst, src), t, t_va1)
                else:
                    t = q.dve(lambda e: e.tensor_tensor(
                        dst, src, BV[0:SK, :].rearrange("p (h d) -> p h d", h=H), ALU.add), t, t_small, got("VA"))
                give(bank, t)
                v_t[b] = t
                qt_t[b] = qts

            def scores(u, half):
                n, c = u // 2, u % 2
                b, s = n // 2, (n // 2) % 2
                while b not in qt_t:
                    step()
                w = (2 * u + half) % 3
                s_t[u, half] = q.pe(lambda e: e.matmul(
                    psum_scores(u, half),
                    QT[:, s, c, (n % 2) * P:(n % 2) * P + P],
                    KBD[:, s, c, half * 480:half * 480 + 480].rearrange("p (h k) -> p h k", h=4),
                    start=True, stop=True), qt_t[b], kb_t[b], got(("S", w)))
                free[("QT", s)] = free[("KBD", s)] = s_t[u, half]

            def psum_scores(u, half):
                return PS[:, (2 * u + half) % 3, :].rearrange("p (h k) -> p h k", k=P)[:, :, 0:SK]

            def cap(u, half):
                n, z = u // 2, u % 3
                s_t[u, half] = q.dve(lambda e: e.scalar_tensor_tensor(
                    out=SM[:, z, 4 * half:4 * half + 4, :], in0=psum_scores(u, half), scalar=-1.0e9,
                    in1=CAPM[:, n % 2, :].unsqueeze(1).broadcast_to([P, 4, SK]),
                    op0=ALU.max, op1=ALU.min), s_t[u, half], t_cap, got(("SM", z)))
                free[("S", (2 * u + half) % 3)] = s_t[u, half]

            def highest(u, half):
                z, hs = u % 3, slice(4 * half, 4 * half + 4)
                src = SM[:, z, hs, :] if l == 0 else psum_scores(u, half)
                mx_t[u, half] = q.dve(lambda e: e.tensor_reduce(
                    MX[:, z, hs], src, AX.X, ALU.max, negate=True), s_t[u, half], got(("MX", z)))

            def exps(u, half):
                z = u % 3
                src = SM[:, z, 4 * half:4 * half + 4, :] if l == 0 else psum_scores(u, half)
                for i in range(4):
                    h = 4 * half + i
                    t = q.act(lambda e, h=h, i=i: e.activation(
                        SM[:, z, h, :], src[:, i, :], ACT.Exp, bias=MX[:, z, h:h + 1]), mx_t[u, half],
                        got(("SM", z)) if l else None)
                ex_t[u, half] = t
                free[("MX", z)] = t
                if l:
                    free[("S", (2 * u + half) % 3)] = t

            def turn(u, half):
                z = u % 3

                def go(e):
                    for i in range(4):
                        m = e.transpose(PS[0:SK, 3 + half, i * P:i * P + P], SM[:, z, 4 * half + i, :], ident)
                    return m
                pt_t[u, half] = q.pe(go, ex_t[u, half], got(("PT", half)))
                free[("SM", z)] = pt_t[u, half]

            def turned(u, half):
                r = 2 * (u % 2) + half
                src = PS[0:SK, 3 + half, :].rearrange("p (h t) -> p h t", h=4)
                if l == 1 and half == 1:
                    t = q.dve(lambda e: e.tensor_copy(PT[0:SK, r, :, :], src), pt_t[u, half], got(("PTS", r)))
                else:
                    t = q.act(lambda e: e.copy(PT[0:SK, r, :, :], src), pt_t[u, half], got(("PTS", r)))
                free[("PT", half)] = pt_t[u, half] = t

            def values(u):
                n, c = u // 2, u % 2
                b = n // 2

                def go(e):
                    for i in range(8):
                        h = 8 * c + i
                        m = e.matmul(PS[:, 6, h * 17:h * 17 + 17], PT[0:SK, 2 * (u % 2) + i // 4, i % 4, :],
                                     VA[0:SK, b, h, :], start=True, stop=True)
                    return m
                t = q.pe(go, pt_t[u, 0], pt_t[u, 1], v_t[b], got("O"))
                free[("PTS", 2 * (u % 2))] = free[("PTS", 2 * (u % 2) + 1)] = t
                free["VA"] = c_t[n] = t

            def divide(n):
                s = n % 2
                O = PS[:, 6, 0:272].rearrange("p (h d) -> p h d", h=H)
                t = q.dve(lambda e: e.reciprocal(RC[:, s, :], O[:, :, 16]), c_t[n])
                t = q.dve(lambda e: e.tensor_tensor(
                    CX[:, s, :].rearrange("p (h d) -> p h d", h=H), O[:, :, 0:16],
                    RC[:, s, :].unsqueeze(2).broadcast_to([P, H, 16]), ALU.mult), t, got(("CX", s)))
                free["O"] = c_t[n] = t
                active.append(finish(n))

            def finish(n):
                s = n % 2
                yield
                yield
                bank, m = yield from misc()
                t = q.pe(lambda e, m=m: tr2(e, m, CX[:, s, :]), c_t[n], got_bank(bank))
                free[("CX", s)] = t
                yield
                t = q.act(lambda e, m=m: e.copy(CXT[:, s, :, :], m.rearrange("p (c t) -> p c t", c=2)),
                          t, got(("CXT", s)))
                give(bank, t)
                yield
                yield
                bank, m = yield from misc()

                def go(e):
                    pairs = [(CXT[:, s, k, :], wo[:, k, :]) for k in range(2)]
                    if l == 1:
                        pairs.append((ones[0:1, :], BO[0:1, :]))
                    return mm(e, m, pairs)
                t = q.pe(go, t, tw[3], got_bank(bank), t_small if l else None)
                free[("CXT", s)] = t
                yield
                t = q.dve(lambda e: e.tensor_tensor(X[:, n, :], m, X[:, n, :], ALU.add), t)
                give(bank, t)
                x_t[n] = t
                if n >= NT - 2:
                    active.append(behind([n]))
                elif n % 2:
                    active.append(behind([n - 1, n]))

            def behind(ns):
                for n in ns:
                    while n > 3 and (n - 4) not in hr_left:
                        yield
                made = []
                yield from layernorm(ns, 2 + (ns[0] // 2 + (ns[0] == NT - 1)) % 2, lambda i: HR[:, ns[i] % 4, 0:D],
                                     [x_t[n] for n in ns] + [got(("HR", n % 4)) for n in ns], made)
                for n, t in zip(ns, made):
                    h2_t[n] = t
                    active.append(per_tile(n))

            def per_tile(n):
                bank, m = yield from misc()
                t = q.pe(lambda e: tr2(e, m, HR[:, n % 4, 0:D]), h2_t[n], got_bank(bank))
                yield
                t = q.act(lambda e: e.copy(
                    H2T[:, :, n * P:n * P + P], m.rearrange("p (c t) -> p c t", c=2)), t, got("H2T"))
                give(bank, t)
                h2T_t[n] = t
                yield
                yield
                yield from route(n)
                while n not in sum_t:
                    yield
                yield from rows(n)
                hr_left.add(n)

            active, hr_left = [before], set()

            def step():
                for g in list(active):
                    try:
                        next(g)
                    except StopIteration:
                        active.remove(g)

            NU = 2 * NT
            LEAD = 9
            def main(u, slot):
                here, v, ahead = 0 <= u < NU, u - 1, 0 <= u + 1 < NU
                if slot == 0:
                    if ahead:
                        scores(u + 1, 0)
                    if here:
                        cap(u, 0) if l == 0 else highest(u, 0)
                elif slot == 1:
                    if 0 <= u - 2 < NU:
                        values(u - 2)
                    if here:
                        highest(u, 0) if l == 0 else exps(u, 0)
                elif slot == 2:
                    if 0 <= v < NU:
                        turn(v, 0)
                    if here:
                        if l == 0:
                            cap(u, 1)
                            exps(u, 0)
                        else:
                            highest(u, 1)
                elif slot == 3:
                    if 0 <= v < NU:
                        turn(v, 1)
                        turned(v, 0)
                    if ahead:
                        scores(u + 1, 1)
                    if here:
                        highest(u, 1) if l == 0 else exps(u, 1)
                elif slot == 4:
                    if 0 <= v < NU:
                        turned(v, 1)
                    if 0 <= u - 2 < NU and u % 2:
                        divide((u - 2) // 2)
                    if here and l == 0:
                        exps(u, 1)

            for u in range(-LEAD, NU + 2):
                if u % 4 == (-LEAD) % 4 and (u + LEAD) // 4 < NB:
                    active.append(prepare((u + LEAD) // 4))
                for slot in range(6):
                    main(u, slot)
                    step()
                    if u >= NU - 5 and slot % 2:
                        step()
                if u > -LEAD + 1:
                    clear_some(1)
            active.extend(behind_it(x_t))
            while active:
                step()

        h2_t, h2T_t, sel_t, w_t, xc_t = {}, {}, {}, {}, {}

        def route0(n):
            s = n % 4
            hr = HR[:, n % 4, :]
            bank, m = yield from misc()
            t = q.pe(lambda e: mm(
                e, m[:, 0:65], [(H2T[:, k, n * P:n * P + P], WR0[:, k, :]) for k in range(2)]),
                h2T_t[n], t_wr0, got_bank(bank))
            td = q.act(lambda e: e.copy(hr[:, 264:272], cst("d0")[:, 8 * n:8 * n + 8]), got(("HR", n % 4)))
            yield
            tl = q.dve(lambda e: e.tensor_copy(LG[:, s, :], m[:, 0:64]), t)
            ta = q.dve(lambda e: e.tensor_copy(SIG[:, n:n + 1], m[:, 64:65]), t)
            give(bank, ta)
            yield
            tm = q.dve(lambda e: e.max(M8[:, s, :], LG[:, s, :]), tl)
            ta = q.act(lambda e: e.activation(SIG[:, n:n + 1], SIG[:, n:n + 1], ACT.Exp, scale=-1.0), ta)
            yield
            tr = q.dve(lambda e: e.match_replace(RP[:, s, :], M8[:, s, :], LG[:, s, :], NEG), tm)
            tn = q.dve(lambda e: e.tensor_scalar(SC1[:, s, 0:1], M8[:, s, 0:1], -1.0, None, ALU.mult), tm)
            ti = q.dve(lambda e: e.max_index(IX[:, s, :], M8[:, s, :], LG[:, s, :]), tm)
            te = q.act(lambda e: e.activation(
                EW8[:, s, :], M8[:, s, :], ACT.Exp, bias=SC1[:, s, 0:1], accum_out=SC1[:, s, 1:2]), tn)
            yield
            sel_t[n] = q.dve(lambda e: e.tensor_tensor(SEL[:, s, :], RP[:, s, :], LG[:, s, :], ALU.not_equal), tr)
            tc = q.dve(lambda e: e.tensor_copy(hr[:, 256:264], IX[:, s, :]), ti, got(("HR", n % 4)))
            t1 = q.dve(lambda e: e.tensor_scalar(SIG[:, n:n + 1], SIG[:, n:n + 1], 1.0, None, ALU.add), ta)
            yield
            t = q.dve(lambda e: e.reciprocal(SC1[:, s, 2:3], SC1[:, s, 1:2]), te)
            free[("SIG", n)] = q.dve(lambda e: e.reciprocal(SIG[:, n:n + 1], SIG[:, n:n + 1]), t1)
            yield
            t = q.dve(lambda e: e.tensor_scalar(hr[:, 272:280], EW8[:, s, :], SC1[:, s, 2:3], None, ALU.mult), t)
            w_t[n] = [tc, td, t, h2_t[n], h2T_t[n]]

        sum_t = {0: t_sum0}

        def position(n, width, sel):
            bank, m = yield from misc()
            PO = m[:, 0:width]
            t = q.pe(lambda e: mm(e, PO, [(upper, sel), (ones, SUM[:, n % 2, 0:width])]),
                     sel_t[n], sum_t[n], got_bank(bank))
            yield
            return t, bank, PO

        def rows0(n):
            s, w = n % 4, n % 2
            t, bank, PO = yield from position(n, 64, SEL[:, s, :])
            t1 = q.dve(lambda e: e.scalar_tensor_tensor(
                out=T1_[:, s, :], in0=PO, scalar=float(CAP), in1=SEL[:, s, :], op0=ALU.is_lt, op1=ALU.mult), t)
            t2 = q.dve(lambda e: e.tensor_tensor(T2_[:, s, :], cst("nb0"), PO, ALU.subtract), t)
            give(bank, t2)
            sum_t[n + 1] = q.dve(lambda e: e.tensor_tensor(
                SUM[:, 1 - w, :], SUM[:, w, :], SEL[:, s, :], ALU.add), sel_t[n], sum_t[n], t)
            yield
            t = q.dve(lambda e: e.tensor_tensor(KEY[:, s, :], T1_[:, s, :], T2_[:, s, :], ALU.mult), t1, t2)
            yield
            t = q.dve(lambda e: e.max(K8[:, s, :], KEY[:, s, :]), t)
            yield
            t = q.dve(lambda e: e.tensor_scalar(
                RI[:, n % 4, :], K8[:, s, :], -1.0, BIG, ALU.mult, ALU.add), t, got(("HR", n % 4)))
            for k in range(K0):
                free[("HR", n % 4)] = q.dma(f"sc{n % 4}", lambda e, k=k: e.indirect_dma_start(
                    out=buf0[:, :], out_offset=bass.IndirectOffsetOnAxis(
                        ap=RI[:, n % 4, k:k + 1].bitcast(U32), axis=0),
                    in_=HR[:, n % 4, :], in_offset=None, bounds_check=E0 * P - 1, oob_is_err=False),
                    t, w_t[n], clr["b0"][-1], engine="pool")

        def matches(i, scalar, *waits):
            s = i % 2
            ids, dd, ww = (BX[:, i % 4, o:o + 8] for o in (256, 264, 272))
            t1 = q.dve(lambda e: e.scalar_tensor_tensor(
                out=JK[:, s, 0, :], in0=ids, scalar=scalar, in1=dd, op0=ALU.is_equal, op1=ALU.mult,
                accum_out=DF[:, i % 4:i % 4 + 1]), *waits, got(("DF", i % 4)))
            t2 = q.dve(lambda e: e.scalar_tensor_tensor(
                out=JK[:, s, 1, :], in0=ids, scalar=scalar, in1=ww, op0=ALU.is_equal, op1=ALU.mult,
                accum_out=WC[:, i % 8:i % 8 + 1]), got(("WC", i % 8)))
            t3 = q.dve(lambda e: e.tensor_scalar(DI[:, i:i + 1], DF[:, i % 4:i % 4 + 1], OFF, None, ALU.add), t1)
            free[("DF", i % 4)] = t3
            free[("BXd", i % 4)] = t2
            return t2, t3

        def put_back(i, t, idx_t, w_tok, yb, bound):
            s = i % 3
            t = q.act(lambda e: e.activation(YT[:, s, :], PS[:, 4 + i % 2, 0:256], ACT.Copy, scale=WC[:, i % 8:i % 8 + 1]),
                      t, w_tok, got(("YT", s)))
            free[("Y", i % 2)] = free[("WC", i % 8)] = t
            free[("YT", s)] = q.dma(f"yt{s}", lambda e: e.indirect_dma_start(
                out=yb[:, :], out_offset=bass.IndirectOffsetOnAxis(ap=DI[:, i:i + 1].bitcast(U32), axis=0),
                in_=YT[:, s, :], in_offset=None, bounds_check=bound, oob_is_err=False),
                t, idx_t, engine="pool")
            return free[("YT", s)]

        def pause(n):
            for _ in range(n):
                yield

        def shared(nchunk, gate, up, down, w_tok, add, ybanks, before, pace=1):
            q.wait("pe", *before())
            for g in range(4):
                while any(4 * g + j not in h2T_t for j in range(4)):
                    yield
                act_t = []
                for i in range(nchunk):
                    w, z = (g * nchunk + i) % 2, (g * nchunk + i) % 4
                    rhs = [H2T[:, k, g * 512:g * 512 + 512] for k in range(2)]
                    tg = q.pe(lambda e, i=i, w=w, rhs=rhs: mm(
                        e, PS[:, 2 * w, :], [(gate(k, i), rhs[k]) for k in range(2)]),
                        [h2T_t[4 * g + j] for j in range(4)], w_tok, got(("shg", w)))
                    tu = q.pe(lambda e, i=i, w=w, rhs=rhs: mm(
                        e, PS[:, 2 * w + 1, :], [(up(k, i), rhs[k]) for k in range(2)]))
                    yield from pause(pace)
                    t = q.act(lambda e, w=w: e.activation(SS_[:, w, :], PS[:, 2 * w, :], ACT.Silu), tg,
                              got(("shs", w)))
                    t = q.dve(lambda e, z=z, w=w: e.tensor_tensor(
                        AS_[:, z, :], SS_[:, w, :], PS[:, 2 * w + 1, :], ALU.mult), t, tu, got(("sha", z)))
                    free[("shg", w)] = free[("shs", w)] = t
                    act_t.append((z, i, t))
                    yield from pause(pace)
                for j in range(4):
                    n = 4 * g + j
                    bank = ybanks[j % 2]
                    t = q.pe(lambda e, j=j, bank=bank, act_t=act_t: mm(
                        e, PS[:, bank, 0:256],
                        [(AS_[:, z, j * P:j * P + P], down(i)) for z, i, _ in act_t]),
                        [v for _, _, v in act_t], got(("shy", bank)))
                    for z, _, _ in act_t:
                        free[("sha", z)] = t
                    yield from pause(pace)
                    free[("shy", bank)] = add(n, bank, t)
            free["H2T"] = tu
            free["shared"] = free[("shy", ybanks[1])]

        def barrier_banks():
            return [v for k, v in free.items() if v and (k == "O" or isinstance(k, tuple) and k[0] in (
                "S", "PT", "M", "shg", "shy", "T", "GU", "Y", "T2"))]

        def add0(n, bank, t):
            return q.dve(lambda e: e.scalar_tensor_tensor(
                out=X[:, n, :], in0=PS[:, bank, 0:256], scalar=SIG[:, n:n + 1], in1=X[:, n, :],
                op0=ALU.mult, op1=ALU.add), t, got(("SIG", n)))

        def tail0(x_t):
            while NT - 1 not in x_t:
                yield
            yield from shared(4, lambda k, i: SG0[:, k, i * P:i * P + P],
                              lambda k, i: SG0[:, k, 512 + i * P:512 + i * P + P], lambda i: SD0[:, i, :],
                              t_s0, add0, (4, 6), lambda: [v for v in barrier_banks() if v not in misc_now()], 3)

        def misc_now():
            return [free.get(("M", b)) for b in (5, 7)]

        t_small, t_s0 = [], []

        def late_loads():
            yield from pause(40)
            t_s0.extend([ld("l_sg0", SG0, chunks("sgu0")), ld("l_sd0", SD0, chunks("sd0"))])
            for i in range(4, 8):
                w_load(i)
            t_small.extend([
                ld("l_s0", BV, a["bv"].partition_broadcast(P)),
                ld("l_s1", BO[:, :], a["bo"].unsqueeze(0)),
                ld("l_s2", BQK[:, :], a["bqk"]),
                ld("l_s4", GB[:, :], a["gbias"].partition_broadcast(P)),
                ld("l_s5", WR1[:, :, :], chunks("gate1")),
                ld("l_s6", WS1[:, 0:256].rearrange("p (c n) -> p c n", c=2), chunks("sg1")),
                ld("l_s7", WS1[:, 256:512].rearrange("p (c n) -> p c n", c=2), chunks("su1")),
                ld("l_s8", WS1[:, 512:768], a["sd1"]),
            ])

        attention(0, t_kz, lambda n: t_x[n // 4], late_loads(), route0, rows0, lambda x_t: [tail0(x_t)])
        scat0 = [free[("HR", i)] for i in range(4)]
        clear_some(100)
        a_done = [free[("SM", i)] for i in range(3)] + [free[("PTS", i)] for i in range(4)] + \
            [free[("CXT", i)] for i in range(2)] + [free[("QT", i)] for i in range(2)] + \
            [free[("CX", i)] for i in range(2)]

        k_done = [free[(k, i)] for k in ("KBD", "KT") for i in range(2)]

        def e0_load(i):
            s = i % NEW
            t1 = ld(f"ew{s}", EWR[s][:, 0:512].rearrange("p (c n) -> p c n", c=2),
                    a["egu"][i].rearrange("(c p) n -> p c n", p=P), a_done if 4 <= i < NEW else None, k_done if 14 <= i < NEW else None, got(("EW", s)))
            return [t1, ld(f"ew{s}", EWR[s][:, 512:768], a["ed"][i])]

        ew_t = {i: e0_load(i) for i in range(NEW)}

        q.wait("dve", clr["y0"][-1], clr["b0"][-1])
        sh_t = free["shared"]
        q.wait("pe", *barrier_banks())

        def bx_load(i, buf, *waits):
            return ld(f"bx{i % 4}", BX[:, i % 4, :], buf[i * P:i * P + P, :], *waits,
                      got(("BXp", i % 4)), got(("BXd", i % 4)))

        def stage_a(i, bx_t, scalar, *waits):
            s = i % 2
            t = q.pe(lambda e: tr2(e, PS[:, s, 0:256], BX[:, i % 4, 0:D]), bx_t[i], got(("T", s)))
            free[("BXp", i % 4)] = t
            t = q.dve(lambda e: e.tensor_copy(XT[:, i % 3, :, :], PS[:, s, 0:256].rearrange("p (c t) -> p c t", c=2)),
                      t, got(("XT", i % 3)))
            free[("T", s)] = t
            return t, matches(i, scalar, bx_t[i], *waits)

        bx_t, xt_t, mt_t, ac_t, sp0 = {}, {}, {}, {}, []
        for i in range(4):
            bx_t[i] = bx_load(i, buf0, scat0)
        for i in range(E0 + 3):
            if i < E0:
                xt_t[i], mt_t[i] = stage_a(i, bx_t, float(i))
                if i + 4 < E0:
                    bx_t[i + 4] = bx_load(i + 4, buf0)
            if 0 <= i - 1 < E0:
                j = i - 1
                s = j % 2

                def go(e, j=j, s=s):
                    for o in range(2):
                        m = mm(e, PS[:, 2 + s, o * P:o * P + P],
                               [(EWR[j % NEW][:, k * 256 + o * P:k * 256 + o * P + P], XT[:, j % 3, k, :])
                                for k in range(2)])
                    return m
                t = q.pe(go, xt_t[j], ew_t[j], got(("GU", s)))
                free[("XT", j % 3)] = t
                t1 = q.act(lambda e, s=s: e.activation(SL[:, s, :], PS[:, 2 + s, 0:P], ACT.Silu), t, got(("SL", s)))
                t = q.dve(lambda e, j=j, s=s: e.tensor_tensor(
                    AC[:, j % 3, :], SL[:, s, :], PS[:, 2 + s, P:2 * P], ALU.mult), t1, got(("AC", j % 3)))
                free[("GU", s)] = free[("SL", s)] = t
                ac_t[j] = t
            if 0 <= i - 3 < E0:
                j = i - 3
                s = j % 2
                t = q.pe(lambda e, j=j, s=s: mm(e, PS[:, 4 + s, 0:256], [(AC[:, j % 3, :], EWR[j % NEW][:, 512:768])]),
                         ac_t[j], got(("Y", s)))
                free[("AC", j % 3)] = t
                free[("EW", j % NEW)] = t
                sp0.append(put_back(j, t, mt_t[j][1], mt_t[j][0], yb0, 2048 * K0 - 1)
                           if j else put_back(j, t, [mt_t[j][1], clr["y0"][-1]], mt_t[j][0], yb0, 2048 * K0 - 1))
                if j + NEW < E0:
                    ew_t[j + NEW] = e0_load(j + NEW)
        scat_y0 = sp0[-3:]

        q.wait("pe", *barrier_banks())
        e0_done = [free[("EW", i)] for i in range(NEW)]
        t_kz = q.dve(lambda e: e.memset(KBD, 0.0), e0_done)
        for e_ in ("dve", "act"):
            q.wait(e_, *e0_done)
        yv = yb0.rearrange("(t k) d -> t (k d)", k=K0)
        def y_add():
            loads = {}

            def load(n):
                loads[n] = ld(f"yl{n % 3}", YL[:, n % 3, :], yv[n * P:n * P + P, :], scat_y0, got(("YL", n % 3)))
            for n in range(3):
                load(n)
            for n in range(NT):
                yl = YL[:, n % 3, :]
                add = q.dve if n < 3 and n != 1 else q.pool
                t = add(lambda e, yl=yl: e.tensor_tensor(
                    yl[:, 0:1024], yl[:, 0:1024], yl[:, 1024:2048], ALU.add), loads[n])
                for w in (512, 256):
                    t = add(lambda e, yl=yl, w=w: e.tensor_tensor(
                        yl[:, 0:w], yl[:, 0:w], yl[:, w:2 * w], ALU.add), t)
                t = add(lambda e, yl=yl, n=n: e.tensor_tensor(
                    X[:, n, :], X[:, n, :], yl[:, 0:256], ALU.add), t, x0_done)
                free[("YL", n % 3)] = t
                xc_t[n] = t
                if n + 3 < NT:
                    load(n + 3)
                for _ in range(7):
                    yield
            for g in (4, 5):
                w1_load(g, [free[("YL", i)] for i in range(3)] + e0_done, "sp")

        x0_done = sh_t
        t_bq = q.dve(lambda e: e.tensor_scalar(BQK[:, 0:2], BQK[:, 0:2], 0.25, None, ALU.mult), t_small)
        t_sum1 = q.dve(lambda e: e.memset(SUM[:, :, :], 0.0))
        sum_t.clear()
        sum_t[0] = t_sum1
        free.pop(("SUM", 0), None)
        free.pop(("SUM", 1), None)

        pos_t = {}

        def route1(n):
            s, z = n % 4, n % 2
            hr = HR[:, n % 4, :]
            bank, m = yield from misc()
            t = q.pe(lambda e: mm(
                e, m[:, 0:R1], [(H2T[:, k, n * P:n * P + P], WR1[:, k, :]) for k in range(2)]),
                h2T_t[n], t_small, got_bank(bank))
            td = q.act(lambda e: e.copy(hr[:, 264:272], cst("d1")[:, 8 * n:8 * n + 8]), got(("HR", n % 4)))
            sco, scb, mk = T1_[:, s, 0:R1], T2_[:, s, 0:R1], KEY[:, s, 0:40]
            idf, gs = hr[:, 256:264], GS[:, s, 0:10]
            yield
            t = q.act(lambda e: e.activation(sco, m[:, 0:R1], ACT.Exp, scale=-1.0), t)
            give(bank, t)
            tk = q.dve(lambda e: e.tensor_copy(mk[:, R1:40], cst("pad")[:, 0:8]))
            yield
            t = q.dve(lambda e: e.tensor_scalar(sco, sco, 1.0, None, ALU.add), t)
            yield
            t_sco = q.dve(lambda e: e.reciprocal(sco, sco), t)
            yield
            t_scb = q.dve(lambda e: e.tensor_tensor(scb, sco, GB[:, :], ALU.add), t_sco)
            yield
            for g in range(4):
                tg = q.dve(lambda e, g=g: e.max(G8[:, s, g, :], scb[:, 8 * g:8 * g + 8]), t_scb)
            yield
            t = q.dve(lambda e: e.tensor_tensor(GS[:, s, 0:4], G8[:, s, :, 0], G8[:, s, :, 1], ALU.add), tg, t_gs)
            yield
            tm = q.dve(lambda e: e.max(M8[:, s, :], gs), t)
            yield
            t = q.dve(lambda e: e.tensor_copy(R8[:, s, 0, 0:2], M8[:, s, 0:2]), tm, t_r8)
            yield
            t = q.dve(lambda e: e.match_replace(RP[:, s, 0:10], R8[:, s, 0, :], gs, -1.0e38), t)
            yield
            t = q.dve(lambda e: e.tensor_tensor(CNTG[:, s, :], RP[:, s, 0:4], GS[:, s, 0:4], ALU.is_equal), t)
            yield
            t = q.dve(lambda e: e.scalar_tensor_tensor(
                out=mk[:, 0:R1].rearrange("p (g k) -> p g k", g=4),
                in0=CNTG[:, s, :].unsqueeze(2).broadcast_to([P, 4, 8]), scalar=-1.0e30,
                in1=scb.rearrange("p (g k) -> p g k", g=4), op0=ALU.mult, op1=ALU.add), t)
            yield
            tm = q.dve(lambda e: e.max(M8[:, s, :], mk), t, tk)
            yield
            t = q.dve(lambda e: e.tensor_copy(R8[:, s, 1, 0:6], M8[:, s, 0:6]), tm)
            ti = q.dve(lambda e: e.max_index(IX[:, s, :], M8[:, s, :], mk), tm)
            yield
            t = q.dve(lambda e: e.match_replace(RP[:, s, 16:56], R8[:, s, 1, :], mk, -2.0e38), t)
            tc = q.dve(lambda e: e.tensor_copy(idf[:, 0:6], IX[:, s, 0:6]), ti, got(("HR", n % 4)))
            ta = q.dve(lambda e: e.tensor_scalar(AX1[:, s, :], IX[:, s, 0:1], 1, None,
                                                 ALU.logical_shift_right), ti)
            yield
            ts = q.dve(lambda e: e.tensor_tensor(
                SEL[:, s, 0:R1], RP[:, s, 16:16 + R1], mk[:, 0:R1], ALU.not_equal), t)
            tc2 = q.dve(lambda e: e.tensor_copy(SC1[:, s, 4:5], AX1[:, s, :]), ta)
            eq = EQ[:, z, :].rearrange("p (k e) -> p k e", k=6)
            t = q.dve(lambda e: e.tensor_tensor(
                eq, idf[:, 0:6].unsqueeze(2).broadcast_to([P, 6, R1]),
                cst("iota")[:, 0:R1].unsqueeze(1).broadcast_to([P, 6, R1]), ALU.is_equal), tc)
            yield
            sel_t[n] = [ts, q.dve(lambda e: e.tensor_scalar(
                SEL[:, s, R1:E1], cst("iota")[:, 0:NA], SC1[:, s, 4:5], None, ALU.is_equal), tc2)]
            t = q.dve(lambda e: e.tensor_tensor(
                eq, eq, sco.unsqueeze(1).broadcast_to([P, 6, R1]), ALU.mult), t)
            tc3 = q.dve(lambda e: e.tensor_scalar(idf[:, 6:7], SC1[:, s, 4:5], float(R1), None, ALU.add), tc2)
            yield
            t = q.dve(lambda e: e.tensor_reduce(EW8[:, s, 0:6], eq, AX.X, ALU.add), t)
            tc4 = q.dve(lambda e: e.memset(idf[:, 7:8], -1.0))
            tw_ = q.dve(lambda e: e.memset(hr[:, 278:280], 0.1))
            yield
            t2 = q.dve(lambda e: e.tensor_reduce(SC1[:, s, 1:2], EW8[:, s, 0:6], AX.X, ALU.add), t)
            yield
            t2 = q.dve(lambda e: e.tensor_scalar(SC1[:, s, 1:2], SC1[:, s, 1:2], 1e-20, None, ALU.add), t2)
            yield
            t2 = q.dve(lambda e: e.reciprocal(SC1[:, s, 2:3], SC1[:, s, 1:2]), t2)
            yield
            t2 = q.dve(lambda e: e.tensor_scalar(
                hr[:, 272:278], EW8[:, s, 0:6], SC1[:, s, 2:3], 0.2, ALU.mult, ALU.mult), t2)
            w_t[n] = [tc, tc3, tc4, t2, tw_, td, ts, h2T_t[n], h2_t[n]]

        def rows1(n):
            s, w = n % 4, n % 2
            t, bank, PO = yield from position(n, E1, SEL[:, s, 0:E1])
            t2 = q.dve(lambda e: e.tensor_tensor(T2_[:, s, 0:E1], cst("nb1"), PO, ALU.subtract), t)
            give(bank, t2)
            sum_t[n + 1] = q.dve(lambda e: e.tensor_tensor(
                SUM[:, 1 - w, 0:E1], SUM[:, w, 0:E1], SEL[:, s, 0:E1], ALU.add), sel_t[n], sum_t[n], t)
            yield
            t = q.dve(lambda e: e.tensor_tensor(KEY[:, s, 0:E1], SEL[:, s, 0:E1], T2_[:, s, 0:E1], ALU.mult), t2)
            yield
            t = q.dve(lambda e: e.max(K8[:, s, :], KEY[:, s, 0:E1]), t)
            yield
            t = q.dve(lambda e: e.tensor_scalar(
                RI[:, s, :], K8[:, s, :], -1.0, BIG1, ALU.mult, ALU.add), t, got(("HR", s)))
            for k in range(K1):
                free[("HR", s)] = q.dma(f"sd{s}", lambda e, k=k: e.indirect_dma_start(
                    out=buf1[:, :], out_offset=bass.IndirectOffsetOnAxis(
                        ap=RI[:, s, k:k + 1].bitcast(U32), axis=0),
                    in_=HR[:, s, :], in_offset=None, bounds_check=(DUM_A + 1) * P - 1, oob_is_err=False),
                    t, w_t[n], engine="pool")

        w1_t = {}

        def w1_load(g, waits, engine, first=0, n=4):
            es = slice(4 * g + first, 4 * g + first + n)
            for k in range(2):
                for o, nm in enumerate(("w1g", "w1u")):
                    ld(f"w1_{g}", W1[:, es, k * 256 + o * P:k * 256 + o * P + P],
                       a[nm][es, k * P:k * P + P, :].rearrange("e p n -> p e n"), waits, engine=engine)
            w1_t[g] = ld(f"w1_{g}", W1[:, es, 512:768], a["w1d"][es].rearrange("e p n -> p e n"), engine=engine)

        def wa_load(g, waits, engine):
            ls = slice(4 * g, 4 * g + 4)
            for k in range(2):
                for o, nm in enumerate(("wag", "wau")):
                    ld(f"wa_{g}", WA[:, ls, k * P + o * 64:k * P + o * 64 + 64],
                       a[nm][ls, k * P:k * P + P, :].rearrange("l p n -> p l n"), waits, engine=engine)
            w1_t["a", g] = ld(f"wa_{g}", WD[:, ls, :], a["wad"][ls].rearrange("l p n -> p l n"), engine=engine)

        def add1(n, bank, t):
            return q.dve(lambda e: e.tensor_tensor(X[:, n, :], PS[:, bank, 0:256], X[:, n, :], ALU.add), t)

        sg1 = WS1[:, 0:256].rearrange("p (c n) -> p c n", c=2)
        su1 = WS1[:, 256:512].rearrange("p (c n) -> p c n", c=2)

        def tail(x_t):
            while NT - 1 not in x_t:
                yield
            old = [v for k, v in free.items() if isinstance(k, tuple) and k[0] in ("KBD", "CXT", "KT", "YL")] + [free["VA"]]
            for g in range(4):
                w1_load(g, old, "sp")
            yield from shared(1, lambda k, i: sg1[:, k, :], lambda k, i: su1[:, k, :], lambda i: WS1[:, 512:768],
                              t_small, add1, (4, 6), lambda: [v for v in barrier_banks() if v not in misc_now()], 3)

        pad_t = {}

        def pad(x, engine="sp"):
            def go(e):
                r = e.value_load(PAD[0:1, x:x + 1], min_val=0, max_val=DUM_A * P)
                return e.dma_start(buf1[bass.ds(r, P), :], Z[:, :])
            pad_t[x] = q.dma(f"pad{x % 32}", go, T["pad"], t_z, engine=engine)

        T, NTL = {}, T1 + TA

        def tables():
            while NT not in sum_t:
                yield
            bank, m = yield from misc()
            PO = m[:, 0:E1]
            t = q.pe(lambda e: mm(e, PO, [(ones, SUM[:, 0, 0:E1])]), sum_t[NT], got_bank(bank))
            yield
            tt = q.dve(lambda e: e.tensor_copy(TOT[:, :], PO), t)
            give(bank, tt)
            yield
            hh_done = [free[("HH", i, j)] for i in range(2) for j in range(2)]
            PADF = R[:, lo + E1 * 16:lo + E1 * 17]
            t = q.dve(lambda e: e.tensor_tensor(PADF[:, :], TOT[:, :], cst("nb1"), ALU.subtract), tt, hh_done)
            yield
            t_pad = T["pad"] = q.dve(lambda e: e.tensor_scalar(PAD[:, :], PADF[:, :], BIG1, None, ALU.add), t)
            for x in range(8):
                pad(x)
            CM3 = R[:, lo:lo + E1 * 16].rearrange("p (e j) -> p e j", j=16)
            t = q.dve(lambda e: e.tensor_tensor(
                CM3, TOT[:, :].unsqueeze(2).broadcast_to([P, E1, 16]),
                cst("step").unsqueeze(1).broadcast_to([P, E1, 16]), ALU.is_gt), tt, hh_done)
            yield
            t = q.dve(lambda e: e.tensor_reduce(TIL[:, :], CM3, AX.X, ALU.add), t)
            yield
            part, two = cst("part"), []
            for i, (es, top, first, dummy) in enumerate(((slice(0, R1), R1 - 1, 0, DUM), (slice(R1, E1), NA - 1, SEG_A, DUM_A))):
                two.append([es, top, first, dummy, CNT[:, 4 * i:4 * i + 4],
                            q.dve(lambda e, es=es: e.tensor_tensor_scan(
                                CUM[:, es], ones[:, 0:es.stop - es.start], TIL[:, es], 0.0, ALU.mult, ALU.add), t)])
            yield
            for v in two:
                es, c = v[0], v[4]
                t = q.dve(lambda e, es=es, c=c: e.tensor_scalar(
                    CMP[:, es], CUM[:, es], part, 0.0, ALU.is_le, ALU.add, accum_out=c[:, 0:1]), v[5])
                v.append(q.dve(lambda e, es=es, c=c: e.scalar_tensor_tensor(
                    out=PADF[:, es], in0=CUM[:, es], scalar=part, in1=TIL[:, es], op0=ALU.is_le, op1=ALU.mult,
                    accum_out=c[:, 1:2]), v[5], t_pad))
                v.append(t)
                yield
            t_tab = T["tab"] = []
            for es, top, first, dummy, c, _, t_ex, t_n in two:
                t = q.dve(lambda e, c=c: e.tensor_scalar(
                    c[:, 2:3], c[:, 0:1], float(SEG), c[:, 1:2], ALU.mult, ALU.subtract), t_ex, t_n)
                t = q.dve(lambda e, c=c, first=first: e.tensor_scalar(
                    c[:, 2:3], c[:, 2:3], part, float(first), ALU.add, ALU.add), t)
                t_tab.append(q.dve(lambda e, c=c, dummy=dummy: e.tensor_scalar(
                    c[:, 2:3], c[:, 2:3], float(dummy), None, ALU.min), t))
                t_tab.append(q.dve(lambda e, c=c, top=top: e.tensor_scalar(
                    c[:, 3:4], c[:, 0:1], float(top), None, ALU.min), t_n))
                yield
            bank, m = yield from misc()

            def tiles(e):
                for o, col in ((0, 3), (NTL, 2)):
                    e.matmul(PS[:, bank, o:o + T1], CNT[:, col:col + 1].broadcast_to([P, P]), ident, start=True, stop=True)
                    m = e.matmul(PS[:, bank, o + T1:o + NTL], CNT[:, col + 4:col + 5].broadcast_to([P, P]), ident[:, 0:TA],
                                 start=True, stop=True)
                return m
            t = q.pe(tiles, t_tab, got_bank(bank))
            yield
            T["tu"] = q.dve(lambda e: e.tensor_copy(TU[:, :], PS[:, bank, NTL:2 * NTL]), t)
            T["ti"] = q.dve(lambda e: e.tensor_copy(TI[:, :], PS[:, bank, 0:NTL]), t)
            t = q.dve(lambda e: e.tensor_copy(TE[:, 0:T1], PS[:, bank, 0:T1]), t)
            T["te"] = q.dve(lambda e: e.tensor_scalar(TE[:, T1:NTL], PS[:, bank, T1:NTL], float(R1), None, ALU.add), t)
            give(bank, T["te"])


        CNTG = sb("CNTG", [P, 4, 4])
        q.lists["act"].append(("set", "natural_log_exp_and_others"))
        attention(1, t_kz, lambda n: xc_t[n], y_add(), route1, rows1, lambda x_t: [tail(x_t), tables()])
        scat1 = [free[("HR", i)] for i in range(4)]
        clear_some(100)

        for x in range(8, 16):
            pad(x, "act")
        t_tu, t_ti, t_te = T["tu"], T["ti"], T["te"]
        a1_done = [v for k, v in free.items() if isinstance(k, tuple) and k[0] in (
            "SM", "PTS", "CXT", "CX", "QT", "KBD", "HH", "HT", "YL", "KT")] + [free["VA"]] + T["tab"]
        sh1_t = free["shared"]
        q.wait("sp", *a1_done)
        q.wait("act", *a1_done)

        q.wait("pe", t_tu, t_ti, t_te, *barrier_banks())

        bx_t, xt_t, mt_t, ac_t, at_t, sp1 = {}, {}, {}, {}, {}, []
        reg_v, reg_u = {}, {}

        def width(i):
            return P if i < T1 else 64

        def bx1_load(i):
            q.register("sp", lambda e: reg_u.update({i: e.value_load(TU[0:1, i:i + 1], min_val=0, max_val=DUM_A)}), t_tu)

            def go(e):
                return e.dma_start(BX[:, i % 4, :], buf1.rearrange("(u p) r -> u p r", p=P)[
                    bass.ds(reg_u[i], 1), :, :].rearrange("a p r -> (a p) r"))
            last = i if i < R1 else R1 - 1
            if i >= T1:
                last = R1 + min(i - T1, NA - 1)
            bx_t[i] = q.dma(f"bx{i % 4}", go, t_tu, scat1, t_dum, [pad_t[x] for x in range(last + 1)],
                            got(("BXp", i % 4)), got(("BXd", i % 4)))

        for i in range(4):
            bx1_load(i)
        yv1 = yb1.rearrange("(t k) d -> t (k d)", k=6)
        yf_t, xf_t = {}, {}

        def yf_load(n):
            yf_t[n] = ld(f"yf{n}", YF[:, n, :], yv1[n * P:n * P + P, :], routed_done)

        def yf_add(n):
            yl = YF[:, n, :]
            t = q.dve(lambda e: e.tensor_tensor(yl[:, 0:768], yl[:, 0:768], yl[:, 768:1536], ALU.add), yf_t[n])
            t1 = q.dve(lambda e: e.tensor_tensor(X[:, n, :], X[:, n, :], yl[:, 512:768], ALU.add), t, sh1_t)
            t2 = q.dve(lambda e: e.tensor_tensor(yl[:, 0:256], yl[:, 0:256], yl[:, 256:512], ALU.add), t)
            xf_t[n] = q.dve(lambda e: e.tensor_tensor(X[:, n, :], X[:, n, :], yl[:, 0:256], ALU.add), t1, t2)

        for i in range(NTL + 3):
            if i < NTL:
                q.register("pe", lambda e, i=i: reg_v.update({i: e.value_load(
                    TI[0:1, i:i + 1], min_val=0, max_val=(R1 if i < T1 else NA) - 1)}))
                xt_t[i], mt_t[i] = stage_a(i, bx_t, TE[:, i:i + 1], t_te)
                if i + 4 < NTL:
                    bx1_load(i + 4)
                if i < 16:
                    pad(16 + i, "act" if i % 2 else "sp")
                if i >= 32 and i % 5 == 0 and 32 + (i - 35) // 5 < E1:
                    pad(32 + (i - 35) // 5)
                if i in (0, 3, 6, 9):
                    w1_load(6 + i // 6, a1_done, "act", 2 * (i // 3 % 2), 2)
                if i in (30, 42, 54, 66):
                    wa_load((i - 30) // 12, a1_done, "act")
            if 0 <= i - 1 < NTL:
                j = i - 1
                s = j % 2
                w = width(j)

                def go(e, j=j, s=s, w=w):
                    r = reg_v[j]
                    src = W1 if j < T1 else WA
                    for k in range(2):
                        m = e.matmul(PS[:, 2 + s, 0:2 * w], XT[:, j % 3, k, :],
                                     src[:, bass.ds(r, 1), k * 2 * w:(k + 1) * 2 * w].rearrange("p a n -> p (a n)"),
                                     start=(k == 0), stop=(k == 1))
                    return m
                t = q.pe(go, xt_t[j], w1_t[min(j // 4, 7)] if j < T1 else [w1_t["a", g] for g in range(4)], got(("GU", s)))
                free[("XT", j % 3)] = t
                t1 = q.act(lambda e, s=s, w=w: e.activation(SL[:, s, 0:w], PS[:, 2 + s, 0:w], ACT.Silu), t,
                           got(("SL", s)))
                t = q.dve(lambda e, s=s, w=w: e.tensor_tensor(
                    AC[:, s, 0:w], SL[:, s, 0:w], PS[:, 2 + s, w:2 * w], ALU.mult), t1, got(("AC", s)))
                free[("GU", s)] = free[("SL", s)] = t
                ac_t[j] = t
            if 0 <= i - 2 < NTL:
                j = i - 2
                s = j % 2
                w = width(j)
                t = q.pe(lambda e, s=s, w=w: e.transpose(PS[0:w, 6 + s, 0:P], AC[:, s, 0:w], ident), ac_t[j],
                         got(("T2", s)))
                free[("AC", s)] = t
                t = q.act(lambda e, s=s, w=w: e.copy(AT[0:w, s, :], PS[0:w, 6 + s, 0:P]), t, got(("AT", s)))
                free[("T2", s)] = t
                at_t[j] = t
            if 0 <= i - 3 < NTL:
                j = i - 3
                s = j % 2
                w = width(j)

                def go(e, j=j, s=s, w=w):
                    src = W1[:, bass.ds(reg_v[j], 1), 512:768] if j < T1 else WD[:, bass.ds(reg_v[j], 1), :]
                    return e.matmul(PS[:, 4 + s, 0:256], AT[0:w, s, :], src.rearrange("p a n -> p (a n)"),
                                    start=True, stop=True)
                t = q.pe(go, at_t[j], got(("Y", s)))
                free[("AT", s)] = t
                free["E1"] = t
                yb, bound = (yb1, 2048 * 6 - 1) if j < T1 else (yba, 2047)
                sp1.append(put_back(j, t, mt_t[j][1], mt_t[j][0], yb, bound))
                if j == T1 - 1:
                    routed_done = [t] + sp1[-3:]
            n = (i - T1 - 4) // 2
            if i - T1 - 4 >= 0 and i % 2 == 0 and n < NT:
                yf_load(n)
                if n >= 2:
                    yf_add(n - 2)

        yva = yba.rearrange("(n p) d -> p n d", p=P)
        last = [free["E1"]] + sp1[-3:]
        ya_t = [ld(f"ya{g}", YA[:, 4 * g:4 * g + 4, :], yva[:, 4 * g:4 * g + 4, :], last) for g in range(4)]
        for n in range(NT - 2, NT):
            yf_add(n)
        for g in range(4):
            ns = slice(4 * g, 4 * g + 4)
            t = q.dve(lambda e, ns=ns: e.tensor_tensor(X[:, ns, :], X[:, ns, :], YA[:, ns, :], ALU.add),
                      ya_t[g], [xf_t[n] for n in range(4 * g, 4 * g + 4)])
            t_out = ld("out", out_d[:, ns, :], X[:, ns, :], t, engine="act")
        q.wait("act", t_out)

        sems = {name: ctx.enter_context(nc.semaphore("s_" + name)) for name in q.count}
        block = ctx.enter_context(nc.Block())

        @block.sync
        def _(e):
            q.run("sp", e, sems)

        @block.gpsimd
        def _(e):
            q.run("pool", e, sems)

        @block.scalar
        def _(e):
            q.run("act", e, sems)

        @block.vector
        def _(e):
            q.run("dve", e, sems)

        @block.tensor
        def _(e):
            q.run("pe", e, sems)


def kernel(**inputs):
    import concourse.bacc as _bacc
    from concourse.bass_utils import run_bass_kernel_spmd as _run

    g = {k: np.asarray(v) for k, v in inputs.items()}
    c = np.ascontiguousarray
    arrays = {
        "x": g["x"],
        "cst": constants()[0],
        "ctxT": c(g["ctx_1024"].reshape(NB * SK, D).T),
        "mask": c(g["mask_1x1xSxS2_ik0"].reshape(256, SK)),
        "wq0": c(g["L0_xattn_w_q"].T), "wk0": c(g["L0_xattn_w_k"].T),
        "wv0": c(g["L0_xattn_w_v"].T), "wo0": c(g["L0_xattn_w_o"].T),
        "wq1": g["L1_xattn_W_q"], "wk1": g["L1_xattn_W_k"],
        "wv1": g["L1_xattn_W_v"], "wo1": g["L1_xattn_W_o"],
        "bqk": np.concatenate([g["L1_xattn_b_q"].reshape(2, P).T, g["L1_xattn_b_k"].reshape(2, P).T], 1),
        "bv": g["L1_xattn_b_v"], "bo": g["L1_xattn_b_o"],
        "gate0": np.concatenate([g["L0_ffn_gate_w"], g["L0_ffn_shared_gate_w"]], 1),
        "sgu0": g["L0_ffn_shared_gate_up_w"], "sd0": g["L0_ffn_shared_down_w"],
        "egu": g["L0_ffn_expert_gate_up_w"], "ed": g["L0_ffn_expert_down_w"],
        "gate1": c(g["L1_ffn_gate_weight"].T), "gbias": g["L1_ffn_gate_bias"],
        "w1g": g["L1_ffn_w_gate"], "w1u": g["L1_ffn_w_up"], "w1d": g["L1_ffn_w_down"],
        "sg1": g["L1_ffn_shared_w_gate"], "su1": g["L1_ffn_shared_w_up"], "sd1": g["L1_ffn_shared_w_down"],
        "wag": g["L1_ffn_anchor_w_gate"], "wau": g["L1_ffn_anchor_w_up"], "wad": g["L1_ffn_anchor_w_down"],
    }
    nc = _bacc.Bacc("TRN2", target_bir_lowering=False, num_devices=1)
    feed, args = {}, {}
    for name, v in arrays.items():
        v = np.ascontiguousarray(v)
        feed["in_" + name] = v
        args[name] = nc.dram_tensor("in_" + name, v.shape, mybir.dt.from_np(v.dtype), kind="ExternalInput").ap()
    out = nc.dram_tensor("out_0", (NB, 256, D), F32, kind="ExternalOutput").ap()
    build(nc, args, out)
    r = _run(nc, [feed], core_ids=[0])
    return r.results[0]["out_0"]
```
